# Optimizing a Trainium2 kernel written in Bass

```python
import numpy as np
import jax
import jax.numpy as jnp

def _softmax(x, axis=-1):
    return jax.nn.softmax(x, axis=axis)

def _gelu(x):
    return jax.nn.gelu(x, approximate=True)

def _silu(x):
    return jax.nn.silu(x)

def _sigmoid(x):
    return jax.nn.sigmoid(x)

def _layernorm(x, axis=-1, eps=1e-05):
    m = jnp.mean(x, axis=axis, keepdims=True)
    v = jnp.var(x, axis=axis, keepdims=True)
    return (x - m) / jnp.sqrt(v + eps)

def _scatter_add(tgt, idx, src, axis=0):
    return tgt.at[idx].add(src)

def _segment_sum(src, seg, n):
    return jax.ops.segment_sum(src, seg, n)
kernel_name = 'mk_xattn_ffn_d1_seqx_r2_db2d44'

def setup_inputs(seed: int=0):
    np.random.seed(seed)
    _w = jnp.asarray

    def _rec_inputs():
        import jax
        import jax.numpy as jnp
        _rk = jax.random.key(seed)
        x = 7.22e-05 + 1 * jax.random.normal(jax.random.fold_in(_rk, 1), (32, 512, 512), jnp.float32)
        _lenS = 512 - jax.random.randint(jax.random.fold_in(_rk, 7), (32,), 0, max(1, 512 // 4) + 1, jnp.int32)
        _lenS2 = 512 - jax.random.randint(jax.random.fold_in(_rk, 8), (32,), 0, max(1, 512 // 4) + 1, jnp.int32)
        _ctx_1024P = jax.random.normal(jax.random.fold_in(_rk, 11), (32, 16, 512), jnp.float32)
        _ctx_1024c = jax.random.dirichlet(jax.random.fold_in(_rk, 511), 0.3 * jnp.ones((16,), jnp.float32), (32, 512))
        _ctx_1024t = jnp.einsum('bsk,bkd->bsd', _ctx_1024c, _ctx_1024P)
        _ctx_1024t = _ctx_1024t * jax.lax.rsqrt(jnp.mean(jnp.square(_ctx_1024t)) + 1e-12) * 0.953939
        ctx_1024 = 4.13588e-05 + 0.999923 * (_ctx_1024t + 0.3 * jax.random.normal(jax.random.fold_in(_rk, 611), (32, 512, 512), jnp.float32))
        return (x, ctx_1024)
    x, ctx_1024 = _rec_inputs()

    def _L0_xattn_setup():
        import jax, jax.numpy as jnp
        import numpy as np
        R = 3.9
        STRENGTH = 0.1
        N_ITER = 10
        I0 = 1.0
        OMEGA = 1.0
        KWAVE = 2.0
        ALPHA_BASE = 1.0
        LC = 0.5
        DE = 2.0
        CHIRP_N = 1
        AMIN = 0.1
        AMAX = 3.0
        FD = 1.5
        T = 0.0
        ATT_ALPHA = 1.5
        EPS = 1e-10
        FCI = 0.7
        STAB = 0.8
        DEMAND = 0.6
        BASE = 0.5
        SENS = 1.0
        DECAY = 0.1
        B, S, D4 = (4, 1024, 512)

        def hamilton(a, b):
            aw, ax, ay, az = jnp.split(a, 4, axis=-1)
            bw, bx, by, bz = jnp.split(b, 4, axis=-1)
            w = aw * bw - ax * bx - ay * by - az * bz
            x = aw * bx + ax * bw + ay * bz - az * by
            y = aw * by - ax * bz + ay * bw + az * bx
            z = aw * bz + ax * by - ay * bx + az * bw
            return jnp.concatenate([w, x, y, z], axis=-1)
        key = jax.random.key(seed)
        ks = jax.random.split(key, 8)
        sc = 0.02
        return {'query': jax.random.normal(ks[0], (B, S, D4), jnp.float32), 'memory': jax.random.normal(ks[1], (B, S, D4), jnp.float32), 'Wq': jax.random.normal(ks[2], (D4, D4), jnp.float32) * sc, 'bq': jnp.zeros((D4,), jnp.float32), 'Wk': jax.random.normal(ks[3], (D4, D4), jnp.float32) * sc, 'bk': jnp.zeros((D4,), jnp.float32), 'Wv': jax.random.normal(ks[4], (D4, D4), jnp.float32) * sc, 'bv': jnp.zeros((D4,), jnp.float32)}
    _L0_xattn_all = _L0_xattn_setup()
    _L0_xattn_in = {k: v for k, v in _L0_xattn_all.items() if k in ('Wq', 'bq', 'Wk', 'bk', 'Wv', 'bv')}
    del _L0_xattn_all

    def _L0_ffn_setup():
        import jax, jax.numpy as jnp
        import numpy as np
        B, L, H, E, I = (4, 1024, 512, 8, 2048)
        S = B * L
        CAP_FACTOR_EVAL = 2.0
        MIN_CAP = 4
        _cap = int(np.floor(CAP_FACTOR_EVAL * S / E))
        _cap += _cap % 2
        CAPACITY = max(_cap, MIN_CAP)

        def _layer_norm(x, g, b, eps=1e-05):
            mu = x.mean(-1, keepdims=True)
            var = ((x - mu) ** 2).mean(-1, keepdims=True)
            return (x - mu) * jax.lax.rsqrt(var + eps) * g + b
        key = jax.random.key(seed)
        ks = jax.random.split(key, 8)
        gate_std = float(np.sqrt(0.1 / H))
        return {'inputs': jax.random.normal(ks[0], (B, L, H), jnp.float32), 'gate_weight': jax.random.normal(ks[1], (E, H), jnp.float32) * gate_std, 'ln_gamma': jnp.ones((H,), jnp.float32), 'ln_beta': jnp.zeros((H,), jnp.float32), 'wi': jax.random.normal(ks[2], (E, H, I), jnp.float32) * float(1.0 / np.sqrt(H)), 'wo': jax.random.normal(ks[3], (E, I, H), jnp.float32) * float(1.0 / np.sqrt(I)), 'conf_w1': jax.random.normal(ks[4], (H // 2, H), jnp.float32) * float(np.sqrt(2.0 / (H + H // 2))), 'conf_b1': -jnp.ones((H // 2,), jnp.float32), 'conf_w2': jax.random.normal(ks[5], (1, H // 2), jnp.float32) * float(np.sqrt(2.0 / (1 + H // 2))), 'conf_b2': -jnp.ones((1,), jnp.float32), 'comp_w': jax.random.normal(ks[6], (1, H), jnp.float32) * float(1.0 / np.sqrt(H)), 'comp_b': jnp.zeros((1,), jnp.float32)}
    _L0_ffn_all = _L0_ffn_setup()
    _L0_ffn_in = {k: v for k, v in _L0_ffn_all.items() if k in ('gate_weight', 'ln_gamma', 'ln_beta', 'wi', 'wo', 'conf_w1', 'conf_b1', 'conf_w2', 'conf_b2', 'comp_w', 'comp_b')}
    del _L0_ffn_all
    return {'x': x, 'ctx_1024': ctx_1024, 'L0_xattn_Wq': _L0_xattn_in['Wq'], 'L0_xattn_bq': _L0_xattn_in['bq'], 'L0_xattn_Wk': _L0_xattn_in['Wk'], 'L0_xattn_bk': _L0_xattn_in['bk'], 'L0_xattn_Wv': _L0_xattn_in['Wv'], 'L0_xattn_bv': _L0_xattn_in['bv'], 'L0_ffn_gate_weight': _L0_ffn_in['gate_weight'], 'L0_ffn_ln_gamma': _L0_ffn_in['ln_gamma'], 'L0_ffn_ln_beta': _L0_ffn_in['ln_beta'], 'L0_ffn_wi': _L0_ffn_in['wi'], 'L0_ffn_wo': _L0_ffn_in['wo'], 'L0_ffn_conf_w1': _L0_ffn_in['conf_w1'], 'L0_ffn_conf_b1': _L0_ffn_in['conf_b1'], 'L0_ffn_conf_w2': _L0_ffn_in['conf_w2'], 'L0_ffn_conf_b2': _L0_ffn_in['conf_b2'], 'L0_ffn_comp_w': _L0_ffn_in['comp_w'], 'L0_ffn_comp_b': _L0_ffn_in['comp_b']}

def reference(x, ctx_1024, L0_xattn_Wq, L0_xattn_bq, L0_xattn_Wk, L0_xattn_bk, L0_xattn_Wv, L0_xattn_bv, L0_ffn_gate_weight, L0_ffn_ln_gamma, L0_ffn_ln_beta, L0_ffn_wi, L0_ffn_wo, L0_ffn_conf_w1, L0_ffn_conf_b1, L0_ffn_conf_w2, L0_ffn_conf_b2, L0_ffn_comp_w, L0_ffn_comp_b):
    import jax
    import jax.numpy as jnp

    def _L0_xattn_ref(query, memory, Wq, bq, Wk, bk, Wv, bv):
        import jax, jax.numpy as jnp
        import numpy as np
        R = 3.9
        STRENGTH = 0.1
        N_ITER = 10
        I0 = 1.0
        OMEGA = 1.0
        KWAVE = 2.0
        ALPHA_BASE = 1.0
        LC = 0.5
        DE = 2.0
        CHIRP_N = 1
        AMIN = 0.1
        AMAX = 3.0
        FD = 1.5
        T = 0.0
        ATT_ALPHA = 1.5
        EPS = 1e-10
        FCI = 0.7
        STAB = 0.8
        DEMAND = 0.6
        BASE = 0.5
        SENS = 1.0
        DECAY = 0.1
        B, S, D4 = (4, 1024, 512)

        def hamilton(a, b):
            aw, ax, ay, az = jnp.split(a, 4, axis=-1)
            bw, bx, by, bz = jnp.split(b, 4, axis=-1)
            w = aw * bw - ax * bx - ay * by - az * bz
            x = aw * bx + ax * bw + ay * bz - az * by
            y = aw * by - ax * bz + ay * bw + az * bx
            z = aw * bz + ax * by - ay * bx + az * bw
            return jnp.concatenate([w, x, y, z], axis=-1)
        s = jax.nn.sigmoid(jnp.linalg.norm(query, axis=-1))
        for _ in range(N_ITER):
            s = R * s * (1.0 - s)
        q = query * (1.0 + STRENGTH * (s[..., None] - 0.5))
        seq = q.shape[1]
        alpha = float(np.clip(ALPHA_BASE * (1.0 + LC * (FD - DE) / DE), AMIN, AMAX))
        beta = 2 * CHIRP_N + 1 - 2 * FD
        lam = jnp.arange(seq, dtype=q.dtype) / seq
        wave = I0 * jnp.sin(OMEGA * T + alpha * lam) * jnp.cos(OMEGA * T - KWAVE * lam + beta * lam ** 2)
        q = q * (1.0 + 0.1 * wave[None, :, None])
        dop = (1 - DECAY) * BASE + DECAY * jax.nn.sigmoid(jnp.float32(FCI * SENS))
        ser = (1 - DECAY) * BASE + DECAY * jax.nn.sigmoid(jnp.float32(STAB * SENS))
        nor = (1 - DECAY) * BASE + DECAY * jax.nn.sigmoid(jnp.float32(DEMAND * SENS))
        mem = memory * (0.4 * dop + 0.3 * ser + 0.3 * nor)
        Q = q @ Wq.T + bq
        K = mem @ Wk.T + bk
        V = mem @ Wv.T + bv
        Qf = jnp.fft.fft(Q, axis=-2)
        Kf = jnp.fft.fft(K, axis=-2)
        Vf = jnp.fft.fft(V, axis=-2)
        kidx = jnp.arange(seq, dtype=jnp.float32)
        filt = jnp.exp(1j * ATT_ALPHA * jnp.arctan(jnp.log(kidx + EPS)))[None, :, None]
        QK = hamilton(Qf * filt, Kf * filt)
        QKV = hamilton(QK, Vf * filt)
        attended = jnp.fft.ifft(QKV, axis=-2).real.astype(query.dtype)
        return attended

    def _L0_ffn_ref(inputs, gate_weight, ln_gamma, ln_beta, wi, wo, conf_w1, conf_b1, conf_w2, conf_b2, comp_w, comp_b):
        import jax, jax.numpy as jnp
        import numpy as np
        B, L, H, E, I = (4, 1024, 512, 8, 2048)
        S = B * L
        CAP_FACTOR_EVAL = 2.0
        MIN_CAP = 4
        _cap = int(np.floor(CAP_FACTOR_EVAL * S / E))
        _cap += _cap % 2
        CAPACITY = max(_cap, MIN_CAP)

        def _layer_norm(x, g, b, eps=1e-05):
            mu = x.mean(-1, keepdims=True)
            var = ((x - mu) ** 2).mean(-1, keepdims=True)
            return (x - mu) * jax.lax.rsqrt(var + eps) * g + b
        tokens = inputs.reshape(-1, H)
        residual = tokens
        tokens = _layer_norm(tokens, ln_gamma, ln_beta)
        complexity_score = jax.nn.sigmoid(tokens @ comp_w.T + comp_b).mean()
        hdn = jax.nn.relu(tokens @ conf_w1.T + conf_b1)
        confidence_score = jax.nn.sigmoid(hdn @ conf_w2.T + conf_b2).mean()
        logits = tokens.astype(jnp.float32) @ gate_weight.astype(jnp.float32).T
        probs = jax.nn.softmax(logits, axis=-1)
        top1 = jnp.argmax(logits, axis=-1)
        onehot = jax.nn.one_hot(top1, E, dtype=jnp.int32)
        rank_e = jnp.cumsum(onehot, axis=0) - onehot
        rank = jnp.sum(rank_e * onehot, axis=-1)
        keep = rank < CAPACITY
        weight = jnp.take_along_axis(probs, top1[:, None], axis=-1)[:, 0]
        weight = (weight * keep).astype(tokens.dtype)
        slot = jnp.where(keep, rank, 0)
        dispatch = jnp.zeros((E, CAPACITY, H), tokens.dtype)
        dispatch = dispatch.at[top1, slot].add(tokens * keep[:, None])
        h = jax.nn.gelu(jnp.einsum('ech,ehi->eci', dispatch, wi), approximate=False)
        expert_out = jnp.einsum('eci,eih->ech', h, wo)
        combined = weight[:, None] * expert_out[top1, slot]
        out = (residual + combined).reshape(inputs.shape)
        return out
    x = x + _L0_xattn_ref(_layernorm(x, axis=-1), ctx_1024, L0_xattn_Wq, L0_xattn_bq, L0_xattn_Wk, L0_xattn_bk, L0_xattn_Wv, L0_xattn_bv)
    x = x + _L0_ffn_ref(_layernorm(x, axis=-1), L0_ffn_gate_weight, L0_ffn_ln_gamma, L0_ffn_ln_beta, L0_ffn_wi, L0_ffn_wo, L0_ffn_conf_w1, L0_ffn_conf_b1, L0_ffn_conf_w2, L0_ffn_conf_b2, L0_ffn_comp_w, L0_ffn_comp_b)
    return x

_drawn_inputs = setup_inputs


def setup_inputs(seed=0):
    import zlib

    import numpy as np

    out = dict(_drawn_inputs(seed))
    spreads = {'L0_xattn_bq': (0.0, 0.1),
     'L0_xattn_bk': (0.0, 0.1),
     'L0_xattn_bv': (0.0, 0.1),
     'L0_ffn_ln_gamma': (1.0, 0.6),
     'L0_ffn_ln_beta': (0.0, 2.0),
     'L0_ffn_conf_b1': (-1.0, 0.2)}
    factors = {'L0_ffn_gate_weight': 30.773, 'L0_ffn_wi': 42.32, 'L0_ffn_wo': 34.922}
    for name, (base, spread) in spreads.items():
        noise = np.random.default_rng([zlib.crc32(name.encode()), seed]).standard_normal(out[name].shape)
        drawn = base * np.exp(spread * noise) if base else spread * noise
        out[name] = jnp.asarray(drawn.astype(out[name].dtype))
    for name, factor in factors.items():
        out[name] = (out[name] * factor).astype(out[name].dtype)
    return out
```

```python
import concourse.bass as bass
import numpy as np
from concourse import mybir
from contextlib import ExitStack

P = 128
BATCH, SEQ, DIM = 32, 512, 512
ROWT = SEQ // P
CB = DIM // P
EXPERTS, INNER = 8, 2048
CAPACITY = 2 * (4 * 1024) // EXPERTS
SLOTS = EXPERTS * CAPACITY
META = 8
ROW = DIM + META
EPS = 1e-5
R_MAP, MAP_STEPS = 3.9, 10
SKIPPED = 1 << 20

GROUP = 512
GT = GROUP // P
ISTEPS = INNER // P
PAIRS = ISTEPS // 2
RING = 4


def sigmoid(v):
    return 1.0 / (1.0 + np.exp(-v))


def memory_scale():
    dop, ser, nor = (0.9 * 0.5 + 0.1 * sigmoid(v) for v in (0.7, 0.8, 0.6))
    return float(0.4 * dop + 0.3 * ser + 0.3 * nor)


def forward_matrix():
    n = np.arange(256)[:, None]
    j = np.arange(128)[None, :]
    m = np.empty((256, 2, 2, 128))
    for tile in (0, 1):
        angle = 2 * np.pi * (((2 * j + tile) * n) % 512) / 512
        m[:, tile, 0], m[:, tile, 1] = np.cos(angle), -np.sin(angle)
    m[:, 0, 1, 0] = 1 - 2 * (np.arange(256) % 2)
    return m.reshape(2, 128, 2, 256).transpose(1, 0, 2, 3).reshape(128, -1).astype(np.float32)


def inverse_matrix():
    k = np.arange(512)
    filt = np.exp(3j * 1.5 * np.arctan(np.log(k + 1e-10)))
    h = (filt + np.conj(filt[-k % 512])) / 2
    n = np.arange(256)[None, :]
    m = np.empty((128, 2, 2, 256))
    for tile in (0, 1):
        f = (2 * np.arange(128) + tile)[:, None]
        e = h[f] * np.exp(2j * np.pi * ((f * n) % 512) / 512) / 512
        m[:, tile, 0], m[:, tile, 1] = e.real, -e.imag
    m[0, 0, 0] = h[0].real / 512
    m[0, 0, 1] = h[256].real * (1 - 2 * (np.arange(256) % 2)) / 512
    return m.reshape(128, -1).astype(np.float32)


def position_scale():
    lam = np.arange(SEQ) / SEQ
    alpha = float(np.clip(1.0 * (1.0 + 0.5 * (1.5 - 2.0) / 2.0), 0.1, 3.0))
    wave = np.sin(alpha * lam) * np.cos(-2.0 * lam + 0.0 * lam ** 2)
    return (1 + 0.1 * wave).reshape(ROWT, P).T.astype(np.float32)


def quaternion_signs():
    return np.array([[-1, 1, -1, 1], [-1, 1, 1, -1], [-1, -1, 1, 1]], np.float32)


class Chain:

    def __init__(self, engine, sem, per):
        self.engine, self.sem, self.per = engine, sem, per

    def begin(self, round_):
        self.base, self.n = round_ * self.per, 0

    def step(self, ins):
        self.n += 1
        ins.then_inc(self.sem, 1)
        return self.n

    def wait(self, n=None):
        self.engine.wait_ge(self.sem, self.base + (self.n if n is None else n))

    def end(self):
        assert self.n == self.per, (self.n, self.per)


def wait(engine, sem, value):
    if not isinstance(value, int) or value > 0:
        engine.wait_ge(sem, value)


def xattn_moe_kernel(nc, x, ctx_in, wq, wk, wv, bq, bk, bv, gate, gamma, beta, wi, wo, out):
    f32, f32r, bf16 = mybir.dt.float32, mybir.dt.float32r, mybir.dt.bfloat16
    i32, u32 = mybir.dt.int32, mybir.dt.uint32
    ALU, ACT, AX = mybir.AluOpType, mybir.ActivationFunctionType, mybir.AxisListType

    c_fwd = nc.inline_tensor(forward_matrix(), "c_fwd").ap()
    c_inv = nc.inline_tensor(inverse_matrix(), "c_inv").ap()
    c_pos = nc.inline_tensor(position_scale(), "c_pos").ap()
    c_sgn = nc.inline_tensor(np.tile(np.repeat(quaternion_signs().reshape(1, 12), 8, 1), (16, 1)), "c_sgn").ap()
    c_tri = nc.inline_tensor(np.triu(np.ones((P, P), np.float32), 1), "c_tri").ap()
    c_eye = nc.inline_tensor(np.eye(P, dtype=np.float32), "c_eye").ap()
    c_tok = nc.inline_tensor((np.arange(SEQ, dtype=np.float32)).reshape(ROWT, P).T.copy(), "c_tok").ap()
    c_exp = nc.inline_tensor(np.tile(np.arange(EXPERTS, dtype=np.float32) - EXPERTS, (P, ROWT)), "c_exp").ap()
    bins_in = nc.dram_tensor("bins_in", [1, 6 * DIM], f32, kind="Internal").ap()
    bins_out = nc.dram_tensor("bins_out", [1, 2 * DIM], f32, kind="Internal").ap()
    slots = nc.dram_tensor("slots", [SLOTS, ROW], f32, kind="Internal").ap()

    outer = ExitStack()
    with outer:
        def sem(name):
            return outer.enter_context(nc.semaphore(name))

        with ExitStack() as mem:
            def sb(name, shape, dt=f32):
                return mem.enter_context(nc.sbuf_tensor(name, shape, dt))

            def pb(name, shape):
                return mem.enter_context(nc.psum_tensor(name, shape, f32))

            fwd = sb("fwd", [P, 2, 2, 256])
            inv = sb("inv", [P, 2, 2, 256])
            w_q = sb("w_q", [P, CB, DIM])
            w_kh, w_kl, w_vh, w_vl = (sb(n, [P, CB, DIM], f32r) for n in ("w_kh", "w_kl", "w_vh", "w_vl"))
            c_high, c_low = (sb(n, [P, CB, 512], f32r) for n in ("c_high", "c_low"))
            pos = sb("pos", [P, ROWT])
            signs = sb("signs", [16, 3, 4, 8])
            tri, ones = sb("tri", [P, P], bf16), sb("ones", [P, P], bf16)
            eye = sb("eye", [P, P])
            token = sb("token", [P, ROWT])
            iota8 = sb("iota8", [P, ROWT, EXPERTS])
            gate_t = sb("gate_t", [P, CB, EXPERTS])
            gate_b = sb("gate_b", [P, CB, EXPERTS])
            gate_g = sb("gate_g", [P, CB, EXPERTS])
            gam, bet = sb("gam", [P, CB]), sb("bet", [P, CB])
            gate_c = sb("gate_c", [P, EXPERTS])
            values = dict(minus_half=-0.5, half=0.5, minus_one=-1.0, zero=0.0, one=1.0, eps=EPS, dim=float(DIM), seq=float(SEQ),
                          inv_e=float(np.exp(-1.0)), r_map=R_MAP, strength=0.1, rest=1.0 - 0.1 * 0.5)
            const = {n: sb(n, [P, ROWT]) for n in values}
            bias16 = sb("bias16", [16, 3, 4, 8])
            running = sb("running", [P, EXPERTS])

            x_in, c_in, x_res = (sb(n, [P, ROWT, DIM]) for n in ("x_in", "c_in", "x_res"))
            base = x_res
            q_rows = sb("q_rows", [P, ROWT, DIM])
            q_fold, c_fold = (sb(n, [P, 2, 2, DIM]) for n in ("q_fold", "c_fold"))
            q_spec, c_spec = (sb(n, [P, CB, 512]) for n in ("q_spec", "c_spec"))
            re_buf = [sb(f"re{i}", [P, DIM]) for i in (0, 1)]
            s1, s2 = sb("s1", [P, 2, 4, P]), sb("s2", [P, 2, 4, P])
            tri32, ones32 = s2[:, 0, 0], s2[:, 0, 1]
            prod = sb("prod", [P, 4, 2, DIM])
            w_raw = prod[:].rearrange("p (w a) b n -> p w (a b) n", w=2)
            r_spec = sb("r_spec", [P, 2, 2, 4, P])
            real_row = sb("real_row", [1, 3, 2, DIM])
            real_in = sb("real_in", [16, 3, 2, 4, 8])
            real_t = sb("real_t", [16, 2, 4, 4, 8])
            real_u = sb("real_u", [16, 2, 4, 8])
            real_v = sb("real_v", [16, 2, 4, 8])
            real_p = sb("real_p", [16, 2, 4, 8])
            rows = sb("rows", [P, ROWT, ROW])
            x_tok = sb("x_tok", [P, ROWT, DIM])
            x_tok_t = [sb(f"x_tok_t{i}", [P, CB, P]) for i in (0, 1)]
            bn1, bn2 = sb("bn1", [P, ROWT, 6]), sb("bn2", [P, ROWT, 6])
            mv1, mv2 = sb("mv1", [P, ROWT, 2]), sb("mv2", [P, ROWT, 2])
            st = [sb(f"st{i}", [P, ROWT]) for i in range(10)]
            q_scale, q_bias = sb("q_scale", [P, ROWT]), sb("q_bias", [P, ROWT])
            tt = [sb(f"tt{i}", [P, ROWT]) for i in range(6)]
            logit, over, e_over, cand, picked = (sb(n, [P, ROWT, EXPERTS]) for n in ("logit", "over", "e_over", "cand", "picked"))
            onehot = sb("onehot", [P, ROWT, EXPERTS], bf16)
            top = sb("top", [P, ROWT])
            first = sb("first", [P, ROWT])
            denom = sb("denom", [P, ROWT])
            rank = sb("rank", [P, ROWT])
            far = sb("far", [P, ROWT])
            slot_f = sb("slot_f", [P, ROWT])
            slot_i = sb("slot_i", [P, ROWT], i32)

            pair = [pb(f"pair{i}", [P, 2, 512]) for i in (0, 1)]
            xt_ps = [pb(f"xt_ps{i}", [P, 512]) for i in (0, 1)]
            even_ps, odd_ps = pb("even_ps", [P, 512]), pb("odd_ps", [P, 512])

            SETUP_DMAS = 17
            ZEROED = len(values) + 4
            consts_in = sem("consts_in")
            zeroed = sem("zeroed")
            token_next = sem("token_next")
            setup_v = sem("setup_v")
            setup_mm = sem("setup_mm")
            scaled = sem("scaled")
            w_split, c_split = sem("w_split"), sem("c_split")
            slots_clear = sem("slots_clear")
            x_loaded, c_loaded, res_loaded = sem("x_loaded"), sem("c_loaded"), sem("res_loaded")
            real_left, real_back = sem("real_left"), sem("real_back")
            real_loaded, real_stored = sem("real_loaded"), sem("real_stored")
            base_stored, scattered = sem("base_stored"), sem("scattered")
            bn1_step = sem("bn1_step")
            stat1 = sem("stat1")
            q_ready = sem("q_ready")
            qf_ready, cf_ready = sem("qf_ready"), sem("cf_ready")
            f1_mm, f1_ev = sem("f1_mm"), sem("f1_ev")
            f2_mm, re_ready, conv = sem("f2_mm"), sem("re_ready"), sem("conv")
            ham = sem("ham")
            inv_mm, unfold = sem("inv_mm"), sem("unfold")
            bn2_step, stat2 = sem("bn2_step"), sem("stat2")
            tok_ready, base_ready = sem("tok_ready"), sem("base_ready")
            g_mm, g_ev, logit_mm = sem("g_mm"), sem("g_ev"), sem("logit_mm")
            route, exp_done, rank_mm = sem("route"), sem("exp_done"), sem("rank_mm")
            real_step = sem("real_step")

            BN, STAT1, STAT2, CONV, HAM, UNF, ROUTE, REAL = 8, 45, 11, 24, 54, 8, 16, 27
            HAM_E, HAM_O = 27, 54
            PROJ = [(0, 0), (0, 1), (0, 2), (1, 0), (1, 1), (1, 2)]

            def seq(v, b):
                return v[bass.ds(b, 1), :, :].rearrange("a (t p) n -> p (a t) n", p=P)

            with nc.Block() as block:

                @block.sync
                def _(sp):
                    def load_x(b):
                        if not isinstance(b, int) or b > 0:
                            sp.wait_ge(q_ready, b * 4)
                        sp.dma_start(x_in[:], seq(x, b)).then_inc(x_loaded, 16)

                    def load_c(b):
                        if not isinstance(b, int) or b > 0:
                            sp.wait_ge(cf_ready, b * 2)
                        sp.dma_start(c_in[:], seq(ctx_in, b)).then_inc(c_loaded, 16)

                    def batch(b, back, ahead):
                        if not back:
                            load_res(b)
                        if ahead:
                            load_x(b + 2)
                        sp.wait_ge(re_ready, b * 6 + 3)
                        sp.dma_start(bins_in, real_row[:].rearrange("o a s n -> o (a s n)")).then_inc(real_left, 16)
                        sp.wait_ge(real_left, b * 16 + 16)
                        sp.dma_start(real_in[:].rearrange("q a s c e -> q (a s c) e"),
                                     bins_in.rearrange("o (k q e) -> q (o k) e", q=16, e=8)).then_inc(real_loaded, 16)
                        sp.wait_ge(real_step, b * REAL + REAL)
                        sp.dma_start(bins_out.rearrange("o (k q e) -> q (o k) e", q=16, e=8),
                                     real_p[:].rearrange("q s c e -> q (s c) e")).then_inc(real_back, 16)
                        sp.wait_ge(ham, b * HAM + HAM_E)
                        sp.wait_ge(real_back, b * 16 + 16)
                        sp.dma_start(r_spec[0:1, 0].rearrange("o s c e -> o (s c e)"), bins_out).then_inc(real_stored, 16)
                        if ahead:
                            load_c(b + 2)
                        if back:
                            store(b - 1)
                            load_res(b)

                    def load_res(b):
                        wait(sp, base_stored, b * 16)
                        sp.dma_start(x_res[:], seq(x, b)).then_inc(res_loaded, 16)

                    def store(b):
                        sp.wait_ge(base_ready, b * 4 + 4)
                        sp.dma_start(seq(out, b), base[:]).then_inc(base_stored, 16)

                    for dst, src in ((fwd[:].rearrange("p a b c -> p (a b c)"), c_fwd),
                                     (inv[:].rearrange("p a b c -> p (a b c)"), c_inv),
                                     (pos[:], c_pos), (signs[:].rearrange("p a b c -> p (a b c)"), c_sgn),
                                     (tri32, c_tri), (eye[:], c_eye), (token[:], c_tok),
                                     (iota8[:].rearrange("p t e -> p (t e)"), c_exp),
                                     (w_q[:], wq.rearrange("(k p) n -> p k n", p=P)),
                                     (w_raw[:, 0], wk.rearrange("(k p) n -> p k n", p=P)),
                                     (w_raw[:, 1], wv.rearrange("(k p) n -> p k n", p=P)),
                                     (gate_t[:], gate.rearrange("(k p) e -> p k e", p=P)),
                                     (gam[:], gamma),
                                     (bet[:], beta)):
                        sp.dma_start(dst, src).then_inc(consts_in, 16)
                    for a, v in enumerate((bq, bk, bv)):
                        sp.dma_start(bias16[:, a], v.rearrange("(c q e) -> q c e", c=4, q=16)).then_inc(consts_in, 16)
                    load_x(0)
                    load_c(0)
                    sp.wait_ge(setup_v, 1)
                    for t in range(ROWT):
                        sp.dma_start(slots.rearrange("(s t p) n -> p s t n", t=ROWT, p=P)[:, :, t, :],
                                     rows[:, 0:1, :].broadcast_to([P, SLOTS // (ROWT * P), ROW])
                                     ).then_inc(slots_clear, 16)
                    load_x(1)
                    load_c(1)
                    batch(0, False, True)
                    with sp.Fori(1, BATCH - 2) as b:
                        batch(b, True, True)
                    batch(BATCH - 2, True, False)
                    batch(BATCH - 1, True, False)
                    store(BATCH - 1)
                    sp.wait_ge(base_stored, 16 * BATCH)
                    sp.wait_ge(scattered, 64 * BATCH)

                @block.tensor
                def _(pe):
                    pe.wait_ge(consts_in, 16 * SETUP_DMAS)

                    def dft(b, folded, ready, first_unit, after_gate):
                        pe.wait_ge(ready, b * 2 + 2)
                        for u in range(4):
                            if u < 2:
                                if first_unit:
                                    if after_gate:
                                        pe.wait_ge(g_ev, (b - 1) * 4)
                                    pe.wait_ge(f1_ev, b * 8 + first_unit)
                                else:
                                    wait(pe, f1_ev, b * 8)
                            else:
                                pe.wait_ge(f1_ev, b * 8 + first_unit + u - 1)
                            ps = xt_ps[u % 2]
                            for eo in range(2):
                                for t in range(2):
                                    last = nc.tensor.matmul(ps[:, eo * 256:eo * 256 + 256],
                                                            folded[:, eo, t, u * P:(u + 1) * P], fwd[:, t, eo, :],
                                                            start=(t == 0), stop=(t == 1))
                            last.then_inc(f1_mm, 1)

                    def project(b, k):
                        tile, which = PROJ[k]
                        wh, wl = ((w_kh, w_kl), (w_vh, w_vl))[which - 1]
                        terms = ((q_spec, w_q),) if which == 0 else ((c_high, wh), (c_low, wh), (c_high, wl))
                        if k == 0:
                            pe.wait_ge(f1_ev, b * 8 + 4)
                        if k == 1:
                            pe.wait_ge(c_split, b * 2 + 2)
                        wait(pe, conv, b * CONV + (k - 1) * 4)
                        for s in range(2):
                            for c in range(CB):
                                for n, (spec, w) in enumerate(terms):
                                    last = nc.tensor.matmul(pair[k % 2][:, s, :],
                                                            spec[:, c, tile * 256 + s * P:tile * 256 + (s + 1) * P],
                                                            w[:, c, :], start=(c == 0 and n == 0),
                                                            stop=(c == CB - 1 and n == len(terms) - 1))
                        last.then_inc(f2_mm, 1)

                    def inverse(b):
                        pe.wait_ge(ham, b * HAM + HAM_O)
                        pe.wait_ge(real_stored, b * 16 + 16)
                        wait(pe, route, b * ROUTE)
                        for t in range(2):
                            for tile, ps in ((0, even_ps), (1, odd_ps)):
                                if t:
                                    pe.wait_ge(unfold, b * UNF + (2 if tile == 0 else 4))
                                for s in range(2):
                                    last = nc.tensor.matmul(ps[:], inv[:, tile, s, t * P:(t + 1) * P],
                                                            r_spec[:, tile, s].rearrange("p c e -> p (c e)"),
                                                            start=(s == 0), stop=(s == 1))
                                last.then_inc(inv_mm, 1)

                    def router(b, f1_done):
                        for t in range(ROWT):
                            pe.wait_ge(tok_ready, b * 4 + t + 1)
                            if t < 2:
                                pe.wait_ge(f1_ev, f1_done)
                            else:
                                pe.wait_ge(g_ev, b * 4 + t - 1)
                            for c in range(CB):
                                last = nc.tensor.transpose(xt_ps[t % 2][:, c * P:(c + 1) * P],
                                                           x_tok[:, t, c * P:(c + 1) * P], eye[:])
                            last.then_inc(g_mm, 1)
                            if t:
                                logits(b, t - 1)
                        logits(b, ROWT - 1)

                    def logits(b, t):
                        pe.wait_ge(g_ev, b * 4 + t + 1)
                        if t == 0:
                            pe.wait_ge(unfold, b * UNF + UNF)
                        for c in range(CB):
                            last = nc.tensor.matmul(even_ps[:, t * EXPERTS:(t + 1) * EXPERTS], x_tok_t[t % 2][:, c, :],
                                                    gate_g[:, c, :], start=(c == 0), stop=(c == CB - 1))
                        last.then_inc(logit_mm, 1)

                    def ranks(b):
                        pe.wait_ge(route, b * ROUTE + 6)
                        for t in range(ROWT + 1):
                            o = odd_ps[:, t * EXPERTS:(t + 1) * EXPERTS]
                            for u in range(t):
                                last = nc.tensor.matmul(o, ones[:], onehot[:, u, :], start=(u == 0),
                                                        stop=(t == ROWT and u == t - 1))
                            if t < ROWT:
                                nc.tensor.matmul(o, tri[:], onehot[:, t, :], start=(t == 0), stop=True)
                        last.then_inc(rank_mm, 1)

                    pe.wait_ge(setup_v, 11)
                    for c in range(CB):
                        last = nc.tensor.matmul(even_ps[:, 0:EXPERTS], ones32, gate_b[:, c, :], start=(c == 0), stop=(c == CB - 1))
                    last.then_inc(setup_mm, 1)
                    pe.wait_ge(setup_v, 12)
                    pe.wait_ge(w_split, 2)
                    dft(0, q_fold, qf_ready, 0, False)
                    dft(0, c_fold, cf_ready, 4, False)

                    def batch(b, back, ahead):
                        project(b, 0)
                        project(b, 1)
                        if back:
                            inverse(b - 1)
                        project(b, 2)
                        project(b, 3)
                        project(b, 4)
                        if ahead:
                            dft(b + 1, q_fold, qf_ready, 0, back)
                        project(b, 5)
                        if back:
                            router(b - 1, b * 8 + (12 if ahead else 8))
                        if ahead:
                            dft(b + 1, c_fold, cf_ready, 4, back)
                        if back:
                            ranks(b - 1)

                    batch(0, False, True)
                    with pe.Fori(1, BATCH - 1) as b:
                        batch(b, True, True)
                    batch(BATCH - 1, True, False)
                    inverse(BATCH - 1)
                    router(BATCH - 1, BATCH * 8)
                    ranks(BATCH - 1)

                @block.scalar
                def _(act):
                    act.wait_ge(consts_in, 16 * SETUP_DMAS)
                    for n in range(2):
                        nc.scalar.activation(w_raw[:, n], w_raw[:, n], ACT.Copy, scale=memory_scale()).then_inc(scaled, 1)
                    for n, high in enumerate((w_kh, w_vh)):
                        act.wait_ge(scaled, n + 1)
                        nc.scalar.activation(high[:], w_raw[:, n], ACT.Copy).then_inc(scaled, 1)

                    def q_of(b):
                        act.wait_ge(stat1, b * STAT1 + STAT1)
                        wait(act, qf_ready, b * 2)
                        for t in range(ROWT):
                            nc.scalar.activation(q_rows[:, t, :], x_in[:, t, :], ACT.Identity, bias=q_bias[:, t:t + 1],
                                                 scale=q_scale[:, t:t + 1]).then_inc(q_ready, 1)

                    def spectra(b, spec, first_unit):
                        for u in range(4):
                            act.wait_ge(f1_mm, b * 8 + first_unit + u + 1)
                            if u == 0:
                                wait(act, f2_mm, b * 6 - (1 if first_unit == 0 else 0))
                            nc.scalar.activation(spec[:, u, :], xt_ps[u % 2][:], ACT.Copy).then_inc(f1_ev, 1)

                    def context_high(b):
                        act.wait_ge(f1_ev, b * 8 + 8)
                        nc.scalar.activation(c_high[:], c_spec[:], ACT.Copy).then_inc(c_split, 1)

                    def real_parts(b, k):
                        tile, which = PROJ[k]
                        act.wait_ge(f2_mm, b * 6 + k + 1)
                        if k == 0:
                            wait(act, real_loaded, b * 16)
                        if tile == 0:
                            nc.scalar.activation(real_row[0:1, which], pair[k % 2][0:1, :, :], ACT.Copy)
                        wait(act, conv, b * CONV + (k - 1) * 4)
                        nc.scalar.activation(re_buf[k % 2][:], pair[k % 2][:, 0, :], ACT.Copy).then_inc(re_ready, 1)

                    def tokens(b):
                        act.wait_ge(stat2, b * STAT2 + STAT2)
                        wait(act, logit_mm, b * 4)
                        for t in range(ROWT):
                            nc.scalar.activation(x_tok[:, t, :], rows[:, t, 0:DIM], ACT.Identity,
                                                 bias=rows[:, t, DIM + 3:DIM + 4],
                                                 scale=rows[:, t, DIM + 2:DIM + 3]).then_inc(tok_ready, 1)
                        wait(act, base_stored, b * 16)
                        for t in range(ROWT):
                            nc.scalar.activation(base[:, t, :], rows[:, t, 0:DIM], ACT.Identity,
                                                 bias=rows[:, t, DIM + 5:DIM + 6],
                                                 scale=rows[:, t, DIM + 4:DIM + 5]).then_inc(base_ready, 1)

                    def token_blocks(b):
                        for t in range(ROWT):
                            act.wait_ge(g_mm, b * 4 + t + 1)
                            if t < 2:
                                wait(act, logit_mm, b * 4)
                            else:
                                act.wait_ge(logit_mm, b * 4 + t - 1)
                            nc.scalar.activation(x_tok_t[t % 2][:].rearrange("p c e -> p (c e)"), xt_ps[t % 2][:],
                                                 ACT.Copy).then_inc(g_ev, 1)

                    def exps(b):
                        act.wait_ge(route, b * ROUTE + 3)
                        nc.scalar.activation(e_over[:], over[:], ACT.Exp).then_inc(exp_done, 1)

                    q_of(0)
                    spectra(0, q_spec, 0)
                    spectra(0, c_spec, 4)
                    context_high(0)

                    def batch(b, back, ahead):
                        real_parts(b, 0)
                        real_parts(b, 1)
                        real_parts(b, 2)
                        if ahead:
                            q_of(b + 1)
                        real_parts(b, 3)
                        real_parts(b, 4)
                        if back:
                            tokens(b - 1)
                        if ahead:
                            spectra(b + 1, q_spec, 0)
                        real_parts(b, 5)
                        if back:
                            token_blocks(b - 1)
                        if ahead:
                            spectra(b + 1, c_spec, 4)
                        if back:
                            exps(b - 1)
                        if ahead:
                            context_high(b + 1)

                    batch(0, False, True)
                    with act.Fori(1, BATCH - 1) as b:
                        batch(b, True, True)
                    batch(BATCH - 1, True, False)
                    tokens(BATCH - 1)
                    token_blocks(BATCH - 1)
                    exps(BATCH - 1)

                @block.gpsimd
                def _(pool):
                    s1c = Chain(pool, stat1, STAT1)
                    s2c = Chain(pool, stat2, STAT2)
                    rc = Chain(pool, real_step, REAL)
                    ts, tv = nc.gpsimd.tensor_scalar, nc.gpsimd.tensor_tensor

                    k = {n: t[:] for n, t in const.items()}
                    for n, v in values.items():
                        nc.gpsimd.memset(k[n], v).then_inc(zeroed, 1)
                    for dst, v in ((ones32, 1.0), (running[:], 0.0), (rows[:], 0.0)):
                        nc.gpsimd.memset(dst, v).then_inc(zeroed, 1)
                    pool.wait_ge(zeroed, ZEROED - 1)
                    pool.wait_ge(consts_in, 16 * SETUP_DMAS)
                    ts(bias16[:], bias16[:], float(SEQ), 0.0, ALU.mult, ALU.add).then_inc(zeroed, 1)
                    pool.wait_ge(zeroed, ZEROED)

                    def stats1(b):
                        pool.wait_ge(bn1_step, b * BN + BN)
                        wait(pool, q_ready, b * 4)
                        c = s1c
                        c.begin(b)
                        mean, var = mv1[:, :, 0], mv1[:, :, 1]
                        a, rstd, r2, n2, norm, e, s, u, v, rs = (z[:] for z in st)
                        c.step(tv(a, var, k["eps"], ALU.add)); c.wait()
                        c.step(tv(rstd, a, k["minus_half"], ALU.pow)); c.wait()
                        c.step(tv(r2, rstd, rstd, ALU.mult)); c.wait()
                        c.step(tv(n2, var, r2, ALU.mult)); c.wait()
                        c.step(tv(n2, n2, k["dim"], ALU.mult)); c.wait()
                        c.step(tv(norm, n2, k["half"], ALU.pow)); c.wait()
                        c.step(tv(e, k["inv_e"], norm, ALU.pow)); c.wait()
                        c.step(tv(e, e, k["one"], ALU.add)); c.wait()
                        c.step(tv(s, e, k["minus_one"], ALU.pow)); c.wait()
                        for _ in range(MAP_STEPS):
                            c.step(tv(u, s, k["r_map"], ALU.mult))
                            c.step(tv(v, k["one"], s, ALU.subtract)); c.wait()
                            c.step(tv(s, u, v, ALU.mult)); c.wait()
                        c.step(tv(s, s, k["strength"], ALU.mult)); c.wait()
                        c.step(tv(s, s, k["rest"], ALU.add)); c.wait()
                        c.step(tv(rs, s, pos[:], ALU.mult)); c.wait()
                        c.step(tv(q_scale[:], rs, rstd, ALU.mult))
                        c.step(tv(u, k["zero"], mean, ALU.subtract)); c.wait()
                        c.step(tv(q_bias[:], u, q_scale[:], ALU.mult))
                        c.end()

                    def stats2(b):
                        pool.wait_ge(bn2_step, b * BN + BN)
                        c = s2c
                        c.begin(b)
                        mean, var = mv2[:, :, 0], mv2[:, :, 1]
                        a, rstd, r2, v2, n2, neg = (z[:] for z in tt)
                        meta = rows[:, :, DIM:DIM + META]
                        a2, nb2, s1_, nb = (meta[:, :, k] for k in (2, 3, 4, 5))
                        c.step(tv(a, var, k["eps"], ALU.add))
                        c.step(tv(neg, k["zero"], mean, ALU.subtract)); c.wait()
                        c.step(tv(rstd, a, k["minus_half"], ALU.pow)); c.wait()
                        c.step(tv(r2, rstd, rstd, ALU.mult)); c.wait()
                        c.step(tv(v2, var, r2, ALU.mult)); c.wait()
                        c.step(tv(v2, v2, k["eps"], ALU.add)); c.wait()
                        c.step(tv(n2, v2, k["minus_half"], ALU.pow)); c.wait()
                        c.step(tv(a2, rstd, n2, ALU.mult))
                        c.step(tv(s1_, rstd, k["one"], ALU.add)); c.wait()
                        c.step(tv(nb, neg, rstd, ALU.mult))
                        c.step(tv(nb2, neg, a2, ALU.mult))
                        c.end()

                    def fold(b, src, dst, ready, source, users):
                        pool.wait_ge(*source)
                        wait(pool, f1_mm, users)
                        for eo, op in ((0, ALU.add), (1, ALU.subtract)):
                            tv(dst[:, eo], src[:, 0:2], src[:, 2:4], op).then_inc(ready, 1)

                    def real_bins(b):
                        pool.wait_ge(real_loaded, b * 16 + 16)
                        wait(pool, real_stored, b * 16)
                        c = rc
                        c.begin(b)
                        c.step(tv(real_in[:, :, 0], real_in[:, :, 0], bias16[:], ALU.add)); c.wait()
                        left = real_in[:, 0]
                        for which, to in ((1, real_u), (2, real_p)):
                            right = real_in[:, which]
                            for s in range(2):
                                for d in range(4):
                                    a_ = left[:, s, d:d + 1, :]
                                    if d == 0:
                                        o, i0, i1 = real_t[:, s, 0], a_.broadcast_to([16, 4, 8]), right[:, s]
                                    else:
                                        o = real_t[:, s, d].rearrange("q (h l) e -> q h l e", h=2)
                                        i0 = bass.AP(a_.tensor, a_.offset, [list(a_.ap[0]), [0, 2], [0, 2], [1, 8]])
                                        r0 = right[:, s, d:d + 1, :]
                                        i1 = bass.AP(r0.tensor, r0.offset, [list(r0.ap[0]), [16 if d == 1 else -16, 2],
                                                                            [8 if d == 2 else -8, 2], [1, 8]])
                                    c.step(tv(o, i0, i1, ALU.mult))
                            c.wait()
                            for s in range(2):
                                c.step(tv(real_t[:, s, 1:4], real_t[:, s, 1:4], signs[:], ALU.mult))
                            c.wait()
                            c.step(tv(real_v[:], real_t[:, :, 0], real_t[:, :, 1], ALU.add))
                            c.step(tv(real_t[:, :, 2], real_t[:, :, 2], real_t[:, :, 3], ALU.add)); c.wait()
                            c.step(tv(to[:], real_v[:], real_t[:, :, 2], ALU.add))
                            if which == 1:
                                c.wait()
                            left = real_u[:]
                        c.end()

                    def scatter(b):
                        pool.wait_ge(route, b * ROUTE + ROUTE)
                        pool.wait_ge(base_ready, b * 4 + 4)
                        tv(token[:], token[:], k["seq"], ALU.add).then_inc(token_next, 1)
                        for t in range(ROWT):
                            nc.gpsimd.indirect_dma_start(
                                slots, bass.IndirectOffsetOnAxis(ap=slot_i[:, t:t + 1].bitcast(u32), axis=0),
                                rows[:, t, :], None, bounds_check=SLOTS - 1, oob_is_err=False).then_inc(scattered, 16)

                    def folds_q(b):
                        fold(b, q_rows, q_fold, qf_ready, (q_ready, b * 4 + 4), b * 8 - 4)

                    def folds_c(b):
                        fold(b, c_in, c_fold, cf_ready, (c_loaded, b * 16 + 16), b * 8)

                    stats1(0)
                    folds_q(0)
                    folds_c(0)
                    pool.wait_ge(slots_clear, 64)

                    def batch(b, back, ahead):
                        if ahead:
                            stats1(b + 1)
                        if back:
                            stats2(b - 1)
                        if ahead:
                            folds_q(b + 1)
                        real_bins(b)
                        if ahead:
                            folds_c(b + 1)
                        if back:
                            scatter(b - 1)

                    batch(0, False, True)
                    with pool.Fori(1, BATCH - 1) as b:
                        batch(b, True, True)
                    batch(BATCH - 1, True, False)
                    stats2(BATCH - 1)
                    scatter(BATCH - 1)

                @block.vector
                def _(dve):
                    v = nc.vector
                    setup = Chain(dve, setup_v, 12)
                    bn1c, bn2c = Chain(dve, bn1_step, BN), Chain(dve, bn2_step, BN)
                    hc, uc, ro = Chain(dve, ham, HAM), Chain(dve, unfold, UNF), Chain(dve, route, ROUTE)

                    dve.wait_ge(consts_in, 16 * SETUP_DMAS)
                    dve.wait_ge(zeroed, ZEROED - 1)
                    setup.begin(0)
                    setup.step(v.tensor_scalar(rows[:, 0, DIM:DIM + 1].bitcast(i32), token[:, 0:1], 0.0,
                                               float(BATCH * SEQ), ALU.mult, ALU.add))
                    setup.step(v.tensor_copy(tri[:], tri32))
                    setup.step(v.tensor_copy(ones[:], ones32))
                    for c in range(CB):
                        setup.step(v.tensor_scalar(gate_b[:, c, :], gate_t[:, c, :], bet[:, c:c + 1], None, ALU.mult))
                        setup.step(v.tensor_scalar(gate_g[:, c, :], gate_t[:, c, :], gam[:, c:c + 1], None, ALU.mult))
                    dve.wait_ge(scaled, 4)
                    for n, (high, low) in enumerate(((w_kh, w_kl), (w_vh, w_vl))):
                        v.tensor_tensor(low[:], w_raw[:, n], high[:].bitcast(f32), ALU.subtract).then_inc(w_split, 1)
                    dve.wait_ge(w_split, 2)
                    dve.wait_ge(setup_mm, 1)
                    setup.step(v.tensor_copy(gate_c[:], even_ps[:, 0:EXPERTS]))
                    setup.end()
                    setup.wait()

                    def context_low(b):
                        dve.wait_ge(c_split, b * 2 + 1)
                        v.tensor_tensor(c_low[:], c_spec[:], c_high[:].bitcast(f32), ALU.subtract).then_inc(c_split, 1)

                    def stats(b, c, src, bn, ready):
                        c.begin(b)
                        dve.wait_ge(*ready)
                        for t in range(ROWT):
                            c.step(v.bn_stats(bn[:, t, :], src[:, t, 0:DIM]))

                    def mean_var(c, bn, mv):
                        for t in range(ROWT):
                            c.step(v.bn_aggr(mv[:, t, :], bn[:, t, :]))
                        c.end()

                    def stats_x(b):
                        wait(dve, stat1, b * STAT1)
                        stats(b, bn1c, x_in, bn1, (x_loaded, b * 16 + 16))

                    def convert(b, k, dst, free):
                        dve.wait_ge(re_ready, b * 6 + k + 1)
                        if free is not None:
                            dve.wait_ge(*free)
                        re = re_buf[k % 2][:].rearrange("p (h l e) -> p h l e", h=2, l=2)
                        im = pair[k % 2][:, 1, :].rearrange("p (h l e) -> p h l e", h=2, l=2)
                        a_b, d_c = dst[:, :, 0:2, :], down(dst, 3)
                        wy_re, xz_re, wy_im, xz_im = re[:, :, 0], re[:, :, 1], im[:, :, 0], im[:, :, 1]
                        v.tensor_tensor(a_b[:, 0], wy_re, xz_im, ALU.subtract).then_inc(conv, 1)
                        v.tensor_tensor(a_b[:, 1], xz_re, wy_im, ALU.add).then_inc(conv, 1)
                        v.tensor_tensor(d_c[0], wy_re, xz_im, ALU.add).then_inc(conv, 1)
                        v.tensor_tensor(d_c[1], wy_im, xz_re, ALU.subtract).then_inc(conv, 1)

                    def down(s, start):
                        out_ = []
                        for slot in range(2):
                            r = s[:, slot, start:start + 1, :]
                            out_.append(bass.AP(r.tensor, r.offset, [list(r.ap[0]), [-P, 2], [1, P]]))
                        return out_

                    def view(s, slot, first_, steps):
                        r = s[:, slot, first_:first_ + 1, :]
                        return bass.AP(r.tensor, r.offset, [list(r.ap[0]), [steps[0] * P, 2], [steps[1] * P, 2], [1, P]])

                    def hamilton(b, k, sources, statistics=False):
                        dve.wait_ge(*sources)
                        wait(dve, ham, hc.base + hc.n)
                        n0 = hc.n
                        for m, (i, j) in enumerate(((0, 0), (1, 1), (0, 1), (1, 0))):
                            o = prod[:, m].rearrange("p w (h l e) -> p w h l e", h=2, l=2)
                            hc.step(v.tensor_tensor(o[:, 0], view(s1, i, 0, (3, 0)), view(s2, j, 0, (2, 1)), ALU.mult))
                            if statistics and m == 0:
                                mean_var(bn2c, bn2, mv2)
                            hc.step(v.tensor_tensor(o[:, 1], view(s1, i, 1, (1, 0)), view(s2, j, 2, (-2, 1)), ALU.mult))
                        hc.wait(n0 + 4)
                        hc.step(v.tensor_tensor(prod[:, 0], prod[:, 0], prod[:, 1], ALU.subtract))
                        hc.wait(n0 + 8)
                        hc.step(v.tensor_tensor(prod[:, 2], prod[:, 2], prod[:, 3], ALU.add))
                        hc.wait()
                        parts = prod[:].rearrange("p (s z) w (c e) -> p s z w c e", s=2, c=4)[:, :, 0]
                        hc.step(v.tensor_tensor(s1[:, :, 1:3, :], parts[:, :, 0, 1:3], parts[:, :, 1, 1:3], ALU.add))
                        hc.step(v.tensor_tensor(s1[:, :, 0:4:3, :], parts[:, :, 0, 0:4:3], parts[:, :, 1, 0:4:3], ALU.subtract))

                    def back_to_parts(b, tile):
                        hc.wait()
                        r = r_spec[:, tile].rearrange("p s (h l) e -> p s h l e", h=2)
                        d_c = down(s1, 3)
                        both = bass.AP(d_c[0].tensor, d_c[0].offset, [list(d_c[0].ap[0]), [4 * P, 2], [-P, 2], [1, P]])
                        hc.step(v.tensor_tensor(r[:, :, :, 0], s1[:, :, 0:2, :], both, ALU.add))
                        hc.step(v.tensor_tensor(r[:, 0, :, 1], s1[:, 1, 0:2, :], d_c[1], ALU.subtract))
                        hc.step(v.tensor_tensor(r[:, 1, :, 1], d_c[0], s1[:, 0, 0:2, :], ALU.subtract))

                    def add_attended(b):
                        uc.begin(b)
                        dve.wait_ge(res_loaded, b * 16 + 16)
                        wait(dve, scattered, b * 64)
                        wait(dve, base_ready, b * 4)
                        for t in range(2):
                            lo, hi = rows[:, t, 0:DIM], rows[:, t + 2, 0:DIM]
                            dve.wait_ge(inv_mm, b * 4 + 2 * t + 1)
                            uc.step(v.tensor_tensor(lo, x_res[:, t, :], even_ps[:], ALU.add))
                            n = uc.step(v.tensor_tensor(hi, x_res[:, t + 2, :], even_ps[:], ALU.add))
                            dve.wait_ge(inv_mm, b * 4 + 2 * t + 2)
                            uc.wait(n)
                            uc.step(v.tensor_tensor(lo, lo, odd_ps[:], ALU.add))
                            uc.step(v.tensor_tensor(hi, hi, odd_ps[:], ALU.subtract))
                        uc.end()

                    def stats_x2(b):
                        wait(dve, stat2, b * STAT2)
                        stats(b, bn2c, rows, bn2, (unfold, b * UNF + UNF))

                    def choose(b):
                        dve.wait_ge(logit_mm, b * 4 + 4)
                        wait(dve, rank_mm, b)
                        ro.begin(b)
                        lg = even_ps[:, 0:ROWT * EXPERTS].rearrange("p (t e) -> p t e", t=ROWT)
                        ro.step(v.tensor_tensor(logit[:], lg, bass.AP(gate_c[:].tensor, gate_c[:].offset, [list(gate_c[:].ap[0]), [0, ROWT], [1, EXPERTS]]), ALU.add)); ro.wait()
                        ro.step(v.tensor_reduce(top[:], logit[:], AX.X, ALU.max)); ro.wait()
                        ro.step(v.tensor_tensor(over[:], logit[:], top[:].unsqueeze(2).broadcast_to([P, ROWT, EXPERTS]), ALU.subtract)); ro.wait()
                        ro.step(v.scalar_tensor_tensor(cand[:], over[:], 0.0, iota8[:], ALU.is_ge, ALU.mult)); ro.wait()
                        ro.step(v.tensor_reduce(first[:], cand[:], AX.X, ALU.min)); ro.wait()
                        ro.step(v.tensor_tensor(onehot[:], iota8[:], first[:].unsqueeze(2).broadcast_to([P, ROWT, EXPERTS]), ALU.is_equal))

                    def place(b):
                        dve.wait_ge(exp_done, b + 1)
                        ro.step(v.tensor_reduce(denom[:], e_over[:], AX.X, ALU.add)); ro.wait()
                        ro.step(v.reciprocal(rows[:, :, DIM + 1], denom[:]))
                        wait(dve, token_next, b)
                        ro.step(v.tensor_scalar(rows[:, :, DIM].bitcast(i32), token[:], 1.0, None, ALU.mult))
                        dve.wait_ge(rank_mm, b + 1)
                        rk = odd_ps[:, 0:ROWT * EXPERTS].rearrange("p (t e) -> p t e", t=ROWT)
                        ro.step(v.tensor_tensor(cand[:], rk, bass.AP(running[:].tensor, running[:].offset, [list(running[:].ap[0]), [0, ROWT], [1, EXPERTS]]), ALU.add)); ro.wait()
                        ro.step(v.tensor_tensor(running[:], running[:], odd_ps[:, ROWT * EXPERTS:(ROWT + 1) * EXPERTS], ALU.add))
                        ro.step(v.tensor_tensor(picked[:], cand[:], onehot[:], ALU.mult)); ro.wait()
                        ro.step(v.tensor_reduce(rank[:], picked[:], AX.X, ALU.add)); ro.wait()
                        ro.step(v.tensor_scalar(far[:], rank[:], float(CAPACITY), float(SKIPPED), ALU.is_ge, ALU.mult))
                        ro.step(v.scalar_tensor_tensor(slot_f[:], first[:], float(CAPACITY), rank[:], ALU.mult, ALU.add)); ro.wait()
                        ro.step(v.scalar_tensor_tensor(slot_i[:], slot_f[:], float(CAPACITY * EXPERTS), far[:], ALU.add, ALU.add))
                        ro.wait()
                        ro.end()

                    stats_x(0)
                    bn1c.wait()
                    mean_var(bn1c, bn1, mv1)

                    def batch(b, back, ahead):
                        if ahead:
                            stats_x(b + 1)
                            bn1c.wait()
                        context_low(b)
                        hc.begin(b)
                        convert(b, 0, s1, (ham, b * HAM) if back else None)
                        if ahead:
                            mean_var(bn1c, bn1, mv1)
                        convert(b, 1, s2, None)
                        if back:
                            add_attended(b - 1)
                            stats_x2(b - 1)
                            bn2c.wait()
                        hamilton(b, 1, (conv, b * CONV + 8), back)
                        convert(b, 2, s2, (ham, b * HAM + 8))
                        hc.wait()
                        hamilton(b, 2, (conv, b * CONV + 12))
                        wait(dve, inv_mm, b * 4)
                        back_to_parts(b, 0)
                        convert(b, 3, s1, (ham, b * HAM + HAM_E))
                        convert(b, 4, s2, None)
                        hamilton(b, 4, (conv, b * CONV + 20))
                        convert(b, 5, s2, (ham, b * HAM + HAM_E + 8))
                        hc.wait()
                        hamilton(b, 5, (conv, b * CONV + 24))
                        back_to_parts(b, 1)
                        hc.end()
                        if back:
                            choose(b - 1)
                            place(b - 1)

                    batch(0, False, True)
                    dve.wait_ge(slots_clear, 64)
                    with dve.Fori(1, BATCH - 1) as b:
                        batch(b, True, True)
                    batch(BATCH - 1, True, False)
                    add_attended(BATCH - 1)
                    stats_x2(BATCH - 1)
                    bn2c.wait()
                    mean_var(bn2c, bn2, mv2)
                    choose(BATCH - 1)
                    place(BATCH - 1)

        experts(nc, outer, slots, gamma, beta, c_eye, wi, wo, out)


def experts(nc, outer, slots, gamma, beta, c_eye, wi, wo, out):
    f32, f32r, u32 = mybir.dt.float32, mybir.dt.float32r, mybir.dt.uint32
    ALU, ACT = mybir.AluOpType, mybir.ActivationFunctionType

    def sem(name):
        return outer.enter_context(nc.semaphore(name))

    with ExitStack() as mem:
        def sb(name, shape, dt=f32):
            return mem.enter_context(nc.sbuf_tensor(name, shape, dt))

        def pb(name, shape):
            return mem.enter_context(nc.psum_tensor(name, shape, f32))

        eye = sb("eye2", [P, P])
        gam, bet = sb("gam2", [P, CB]), sb("bet2", [P, CB])
        got = [sb(f"got{i}", [P, GT, ROW]) for i in (0, 1)]
        normed = sb("normed", [P, GT, DIM])
        tok32 = [sb(f"tok32_{i}", [P, GROUP]) for i in (0, 1)]
        tok_h = [sb(f"tok_h{i}", [P, CB, GROUP], f32r) for i in (0, 1)]
        tok_l = [sb(f"tok_l{i}", [P, CB, GROUP], f32r) for i in (0, 1)]
        w_raw = [sb(f"w_raw{i}", [P, 2, 1024]) for i in (0, 1)]
        w_h = [sb(f"w_h{i}", [P, 2, 1024], f32r) for i in range(RING)]
        w_l = [sb(f"w_l{i}", [P, 2, 1024], f32r) for i in range(RING)]
        act32 = [sb(f"act32_{i}", [P, GROUP]) for i in (0, 1)]
        act_h = [sb(f"act_h{i}", [P, GROUP], f32r) for i in range(4)]
        act_l = [sb(f"act_l{i}", [P, GROUP], f32r) for i in range(4)]
        res = sb("res", [P, GT, DIM])
        mixed = sb("mixed", [P, GT, DIM])
        tally, unit = sb("tally", [1, 1]), sb("unit", [1, 1])

        hid_ps = [pb(f"hid_ps{i}", [P, 512]) for i in (0, 1)]
        tr_ps = [pb(f"tr_ps{i}", [P, 512]) for i in (0, 1)]
        out_ps = [pb(f"out_ps{i}", [P, 512]) for i in range(GT)]

        const2_in = sem("const2_in")
        tallied, cleared = sem("tallied"), sem("cleared")
        got_in = [sem(f"got_in{i}") for i in (0, 1)]
        raw_in = [sem(f"raw_in{i}") for i in (0, 1)]
        wh_ready, wl_ready = sem("wh_ready"), sem("wl_ready")
        normed_ready = sem("normed_ready")
        tr_mm, th_ready, tv_ready, tl_ready = sem("tr_mm"), sem("th_ready"), sem("tv_ready"), sem("tl_ready")
        hid_mm, gelu, ah_ready, al_ready, out_mm = sem("hid_mm"), sem("gelu"), sem("ah_ready"), sem("al_ready"), sem("out_mm")
        res_ready, mixed_ready, mixed_stored = sem("res_ready"), sem("mixed_ready"), sem("mixed_stored")

        def group(e, g):
            return e * 2 + g

        with nc.Block() as block:
            @block.sync
            def _(sp):
                for dst, src in ((eye[:], c_eye), (gam[:], gamma),
                                 (bet[:], beta)):
                    sp.dma_start(dst, src).then_inc(const2_in, 16)

                def rows_of(e, g):
                    wait(sp, mixed_stored, e * 128 - 64 + 64 * g)
                    src = slots.rearrange("(a t p) n -> a p t n", t=GT, p=P)
                    sp.dma_start(got[g][:], src[bass.ds(e * 2 + g, 1)].rearrange("a p t n -> p (a t) n")).then_inc(got_in[g], 16)

                def weights(e, g, k):
                    n = group(e, g) * PAIRS + k
                    wait(sp, wl_ready, n - 1)
                    wait(sp, wh_ready, n - 1)
                    raw = w_raw[k % 2]
                    sp.dma_start(raw[:, 0].rearrange("p (c n) -> p c n", c=CB),
                                 wi[bass.ds(e, 1), :, k * 256:(k + 1) * 256].rearrange("a (c p) n -> p (a c) n", p=P)
                                 ).then_inc(raw_in[k % 2], 16)
                    sp.dma_start(raw[:, 1].rearrange("p (c n) -> p c n", c=2),
                                 wo[bass.ds(e, 1), k * 256:(k + 1) * 256, :].rearrange("a (c p) n -> p (a c) n", p=P)
                                 ).then_inc(raw_in[k % 2], 16)

                def expert(e, more):
                    for g in range(2):
                        for k in range(PAIRS):
                            weights(e, g, k)
                            if k == 1:
                                if g == 0:
                                    rows_of(e, 1)
                                elif more:
                                    rows_of(e + 1, 0)

                rows_of(0, 0)
                expert(0, True)
                with sp.Fori(1, EXPERTS - 1) as e:
                    expert(e, True)
                expert(EXPERTS - 1, False)

            @block.gpsimd
            def _(pool):
                nc.gpsimd.memset(tally[:], 0.0).then_inc(cleared, 1)
                nc.gpsimd.memset(unit[:], 1.0).then_inc(cleared, 1)
                pool.wait_ge(cleared, 2)

                def store(e, g):
                    wait(pool, tallied, group(e, g))
                    pool.wait_ge(mixed_ready, group(e, g) * GT + GT)
                    nc.gpsimd.tensor_tensor(tally[:], tally[:], unit[:], ALU.add).then_inc(tallied, 1)
                    for t in range(GT):
                        nc.gpsimd.indirect_dma_start(
                            out.rearrange("b s n -> (b s) n"),
                            bass.IndirectOffsetOnAxis(ap=got[g][:, t, DIM:DIM + 1].bitcast(u32), axis=0),
                            mixed[:, t, :], None, bounds_check=BATCH * SEQ - 1, oob_is_err=False).then_inc(mixed_stored, 16)

                store(0, 0)
                store(0, 1)
                with pool.Fori(1, EXPERTS) as e:
                    store(e, 0)
                    store(e, 1)
                pool.wait_ge(mixed_stored, 2 * EXPERTS * GT * 16)

            @block.tensor
            def _(pe):
                pe.wait_ge(const2_in, 48)

                def turn(e, g, c):
                    n = group(e, g)
                    pe.wait_ge(normed_ready, n * GT + GT)
                    wait(pe, tv_ready, n * CB + c - 1)
                    for t in range(GT):
                        last = nc.tensor.transpose(tr_ps[c % 2][:, t * P:(t + 1) * P], normed[:, t, c * P:(c + 1) * P], eye[:])
                    last.then_inc(tr_mm, 1)

                def up(e, g, i):
                    n = group(e, g)
                    if i == 0:
                        pe.wait_ge(tl_ready, n * CB + CB)
                    if i % 2 == 0:
                        pe.wait_ge(wh_ready, n * PAIRS + i // 2 + 1)
                        pe.wait_ge(wl_ready, n * PAIRS + i // 2 + 1)
                    wait(pe, gelu, n * ISTEPS + i - 1)
                    s = (i // 2) % RING
                    wh, wl = (w[s][:, 0].rearrange("p (c n) -> p c n", c=CB)[:, :, (i % 2) * P:(i % 2 + 1) * P] for w in (w_h, w_l))
                    for c in range(CB):
                        for a, b in ((wh, tok_h[g]), (wl, tok_h[g]), (wh, tok_l[g])):
                            first_, last_ = c == 0 and a is wh and b is tok_h[g], c == CB - 1 and b is tok_l[g]
                            last = nc.tensor.matmul(hid_ps[i % 2][:], a[:, c, :], b[:, c, :], start=first_, stop=last_)
                    last.then_inc(hid_mm, 1)

                def down(e, g, i):
                    n = group(e, g)
                    pe.wait_ge(ah_ready, n * ISTEPS + i + 1)
                    pe.wait_ge(al_ready, n * ISTEPS + i + 1)
                    s = (i // 2) % RING
                    oh, ol = (w[s][:, 1, (i % 2) * 512:(i % 2 + 1) * 512] for w in (w_h, w_l))
                    for t in range(GT):
                        if i == 0:
                            wait(pe, mixed_ready, (n - 1) * GT + t + 1)
                        ah, al = act_h[i % 4][:, t * P:(t + 1) * P], act_l[i % 4][:, t * P:(t + 1) * P]
                        nc.tensor.matmul(out_ps[t][:], ah, oh, start=(i == 0), stop=False)
                        nc.tensor.matmul(out_ps[t][:], al, oh, start=False, stop=False)
                        last = nc.tensor.matmul(out_ps[t][:], ah, ol, start=False, stop=(i == ISTEPS - 1))
                    last.then_inc(out_mm, 1)

                def expert(e, more):
                    for g in range(2):
                        for i in range(ISTEPS + 2):
                            if i < ISTEPS:
                                up(e, g, i)
                            if i >= 2:
                                down(e, g, i - 2)
                            if 8 <= i < 8 + CB and (g == 0 or more):
                                turn(e + g, 1 - g, i - 8)

                for c in range(CB):
                    turn(0, 0, c)
                expert(0, True)
                with pe.Fori(1, EXPERTS - 1) as e:
                    expert(e, True)
                expert(EXPERTS - 1, False)

            @block.scalar
            def _(act):
                act.wait_ge(const2_in, 48)

                def norm(e, g):
                    n = group(e, g)
                    act.wait_ge(got_in[g], e * 16 + 16)
                    wait(act, tr_mm, n * CB)
                    for t in range(GT):
                        nc.scalar.activation(normed[:, t, :], got[g][:, t, 0:DIM], ACT.Identity,
                                             bias=got[g][:, t, DIM + 3:DIM + 4],
                                             scale=got[g][:, t, DIM + 2:DIM + 3]).then_inc(normed_ready, 1)

                def affine(e, g, c):
                    n = group(e, g) * CB + c
                    act.wait_ge(tr_mm, n + 1)
                    wait(act, tl_ready, n - 1)
                    nc.scalar.activation(tok32[c % 2][:], tr_ps[c % 2][:], ACT.Identity, bias=bet[:, c:c + 1],
                                         scale=gam[:, c:c + 1]).then_inc(tv_ready, 1)

                def weight_high(e, g, k):
                    n = group(e, g) * PAIRS + k
                    if k % 2 == 0:
                        act.wait_ge(raw_in[0], (group(e, g) * (PAIRS // 2) + k // 2) * 32 + 32)
                    else:
                        act.wait_ge(raw_in[1], (group(e, g) * (PAIRS // 2) + k // 2) * 32 + 32)
                    wait(act, out_mm, (n - RING + 1) * 2)
                    nc.scalar.activation(w_h[k % RING][:], w_raw[k % 2][:], ACT.Copy).then_inc(wh_ready, 1)

                def gelu_of(e, g, i):
                    n = group(e, g) * ISTEPS + i
                    act.wait_ge(hid_mm, n + 1)
                    wait(act, al_ready, n - 1)
                    nc.scalar.activation(act32[i % 2][:], hid_ps[i % 2][:], ACT.Gelu).then_inc(gelu, 1)

                def residual(e, g):
                    n = group(e, g)
                    wait(act, mixed_ready, n * GT)
                    for t in range(GT):
                        nc.scalar.activation(res[:, t, :], got[g][:, t, 0:DIM], ACT.Identity,
                                             bias=got[g][:, t, DIM + 5:DIM + 6],
                                             scale=got[g][:, t, DIM + 4:DIM + 5]).then_inc(res_ready, 1)

                def expert(e, more):
                    for g in range(2):
                        for i in range(ISTEPS):
                            gelu_of(e, g, i)
                            if i % 2 == 1:
                                k = i // 2 + 2
                                if k < PAIRS:
                                    weight_high(e, g, k)
                                elif g == 0:
                                    weight_high(e, 1, k - PAIRS)
                                elif more:
                                    weight_high(e + 1, 0, k - PAIRS)
                            if i == 4:
                                residual(e, g)
                            if g == 0 or more:
                                if i == 6:
                                    norm(e + g, 1 - g)
                                if 8 <= i < 8 + CB:
                                    affine(e + g, 1 - g, i - 8)

                norm(0, 0)
                weight_high(0, 0, 0)
                weight_high(0, 0, 1)
                for c in range(CB):
                    affine(0, 0, c)
                expert(0, True)
                with act.Fori(1, EXPERTS - 1) as e:
                    expert(e, True)
                expert(EXPERTS - 1, False)

            @block.vector
            def _(dve):
                v = nc.vector
                dve.wait_ge(const2_in, 48)

                def token_split(e, g, c):
                    n = group(e, g) * CB + c
                    dve.wait_ge(tv_ready, n + 1)
                    v.tensor_copy(tok_h[g][:, c, :], tok32[c % 2][:]).then_inc(th_ready, 1)
                    dve.wait_ge(th_ready, n + 1)
                    v.tensor_tensor(tok_l[g][:, c, :], tok32[c % 2][:], tok_h[g][:, c, :].bitcast(f32),
                                    ALU.subtract).then_inc(tl_ready, 1)

                def weight_low(e, g, k):
                    n = group(e, g) * PAIRS + k
                    dve.wait_ge(wh_ready, n + 1)
                    v.tensor_tensor(w_l[k % RING][:], w_raw[k % 2][:], w_h[k % RING][:].bitcast(f32), ALU.subtract).then_inc(wl_ready, 1)

                def split(e, g, i):
                    n = group(e, g) * ISTEPS + i
                    dve.wait_ge(gelu, n + 1)
                    wait(dve, out_mm, n - 3)
                    v.tensor_copy(act_h[i % 4][:], act32[i % 2][:]).then_inc(ah_ready, 1)
                    dve.wait_ge(ah_ready, n + 1)
                    v.tensor_tensor(act_l[i % 4][:], act32[i % 2][:], act_h[i % 4][:].bitcast(f32),
                                    ALU.subtract).then_inc(al_ready, 1)

                def mix(e, g):
                    n = group(e, g)
                    dve.wait_ge(out_mm, n * ISTEPS + ISTEPS)
                    dve.wait_ge(res_ready, n * GT + GT)
                    wait(dve, mixed_stored, n * GT * 16)
                    for t in range(GT):
                        v.scalar_tensor_tensor(mixed[:, t, :], out_ps[t][:], got[g][:, t, DIM + 1:DIM + 2], res[:, t, :],
                                               ALU.mult, ALU.add).then_inc(mixed_ready, 1)

                def expert(e, more):
                    for g in range(2):
                        for i in range(ISTEPS):
                            split(e, g, i)
                            if i % 2 == 1:
                                k = i // 2 + 2
                                if k < PAIRS:
                                    weight_low(e, g, k)
                                elif g == 0:
                                    weight_low(e, 1, k - PAIRS)
                                elif more:
                                    weight_low(e + 1, 0, k - PAIRS)
                            if 8 <= i < 8 + CB and (g == 0 or more):
                                token_split(e + g, 1 - g, i - 8)
                        mix(e, g)

                weight_low(0, 0, 0)
                weight_low(0, 0, 1)
                for c in range(CB):
                    token_split(0, 0, c)
                expert(0, True)
                with dve.Fori(1, EXPERTS - 1) as e:
                    expert(e, True)
                expert(EXPERTS - 1, False)


def kernel(**inputs):
    import concourse.bacc as bacc
    from concourse.bass_utils import run_bass_kernel_spmd

    nc = bacc.Bacc("TRN2", target_bir_lowering=False, num_devices=1)
    turned = ("L0_xattn_Wq", "L0_xattn_Wk", "L0_xattn_Wv", "L0_ffn_gate_weight")
    vectors = ("L0_ffn_ln_gamma", "L0_ffn_ln_beta")
    names = ["x", "ctx_1024", "L0_xattn_Wq", "L0_xattn_Wk", "L0_xattn_Wv", "L0_xattn_bq", "L0_xattn_bk", "L0_xattn_bv",
             "L0_ffn_gate_weight", "L0_ffn_ln_gamma", "L0_ffn_ln_beta", "L0_ffn_wi", "L0_ffn_wo"]
    arrays, args = {}, []
    for name in names:
        a = np.asarray(inputs[name])
        if name in vectors:
            a = a.reshape(-1, P)
        a = np.ascontiguousarray(a.T if name in turned + vectors else a)
        arrays[f"in_{name}"] = a
        args.append(nc.dram_tensor(f"in_{name}", a.shape, mybir.dt.from_np(a.dtype), kind="ExternalInput").ap())
    out = nc.dram_tensor("out", (BATCH, SEQ, DIM), mybir.dt.float32, kind="ExternalOutput").ap()
    xattn_moe_kernel(nc, *args, out)
    r = run_bass_kernel_spmd(nc, [arrays], core_ids=[0])
    return r.results[0]["out"]
```

```python
import concourse.bass as bass
import numpy as np
from concourse import mybir
from contextlib import ExitStack

P = 128
BATCH, SEQ, DIM = 32, 512, 512
ROWT = SEQ // P
CB = DIM // P
EXPERTS, INNER = 8, 2048
CAPACITY = 2 * (4 * 1024) // EXPERTS
SLOTS = EXPERTS * CAPACITY
META = 8
ROW = DIM + META
EPS = 1e-5
R_MAP, MAP_STEPS = 3.9, 10
SKIPPED = 1 << 20

GROUP = 512
GT = GROUP // P
ISTEPS = INNER // P
PAIRS = ISTEPS // 2
RING = 4


def sigmoid(v):
    return 1.0 / (1.0 + np.exp(-v))


def memory_scale():
    dop, ser, nor = (0.9 * 0.5 + 0.1 * sigmoid(v) for v in (0.7, 0.8, 0.6))
    return float(0.4 * dop + 0.3 * ser + 0.3 * nor)


def forward_matrix():
    n = np.arange(256)[:, None]
    j = np.arange(128)[None, :]
    m = np.empty((256, 2, 2, 128))
    for tile in (0, 1):
        angle = 2 * np.pi * (((2 * j + tile) * n) % 512) / 512
        m[:, tile, 0], m[:, tile, 1] = np.cos(angle), -np.sin(angle)
    m[:, 0, 1, 0] = 1 - 2 * (np.arange(256) % 2)
    return m.reshape(2, 128, 2, 256).transpose(1, 0, 2, 3).reshape(128, -1).astype(np.float32)


def inverse_matrix():
    k = np.arange(512)
    filt = np.exp(3j * 1.5 * np.arctan(np.log(k + 1e-10)))
    h = (filt + np.conj(filt[-k % 512])) / 2
    n = np.arange(256)[None, :]
    m = np.empty((128, 2, 2, 256))
    for tile in (0, 1):
        f = (2 * np.arange(128) + tile)[:, None]
        e = h[f] * np.exp(2j * np.pi * ((f * n) % 512) / 512) / 512
        m[:, tile, 0], m[:, tile, 1] = e.real, -e.imag
    m[0, 0, 0] = h[0].real / 512
    m[0, 0, 1] = h[256].real * (1 - 2 * (np.arange(256) % 2)) / 512
    return m.reshape(128, -1).astype(np.float32)


def position_scale():
    lam = np.arange(SEQ) / SEQ
    alpha = float(np.clip(1.0 * (1.0 + 0.5 * (1.5 - 2.0) / 2.0), 0.1, 3.0))
    wave = np.sin(alpha * lam) * np.cos(-2.0 * lam + 0.0 * lam ** 2)
    return (1 + 0.1 * wave).reshape(ROWT, P).T.astype(np.float32)


def quaternion_signs():
    return np.array([[-1, 1, -1, 1], [-1, 1, 1, -1], [-1, -1, 1, 1]], np.float32)


class Chain:

    def __init__(self, engine, sem, per):
        self.engine, self.sem, self.per = engine, sem, per

    def begin(self, round_):
        self.base, self.n = round_ * self.per, 0

    def step(self, ins):
        self.n += 1
        ins.then_inc(self.sem, 1)
        return self.n

    def wait(self, n=None):
        self.engine.wait_ge(self.sem, self.base + (self.n if n is None else n))

    def end(self):
        assert self.n == self.per, (self.n, self.per)


def wait(engine, sem, value):
    if not isinstance(value, int) or value > 0:
        engine.wait_ge(sem, value)


def xattn_moe_kernel(nc, x, ctx_in, wq, wk, wv, bq, bk, bv, gate, gamma, beta, wi, wo, out):
    f32, f32r, bf16 = mybir.dt.float32, mybir.dt.float32r, mybir.dt.bfloat16
    i32, u32 = mybir.dt.int32, mybir.dt.uint32
    ALU, ACT, AX = mybir.AluOpType, mybir.ActivationFunctionType, mybir.AxisListType

    c_fwd = nc.inline_tensor(forward_matrix(), "c_fwd").ap()
    c_inv = nc.inline_tensor(inverse_matrix(), "c_inv").ap()
    c_pos = nc.inline_tensor(position_scale(), "c_pos").ap()
    c_sgn = nc.inline_tensor(np.tile(np.repeat(quaternion_signs().reshape(1, 12), 8, 1), (16, 1)), "c_sgn").ap()
    c_tri = nc.inline_tensor(np.triu(np.ones((P, P), np.float32), 1), "c_tri").ap()
    c_eye = nc.inline_tensor(np.eye(P, dtype=np.float32), "c_eye").ap()
    c_tok = nc.inline_tensor((np.arange(SEQ, dtype=np.float32)).reshape(ROWT, P).T.copy(), "c_tok").ap()
    c_exp = nc.inline_tensor(np.tile(np.arange(EXPERTS, dtype=np.float32) - EXPERTS, (P, ROWT)), "c_exp").ap()
    bins_in = nc.dram_tensor("bins_in", [1, 6 * DIM], f32, kind="Internal").ap()
    bins_out = nc.dram_tensor("bins_out", [1, 2 * DIM], f32, kind="Internal").ap()
    slots = nc.dram_tensor("slots", [SLOTS, ROW], f32, kind="Internal").ap()

    outer = ExitStack()
    with outer:
        def sem(name):
            return outer.enter_context(nc.semaphore(name))

        with ExitStack() as mem:
            def sb(name, shape, dt=f32):
                return mem.enter_context(nc.sbuf_tensor(name, shape, dt))

            def pb(name, shape):
                return mem.enter_context(nc.psum_tensor(name, shape, f32))

            fwd = sb("fwd", [P, 2, 2, 256])
            inv = sb("inv", [P, 2, 2, 256])
            w_q = sb("w_q", [P, CB, DIM])
            w_kh, w_kl, w_vh, w_vl = (sb(n, [P, CB, DIM], f32r) for n in ("w_kh", "w_kl", "w_vh", "w_vl"))
            c_high, c_low = (sb(n, [P, CB, 512], f32r) for n in ("c_high", "c_low"))
            pos = sb("pos", [P, ROWT])
            signs = sb("signs", [16, 3, 4, 8])
            tri, ones = sb("tri", [P, P], bf16), sb("ones", [P, P], bf16)
            eye = sb("eye", [P, P])
            token = sb("token", [P, ROWT])
            iota8 = sb("iota8", [P, ROWT, EXPERTS])
            gate_t = sb("gate_t", [P, CB, EXPERTS])
            gate_b = sb("gate_b", [P, CB, EXPERTS])
            gate_g = sb("gate_g", [P, CB, EXPERTS])
            gam, bet = sb("gam", [P, CB]), sb("bet", [P, CB])
            gate_c = sb("gate_c", [P, EXPERTS])
            values = dict(minus_half=-0.5, half=0.5, minus_one=-1.0, zero=0.0, one=1.0, eps=EPS, dim=float(DIM), seq=float(SEQ),
                          inv_e=float(np.exp(-1.0)), r_map=R_MAP, strength=0.1, rest=1.0 - 0.1 * 0.5)
            const = {n: sb(n, [P, ROWT]) for n in values}
            bias16 = sb("bias16", [16, 3, 4, 8])
            running = sb("running", [P, EXPERTS])

            x_in, c_in, x_res = (sb(n, [P, ROWT, DIM]) for n in ("x_in", "c_in", "x_res"))
            base = x_res
            q_rows = x_in
            q_fold, c_fold = (sb(n, [P, 2, 2, DIM]) for n in ("q_fold", "c_fold"))
            q_spec, c_spec = (sb(n, [P, CB, 512]) for n in ("q_spec", "c_spec"))
            re_buf = [sb(f"re{i}", [P, DIM]) for i in (0, 1)]
            s1, s2 = ([sb(f"{n}_{i}", [P, 2, 4, P]) for i in (0, 1)] for n in ("s1", "s2"))
            tri32, ones32 = s2[0][:, 0, 0], s2[0][:, 0, 1]
            prod = sb("prod", [P, 4, 2, DIM])
            w_raw = prod[:].rearrange("p (w a) b n -> p w (a b) n", w=2)
            r_spec = sb("r_spec", [P, 2, 2, 4, P])
            real_row = sb("real_row", [1, 3, 2, DIM])
            real_in = sb("real_in", [16, 3, 2, 4, 8])
            real_t = sb("real_t", [16, 2, 4, 4, 8])
            real_u = sb("real_u", [16, 2, 4, 8])
            real_v = sb("real_v", [16, 2, 4, 8])
            real_p = sb("real_p", [16, 2, 4, 8])
            rows = sb("rows", [P, ROWT, ROW])
            x_tok = sb("x_tok", [P, ROWT, DIM])
            x_tok_t = [sb(f"x_tok_t{i}", [P, CB, P]) for i in (0, 1)]
            bn1, bn2 = sb("bn1", [P, ROWT, 6]), sb("bn2", [P, ROWT, 6])
            mv1, mv2 = sb("mv1", [P, ROWT, 2]), sb("mv2", [P, ROWT, 2])
            st = [sb(f"st{i}", [P, ROWT]) for i in range(10)]
            q_scale, q_bias = sb("q_scale", [P, ROWT]), sb("q_bias", [P, ROWT])
            tt = [sb(f"tt{i}", [P, ROWT]) for i in range(6)]
            logit, over, e_over, cand, picked = (sb(n, [P, ROWT, EXPERTS]) for n in ("logit", "over", "e_over", "cand", "picked"))
            onehot = sb("onehot", [P, ROWT, EXPERTS], bf16)
            top = sb("top", [P, ROWT])
            first = sb("first", [P, ROWT])
            denom = sb("denom", [P, ROWT])
            rank = sb("rank", [P, ROWT])
            far = sb("far", [P, ROWT])
            slot_f = sb("slot_f", [P, ROWT])
            slot_i = sb("slot_i", [P, ROWT], i32)

            pair = [pb(f"pair{i}", [P, 2, 512]) for i in (0, 1)]
            xt_ps = [pb(f"xt_ps{i}", [P, 512]) for i in (0, 1)]
            even_ps, odd_ps = pb("even_ps", [P, 512]), pb("odd_ps", [P, 512])

            SETUP_DMAS = 17
            ZEROED = len(values) + 4
            consts_in = sem("consts_in")
            zeroed = sem("zeroed")
            token_next = sem("token_next")
            setup_v = sem("setup_v")
            setup_mm = sem("setup_mm")
            scaled = sem("scaled")
            w_split, c_split = sem("w_split"), sem("c_split")
            slots_clear = sem("slots_clear")
            x_loaded, c_loaded, res_loaded = sem("x_loaded"), sem("c_loaded"), sem("res_loaded")
            real_left, real_back = sem("real_left"), sem("real_back")
            real_loaded, real_stored = sem("real_loaded"), sem("real_stored")
            base_stored, scattered = sem("base_stored"), sem("scattered")
            bn1_step = sem("bn1_step")
            stat1 = sem("stat1")
            q_ready = sem("q_ready")
            qf_ready, cf_ready = sem("qf_ready"), sem("cf_ready")
            f1_mm, f1_ev = sem("f1_mm"), sem("f1_ev")
            f2_mm, re_ready, conv = sem("f2_mm"), sem("re_ready"), sem("conv")
            ham = sem("ham")
            inv_mm, unfold = sem("inv_mm"), sem("unfold")
            bn2_step, stat2 = sem("bn2_step"), sem("stat2")
            tok_ready, base_ready = sem("tok_ready"), sem("base_ready")
            g_mm, g_ev, logit_mm = sem("g_mm"), sem("g_ev"), sem("logit_mm")
            route, exp_done, rank_mm = sem("route"), sem("exp_done"), sem("rank_mm")
            real_step = sem("real_step")

            BN, STAT1, STAT2, CONV, HAM, UNF, ROUTE, REAL = 8, 45, 11, 24, 54, 8, 16, 27
            HAM_E, HAM_O = 27, 54
            PROJ = [(0, 0), (0, 1), (0, 2), (1, 0), (1, 1), (1, 2)]

            def seq(v, b):
                return v[bass.ds(b, 1), :, :].rearrange("a (t p) n -> p (a t) n", p=P)

            with nc.Block() as block:

                @block.sync
                def _(sp):
                    def load_x(b):
                        wait(sp, qf_ready, b * 2)
                        sp.dma_start(x_in[:], seq(x, b)).then_inc(x_loaded, 16)

                    def load_c(b):
                        wait(sp, cf_ready, b * 2)
                        sp.dma_start(c_in[:], seq(ctx_in, b)).then_inc(c_loaded, 16)

                    def batch(b, back, ahead):
                        if not back:
                            load_res(b)
                        if ahead:
                            load_c(b + 2)
                        sp.wait_ge(re_ready, b * 6 + 3)
                        sp.dma_start(bins_in, real_row[:].rearrange("o a s n -> o (a s n)")).then_inc(real_left, 16)
                        sp.wait_ge(real_left, b * 16 + 16)
                        sp.dma_start(real_in[:].rearrange("q a s c e -> q (a s c) e"),
                                     bins_in.rearrange("o (k q e) -> q (o k) e", q=16, e=8)).then_inc(real_loaded, 16)
                        if ahead:
                            load_x(b + 2)
                        sp.wait_ge(real_step, b * REAL + REAL)
                        sp.dma_start(bins_out.rearrange("o (k q e) -> q (o k) e", q=16, e=8),
                                     real_p[:].rearrange("q s c e -> q (s c) e")).then_inc(real_back, 16)
                        sp.wait_ge(ham, b * HAM + HAM_E)
                        sp.wait_ge(real_back, b * 16 + 16)
                        sp.dma_start(r_spec[0:1, 0].rearrange("o s c e -> o (s c e)"), bins_out).then_inc(real_stored, 16)
                        if back:
                            store(b - 1)
                            load_res(b)

                    def load_res(b):
                        wait(sp, base_stored, b * 16)
                        sp.dma_start(x_res[:], seq(x, b)).then_inc(res_loaded, 16)

                    def store(b):
                        sp.wait_ge(base_ready, b * 4 + 4)
                        sp.dma_start(seq(out, b), base[:]).then_inc(base_stored, 16)

                    for dst, src in ((fwd[:].rearrange("p a b c -> p (a b c)"), c_fwd),
                                     (inv[:].rearrange("p a b c -> p (a b c)"), c_inv),
                                     (pos[:], c_pos), (signs[:].rearrange("p a b c -> p (a b c)"), c_sgn),
                                     (tri32, c_tri), (eye[:], c_eye), (token[:], c_tok),
                                     (iota8[:].rearrange("p t e -> p (t e)"), c_exp),
                                     (w_q[:], wq.rearrange("(k p) n -> p k n", p=P)),
                                     (w_raw[:, 0], wk.rearrange("(k p) n -> p k n", p=P)),
                                     (w_raw[:, 1], wv.rearrange("(k p) n -> p k n", p=P)),
                                     (gate_t[:], gate.rearrange("(k p) e -> p k e", p=P)),
                                     (gam[:], gamma),
                                     (bet[:], beta)):
                        sp.dma_start(dst, src).then_inc(consts_in, 16)
                    for a, v in enumerate((bq, bk, bv)):
                        sp.dma_start(bias16[:, a], v.rearrange("(c q e) -> q c e", c=4, q=16)).then_inc(consts_in, 16)
                    load_x(0)
                    load_c(0)
                    sp.wait_ge(setup_v, 1)
                    for t in range(ROWT):
                        sp.dma_start(slots.rearrange("(s t p) n -> p s t n", t=ROWT, p=P)[:, :, t, :],
                                     rows[:, 0:1, :].broadcast_to([P, SLOTS // (ROWT * P), ROW])
                                     ).then_inc(slots_clear, 16)
                    load_x(1)
                    load_c(1)
                    batch(0, False, True)
                    with sp.Fori(1, BATCH - 2) as b:
                        batch(b, True, True)
                    batch(BATCH - 2, True, False)
                    batch(BATCH - 1, True, False)
                    store(BATCH - 1)
                    sp.wait_ge(base_stored, 16 * BATCH)
                    sp.wait_ge(scattered, 64 * BATCH)

                @block.tensor
                def _(pe):
                    pe.wait_ge(consts_in, 16 * SETUP_DMAS)

                    def dft(b, folded, ready, first_unit):
                        pe.wait_ge(ready, b * 2 + 2)
                        for u in range(4):
                            if u < 2:
                                wait(pe, f1_ev, b * 8 + first_unit)
                            else:
                                pe.wait_ge(f1_ev, b * 8 + first_unit + u - 1)
                            ps = xt_ps[u % 2]
                            for eo in range(2):
                                for t in range(2):
                                    last = nc.tensor.matmul(ps[:, eo * 256:eo * 256 + 256],
                                                            folded[:, eo, t, u * P:(u + 1) * P], fwd[:, t, eo, :],
                                                            start=(t == 0), stop=(t == 1))
                            last.then_inc(f1_mm, 1)

                    def project(b, k, slots=(0, 1)):
                        tile, which = PROJ[k]
                        wh, wl = ((w_kh, w_kl), (w_vh, w_vl))[which - 1]
                        terms = ((q_spec, w_q),) if which == 0 else ((c_high, wh), (c_low, wh), (c_high, wl))
                        if k == 0 and 0 in slots:
                            pe.wait_ge(f1_ev, b * 8 + 8)
                        if k == 1:
                            pe.wait_ge(c_split, b * 2 + 2)
                        if 0 in slots:
                            wait(pe, conv, b * CONV + (k - 1) * 4)
                        for s in slots:
                            for c in range(CB):
                                for n, (spec, w) in enumerate(terms):
                                    last = nc.tensor.matmul(pair[k % 2][:, s, :],
                                                            spec[:, c, tile * 256 + s * P:tile * 256 + (s + 1) * P],
                                                            w[:, c, :], start=(c == 0 and n == 0),
                                                            stop=(c == CB - 1 and n == len(terms) - 1))
                        if 1 in slots:
                            last.then_inc(f2_mm, 1)

                    def inverse(b, t):
                        if t == 0:
                            pe.wait_ge(ham, b * HAM + HAM_O)
                            pe.wait_ge(real_stored, b * 16 + 16)
                            wait(pe, route, b * ROUTE)
                        for tile, ps in ((0, even_ps), (1, odd_ps)):
                            if t:
                                pe.wait_ge(unfold, b * UNF + (2 if tile == 0 else 4))
                            for s in range(2):
                                last = nc.tensor.matmul(ps[:], inv[:, tile, s, t * P:(t + 1) * P],
                                                        r_spec[:, tile, s].rearrange("p c e -> p (c e)"),
                                                        start=(s == 0), stop=(s == 1))
                            last.then_inc(inv_mm, 1)

                    def turn(b, t, f1_done):
                        pe.wait_ge(tok_ready, b * 4 + t + 1)
                        if t < 2:
                            pe.wait_ge(f1_ev, f1_done)
                        else:
                            pe.wait_ge(g_ev, b * 4 + t - 1)
                        for c in range(CB):
                            last = nc.tensor.transpose(xt_ps[t % 2][:, c * P:(c + 1) * P],
                                                       x_tok[:, t, c * P:(c + 1) * P], eye[:])
                        last.then_inc(g_mm, 1)

                    def router(b, f1_done, ahead):
                        turn(b, 0, f1_done)
                        turn(b, 1, f1_done)
                        if ahead:
                            project(b + 2, 0, (0,))
                        for t in range(2):
                            logits(b, t)
                            turn(b, t + 2, f1_done)
                        if ahead:
                            project(b + 2, 0, (1,))
                        logits(b, 2)
                        logits(b, 3)

                    def logits(b, t):
                        pe.wait_ge(g_ev, b * 4 + t + 1)
                        if t == 0:
                            pe.wait_ge(unfold, b * UNF + UNF)
                        for c in range(CB):
                            last = nc.tensor.matmul(even_ps[:, t * EXPERTS:(t + 1) * EXPERTS], x_tok_t[t % 2][:, c, :],
                                                    gate_g[:, c, :], start=(c == 0), stop=(c == CB - 1))
                        last.then_inc(logit_mm, 1)

                    def ranks(b):
                        pe.wait_ge(route, b * ROUTE + 6)
                        for t in range(ROWT + 1):
                            o = odd_ps[:, t * EXPERTS:(t + 1) * EXPERTS]
                            for u in range(t):
                                last = nc.tensor.matmul(o, ones[:], onehot[:, u, :], start=(u == 0),
                                                        stop=(t == ROWT and u == t - 1))
                            if t < ROWT:
                                nc.tensor.matmul(o, tri[:], onehot[:, t, :], start=(t == 0), stop=True)
                        last.then_inc(rank_mm, 1)

                    pe.wait_ge(setup_v, 11)
                    for c in range(CB):
                        last = nc.tensor.matmul(even_ps[:, 0:EXPERTS], ones32, gate_b[:, c, :], start=(c == 0), stop=(c == CB - 1))
                    last.then_inc(setup_mm, 1)
                    pe.wait_ge(setup_v, 12)
                    pe.wait_ge(w_split, 2)
                    dft(0, c_fold, cf_ready, 0)
                    dft(0, q_fold, qf_ready, 4)
                    project(0, 0)
                    project(0, 1)

                    def batch(b, back, ahead):
                        project(b, 2)
                        if back:
                            inverse(b - 1, 0)
                        project(b, 3)
                        if back:
                            inverse(b - 1, 1)
                        if ahead:
                            dft(b + 1, c_fold, cf_ready, 0)
                        project(b, 4)
                        if ahead:
                            dft(b + 1, q_fold, qf_ready, 4)
                        project(b, 5)
                        if back:
                            router(b - 1, b * 8 + (16 if ahead else 8), ahead)
                        elif ahead:
                            project(b + 1, 0)
                        if ahead:
                            project(b + 1, 1)
                        if back:
                            ranks(b - 1)

                    batch(0, False, True)
                    with pe.Fori(1, BATCH - 1) as b:
                        batch(b, True, True)
                    batch(BATCH - 1, True, False)
                    inverse(BATCH - 1, 0)
                    inverse(BATCH - 1, 1)
                    router(BATCH - 1, BATCH * 8, False)
                    ranks(BATCH - 1)

                @block.scalar
                def _(act):
                    act.wait_ge(consts_in, 16 * SETUP_DMAS)
                    for n in range(2):
                        nc.scalar.activation(w_raw[:, n], w_raw[:, n], ACT.Copy, scale=memory_scale()).then_inc(scaled, 1)
                    for n, high in enumerate((w_kh, w_vh)):
                        act.wait_ge(scaled, n + 1)
                        nc.scalar.activation(high[:], w_raw[:, n], ACT.Copy).then_inc(scaled, 1)

                    def q_of(b):
                        act.wait_ge(stat1, b * STAT1 + STAT1)
                        for t in range(ROWT):
                            nc.scalar.activation(q_rows[:, t, :], x_in[:, t, :], ACT.Identity, bias=q_bias[:, t:t + 1],
                                                 scale=q_scale[:, t:t + 1]).then_inc(q_ready, 1)

                    def spectra(b, spec, first_unit, free):
                        for u in range(4):
                            act.wait_ge(f1_mm, b * 8 + first_unit + u + 1)
                            if u == 0:
                                wait(act, *free)
                            nc.scalar.activation(spec[:, u, :], xt_ps[u % 2][:], ACT.Copy).then_inc(f1_ev, 1)

                    def context_high(b):
                        act.wait_ge(f1_ev, b * 8 + 4)
                        wait(act, f2_mm, b * 6)
                        nc.scalar.activation(c_high[:], c_spec[:], ACT.Copy).then_inc(c_split, 1)

                    def real_parts(b, k):
                        tile, which = PROJ[k]
                        act.wait_ge(f2_mm, b * 6 + k + 1)
                        if k == 0:
                            wait(act, real_loaded, b * 16)
                        if tile == 0:
                            nc.scalar.activation(real_row[0:1, which], pair[k % 2][0:1, :, :], ACT.Copy)
                        wait(act, conv, b * CONV + (k - 1) * 4)
                        nc.scalar.activation(re_buf[k % 2][:], pair[k % 2][:, 0, :], ACT.Copy).then_inc(re_ready, 1)

                    def tokens(b):
                        act.wait_ge(stat2, b * STAT2 + STAT2)
                        wait(act, logit_mm, b * 4)
                        for t in range(ROWT):
                            nc.scalar.activation(x_tok[:, t, :], rows[:, t, 0:DIM], ACT.Identity,
                                                 bias=rows[:, t, DIM + 3:DIM + 4],
                                                 scale=rows[:, t, DIM + 2:DIM + 3]).then_inc(tok_ready, 1)

                    def base_of(b):
                        for t in range(ROWT):
                            nc.scalar.activation(base[:, t, :], rows[:, t, 0:DIM], ACT.Identity,
                                                 bias=rows[:, t, DIM + 5:DIM + 6],
                                                 scale=rows[:, t, DIM + 4:DIM + 5]).then_inc(base_ready, 1)

                    def token_blocks(b):
                        for t in range(ROWT):
                            act.wait_ge(g_mm, b * 4 + t + 1)
                            if t < 2:
                                wait(act, logit_mm, b * 4)
                            else:
                                act.wait_ge(logit_mm, b * 4 + t - 1)
                            nc.scalar.activation(x_tok_t[t % 2][:].rearrange("p c e -> p (c e)"), xt_ps[t % 2][:],
                                                 ACT.Copy).then_inc(g_ev, 1)

                    def exps(b):
                        act.wait_ge(route, b * ROUTE + 3)
                        nc.scalar.activation(e_over[:], over[:], ACT.Exp).then_inc(exp_done, 1)

                    def spectra_c(b):
                        spectra(b, c_spec, 0, (c_split, b * 2))

                    def spectra_q(b):
                        spectra(b, q_spec, 4, (f2_mm, b * 6 - 2))

                    q_of(0)
                    spectra_c(0)
                    spectra_q(0)
                    context_high(0)
                    real_parts(0, 0)

                    def batch(b, back, ahead):
                        real_parts(b, 1)
                        if ahead:
                            q_of(b + 1)
                        real_parts(b, 2)
                        real_parts(b, 3)
                        if ahead:
                            spectra_c(b + 1)
                        real_parts(b, 4)
                        if ahead:
                            spectra_q(b + 1)
                        if back:
                            tokens(b - 1)
                        real_parts(b, 5)
                        if back:
                            token_blocks(b - 1)
                        if ahead:
                            context_high(b + 1)
                        if back:
                            base_of(b - 1)
                        if ahead:
                            real_parts(b + 1, 0)
                        if back:
                            exps(b - 1)

                    batch(0, False, True)
                    with act.Fori(1, BATCH - 1) as b:
                        batch(b, True, True)
                    batch(BATCH - 1, True, False)
                    tokens(BATCH - 1)
                    token_blocks(BATCH - 1)
                    base_of(BATCH - 1)
                    exps(BATCH - 1)

                @block.gpsimd
                def _(pool):
                    s1c = Chain(pool, stat1, STAT1)
                    s2c = Chain(pool, stat2, STAT2)
                    rc = Chain(pool, real_step, REAL)
                    ts, tv = nc.gpsimd.tensor_scalar, nc.gpsimd.tensor_tensor

                    k = {n: t[:] for n, t in const.items()}
                    for n, v in values.items():
                        nc.gpsimd.memset(k[n], v).then_inc(zeroed, 1)
                    for dst, v in ((ones32, 1.0), (running[:], 0.0), (rows[:], 0.0)):
                        nc.gpsimd.memset(dst, v).then_inc(zeroed, 1)
                    pool.wait_ge(zeroed, ZEROED - 1)
                    pool.wait_ge(consts_in, 16 * SETUP_DMAS)
                    ts(bias16[:], bias16[:], float(SEQ), 0.0, ALU.mult, ALU.add).then_inc(zeroed, 1)
                    pool.wait_ge(zeroed, ZEROED)

                    def stats1(b):
                        pool.wait_ge(bn1_step, b * BN + BN)
                        wait(pool, q_ready, b * 4)
                        c = s1c
                        c.begin(b)
                        mean, var = mv1[:, :, 0], mv1[:, :, 1]
                        a, rstd, r2, n2, norm, e, s, u, v, rs = (z[:] for z in st)
                        c.step(tv(a, var, k["eps"], ALU.add)); c.wait()
                        c.step(tv(rstd, a, k["minus_half"], ALU.pow)); c.wait()
                        c.step(tv(r2, rstd, rstd, ALU.mult)); c.wait()
                        c.step(tv(n2, var, r2, ALU.mult)); c.wait()
                        c.step(tv(n2, n2, k["dim"], ALU.mult)); c.wait()
                        c.step(tv(norm, n2, k["half"], ALU.pow)); c.wait()
                        c.step(tv(e, k["inv_e"], norm, ALU.pow)); c.wait()
                        c.step(tv(e, e, k["one"], ALU.add)); c.wait()
                        c.step(tv(s, e, k["minus_one"], ALU.pow)); c.wait()
                        for _ in range(MAP_STEPS):
                            c.step(tv(u, s, k["r_map"], ALU.mult))
                            c.step(tv(v, k["one"], s, ALU.subtract)); c.wait()
                            c.step(tv(s, u, v, ALU.mult)); c.wait()
                        c.step(tv(s, s, k["strength"], ALU.mult)); c.wait()
                        c.step(tv(s, s, k["rest"], ALU.add)); c.wait()
                        c.step(tv(rs, s, pos[:], ALU.mult)); c.wait()
                        c.step(tv(q_scale[:], rs, rstd, ALU.mult))
                        c.step(tv(u, k["zero"], mean, ALU.subtract)); c.wait()
                        c.step(tv(q_bias[:], u, q_scale[:], ALU.mult))
                        c.end()

                    def stats2(b):
                        pool.wait_ge(bn2_step, b * BN + BN)
                        c = s2c
                        c.begin(b)
                        mean, var = mv2[:, :, 0], mv2[:, :, 1]
                        a, rstd, r2, v2, n2, neg = (z[:] for z in tt)
                        meta = rows[:, :, DIM:DIM + META]
                        a2, nb2, s1_, nb = (meta[:, :, k] for k in (2, 3, 4, 5))
                        c.step(tv(a, var, k["eps"], ALU.add))
                        c.step(tv(neg, k["zero"], mean, ALU.subtract)); c.wait()
                        c.step(tv(rstd, a, k["minus_half"], ALU.pow)); c.wait()
                        c.step(tv(r2, rstd, rstd, ALU.mult)); c.wait()
                        c.step(tv(v2, var, r2, ALU.mult)); c.wait()
                        c.step(tv(v2, v2, k["eps"], ALU.add)); c.wait()
                        c.step(tv(n2, v2, k["minus_half"], ALU.pow)); c.wait()
                        c.step(tv(a2, rstd, n2, ALU.mult))
                        c.step(tv(s1_, rstd, k["one"], ALU.add)); c.wait()
                        c.step(tv(nb, neg, rstd, ALU.mult))
                        c.step(tv(nb2, neg, a2, ALU.mult))
                        c.end()

                    def fold(b, src, dst, ready, source, users):
                        pool.wait_ge(*source)
                        wait(pool, f1_mm, users)
                        for eo, op in ((0, ALU.add), (1, ALU.subtract)):
                            tv(dst[:, eo], src[:, 0:2], src[:, 2:4], op).then_inc(ready, 1)

                    def real_bins(b):
                        pool.wait_ge(real_loaded, b * 16 + 16)
                        wait(pool, real_stored, b * 16)
                        c = rc
                        c.begin(b)
                        c.step(tv(real_in[:, :, 0], real_in[:, :, 0], bias16[:], ALU.add)); c.wait()
                        left = real_in[:, 0]
                        for which, to in ((1, real_u), (2, real_p)):
                            right = real_in[:, which]
                            for s in range(2):
                                for d in range(4):
                                    a_ = left[:, s, d:d + 1, :]
                                    if d == 0:
                                        o, i0, i1 = real_t[:, s, 0], a_.broadcast_to([16, 4, 8]), right[:, s]
                                    else:
                                        o = real_t[:, s, d].rearrange("q (h l) e -> q h l e", h=2)
                                        i0 = bass.AP(a_.tensor, a_.offset, [list(a_.ap[0]), [0, 2], [0, 2], [1, 8]])
                                        r0 = right[:, s, d:d + 1, :]
                                        i1 = bass.AP(r0.tensor, r0.offset, [list(r0.ap[0]), [16 if d == 1 else -16, 2],
                                                                            [8 if d == 2 else -8, 2], [1, 8]])
                                    c.step(tv(o, i0, i1, ALU.mult))
                            c.wait()
                            for s in range(2):
                                c.step(tv(real_t[:, s, 1:4], real_t[:, s, 1:4], signs[:], ALU.mult))
                            c.wait()
                            c.step(tv(real_v[:], real_t[:, :, 0], real_t[:, :, 1], ALU.add))
                            c.step(tv(real_t[:, :, 2], real_t[:, :, 2], real_t[:, :, 3], ALU.add)); c.wait()
                            c.step(tv(to[:], real_v[:], real_t[:, :, 2], ALU.add))
                            if which == 1:
                                c.wait()
                            left = real_u[:]
                        c.end()

                    def scatter(b):
                        pool.wait_ge(route, b * ROUTE + ROUTE)
                        pool.wait_ge(base_ready, b * 4 + 4)
                        tv(token[:], token[:], k["seq"], ALU.add).then_inc(token_next, 1)
                        for t in range(ROWT):
                            nc.gpsimd.indirect_dma_start(
                                slots, bass.IndirectOffsetOnAxis(ap=slot_i[:, t:t + 1].bitcast(u32), axis=0),
                                rows[:, t, :], None, bounds_check=SLOTS - 1, oob_is_err=False).then_inc(scattered, 16)

                    def folds_q(b):
                        fold(b, q_rows, q_fold, qf_ready, (q_ready, b * 4 + 4), b * 8)

                    def folds_c(b):
                        fold(b, c_in, c_fold, cf_ready, (c_loaded, b * 16 + 16), b * 8 - 4)

                    def batch(b, product, router, ahead):
                        folds_q(b)
                        if product:
                            real_bins(b - 1)
                        if router:
                            stats2(b - 2)
                        if ahead:
                            folds_c(b + 1)
                            stats1(b + 1)
                        if router:
                            scatter(b - 2)

                    folds_c(0)
                    stats1(0)
                    batch(0, False, False, True)
                    batch(1, True, False, True)
                    pool.wait_ge(slots_clear, 64)
                    with pool.Fori(2, BATCH - 1) as b:
                        batch(b, True, True, True)
                    batch(BATCH - 1, True, True, False)
                    real_bins(BATCH - 1)
                    for b in (BATCH - 2, BATCH - 1):
                        stats2(b)
                        scatter(b)

                @block.vector
                def _(dve):
                    v = nc.vector
                    setup = Chain(dve, setup_v, 12)
                    bn1c, bn2c = Chain(dve, bn1_step, BN), Chain(dve, bn2_step, BN)
                    hc, uc, ro = Chain(dve, ham, HAM), Chain(dve, unfold, UNF), Chain(dve, route, ROUTE)

                    dve.wait_ge(consts_in, 16 * SETUP_DMAS)
                    dve.wait_ge(zeroed, ZEROED - 1)
                    setup.begin(0)
                    setup.step(v.tensor_scalar(rows[:, 0, DIM:DIM + 1].bitcast(i32), token[:, 0:1], 0.0,
                                               float(BATCH * SEQ), ALU.mult, ALU.add))
                    setup.step(v.tensor_copy(tri[:], tri32))
                    setup.step(v.tensor_copy(ones[:], ones32))
                    for c in range(CB):
                        setup.step(v.tensor_scalar(gate_b[:, c, :], gate_t[:, c, :], bet[:, c:c + 1], None, ALU.mult))
                        setup.step(v.tensor_scalar(gate_g[:, c, :], gate_t[:, c, :], gam[:, c:c + 1], None, ALU.mult))
                    dve.wait_ge(scaled, 4)
                    for n, (high, low) in enumerate(((w_kh, w_kl), (w_vh, w_vl))):
                        v.tensor_tensor(low[:], w_raw[:, n], high[:].bitcast(f32), ALU.subtract).then_inc(w_split, 1)
                    dve.wait_ge(w_split, 2)
                    dve.wait_ge(setup_mm, 1)
                    setup.step(v.tensor_copy(gate_c[:], even_ps[:, 0:EXPERTS]))
                    setup.end()
                    setup.wait()

                    def context_low(b):
                        dve.wait_ge(c_split, b * 2 + 1)
                        v.tensor_tensor(c_low[:], c_spec[:], c_high[:].bitcast(f32), ALU.subtract).then_inc(c_split, 1)

                    def stats(b, c, src, bn, ready):
                        c.begin(b)
                        dve.wait_ge(*ready)
                        for t in range(ROWT):
                            c.step(v.bn_stats(bn[:, t, :], src[:, t, 0:DIM]))

                    def mean_var(c, bn, mv):
                        for t in range(ROWT):
                            c.step(v.bn_aggr(mv[:, t, :], bn[:, t, :]))
                        c.end()

                    def stats_x(b):
                        wait(dve, stat1, b * STAT1)
                        stats(b, bn1c, x_in, bn1, (x_loaded, b * 16 + 16))

                    def convert(b, k):
                        dve.wait_ge(re_ready, b * 6 + k + 1)
                        tile, which = PROJ[k]
                        dst = s1[tile] if which == 0 else s2[which - 1]
                        re = re_buf[k % 2][:].rearrange("p (h l e) -> p h l e", h=2, l=2)
                        im = pair[k % 2][:, 1, :].rearrange("p (h l e) -> p h l e", h=2, l=2)
                        a_b, d_c = dst[:, :, 0:2, :], down(dst, 3)
                        wy_re, xz_re, wy_im, xz_im = re[:, :, 0], re[:, :, 1], im[:, :, 0], im[:, :, 1]
                        v.tensor_tensor(a_b[:, 0], wy_re, xz_im, ALU.subtract).then_inc(conv, 1)
                        v.tensor_tensor(a_b[:, 1], xz_re, wy_im, ALU.add).then_inc(conv, 1)
                        v.tensor_tensor(d_c[0], wy_re, xz_im, ALU.add).then_inc(conv, 1)
                        v.tensor_tensor(d_c[1], wy_im, xz_re, ALU.subtract).then_inc(conv, 1)

                    def down(s, start):
                        out_ = []
                        for slot in range(2):
                            r = s[:, slot, start:start + 1, :]
                            out_.append(bass.AP(r.tensor, r.offset, [list(r.ap[0]), [-P, 2], [1, P]]))
                        return out_

                    def view(s, slot, first_, steps):
                        r = s[:, slot, first_:first_ + 1, :]
                        return bass.AP(r.tensor, r.offset, [list(r.ap[0]), [steps[0] * P, 2], [steps[1] * P, 2], [1, P]])

                    def hamilton(b, k, between=None):
                        l, r = s1[PROJ[k][0]], s2[PROJ[k][1] - 1]
                        dve.wait_ge(conv, b * CONV + (k + 1) * 4)
                        wait(dve, ham, hc.base + hc.n)
                        n0 = hc.n
                        for m, (i, j) in enumerate(((0, 0), (1, 1), (0, 1), (1, 0))):
                            o = prod[:, m].rearrange("p w (h l e) -> p w h l e", h=2, l=2)
                            hc.step(v.tensor_tensor(o[:, 0], view(l, i, 0, (3, 0)), view(r, j, 0, (2, 1)), ALU.mult))
                            hc.step(v.tensor_tensor(o[:, 1], view(l, i, 1, (1, 0)), view(r, j, 2, (-2, 1)), ALU.mult))
                            if between and m == 3:
                                between()
                        hc.wait(n0 + 4)
                        hc.step(v.tensor_tensor(prod[:, 0], prod[:, 0], prod[:, 1], ALU.subtract))
                        hc.wait(n0 + 8)
                        hc.step(v.tensor_tensor(prod[:, 2], prod[:, 2], prod[:, 3], ALU.add))
                        hc.wait()
                        parts = prod[:].rearrange("p (s z) w (c e) -> p s z w c e", s=2, c=4)[:, :, 0]
                        hc.step(v.tensor_tensor(l[:, :, 1:3, :], parts[:, :, 0, 1:3], parts[:, :, 1, 1:3], ALU.add))
                        hc.step(v.tensor_tensor(l[:, :, 0:4:3, :], parts[:, :, 0, 0:4:3], parts[:, :, 1, 0:4:3], ALU.subtract))

                    def back_to_parts(b, tile, then=None):
                        hc.wait()
                        r = r_spec[:, tile].rearrange("p s (h l) e -> p s h l e", h=2)
                        s = s1[tile]
                        d_c = down(s, 3)
                        both = bass.AP(d_c[0].tensor, d_c[0].offset, [list(d_c[0].ap[0]), [4 * P, 2], [-P, 2], [1, P]])
                        hc.step(v.tensor_tensor(r[:, :, :, 0], s[:, :, 0:2, :], both, ALU.add))
                        if then:
                            then()
                        hc.step(v.tensor_tensor(r[:, 0, :, 1], s[:, 1, 0:2, :], d_c[1], ALU.subtract))
                        hc.step(v.tensor_tensor(r[:, 1, :, 1], d_c[0], s[:, 0, 0:2, :], ALU.subtract))

                    def add_attended(b, t):
                        if t == 0:
                            uc.begin(b)
                            dve.wait_ge(res_loaded, b * 16 + 16)
                            wait(dve, scattered, b * 64)
                            wait(dve, base_ready, b * 4)
                        lo, hi = rows[:, t, 0:DIM], rows[:, t + 2, 0:DIM]
                        dve.wait_ge(inv_mm, b * 4 + 2 * t + 1)
                        uc.step(v.tensor_tensor(lo, x_res[:, t, :], even_ps[:], ALU.add))
                        n = uc.step(v.tensor_tensor(hi, x_res[:, t + 2, :], even_ps[:], ALU.add))
                        dve.wait_ge(inv_mm, b * 4 + 2 * t + 2)
                        uc.wait(n)
                        uc.step(v.tensor_tensor(lo, lo, odd_ps[:], ALU.add))
                        uc.step(v.tensor_tensor(hi, hi, odd_ps[:], ALU.subtract))
                        if t == 1:
                            uc.end()

                    def stats_x2(b):
                        wait(dve, stat2, b * STAT2)
                        stats(b, bn2c, rows, bn2, (unfold, b * UNF + UNF))

                    def choose(b):
                        dve.wait_ge(logit_mm, b * 4 + 4)
                        wait(dve, rank_mm, b)
                        ro.begin(b)
                        lg = even_ps[:, 0:ROWT * EXPERTS].rearrange("p (t e) -> p t e", t=ROWT)
                        ro.step(v.tensor_tensor(logit[:], lg, bass.AP(gate_c[:].tensor, gate_c[:].offset, [list(gate_c[:].ap[0]), [0, ROWT], [1, EXPERTS]]), ALU.add)); ro.wait()
                        ro.step(v.tensor_reduce(top[:], logit[:], AX.X, ALU.max)); ro.wait()
                        ro.step(v.tensor_tensor(over[:], logit[:], top[:].unsqueeze(2).broadcast_to([P, ROWT, EXPERTS]), ALU.subtract)); ro.wait()
                        ro.step(v.scalar_tensor_tensor(cand[:], over[:], 0.0, iota8[:], ALU.is_ge, ALU.mult)); ro.wait()
                        ro.step(v.tensor_reduce(first[:], cand[:], AX.X, ALU.min)); ro.wait()
                        ro.step(v.tensor_tensor(onehot[:], iota8[:], first[:].unsqueeze(2).broadcast_to([P, ROWT, EXPERTS]), ALU.is_equal))

                    def place(b):
                        dve.wait_ge(exp_done, b + 1)
                        ro.step(v.tensor_reduce(denom[:], e_over[:], AX.X, ALU.add)); ro.wait()
                        ro.step(v.reciprocal(rows[:, :, DIM + 1], denom[:]))
                        wait(dve, token_next, b)
                        ro.step(v.tensor_scalar(rows[:, :, DIM].bitcast(i32), token[:], 1.0, None, ALU.mult))
                        dve.wait_ge(rank_mm, b + 1)
                        rk = odd_ps[:, 0:ROWT * EXPERTS].rearrange("p (t e) -> p t e", t=ROWT)
                        ro.step(v.tensor_tensor(cand[:], rk, bass.AP(running[:].tensor, running[:].offset, [list(running[:].ap[0]), [0, ROWT], [1, EXPERTS]]), ALU.add)); ro.wait()
                        ro.step(v.tensor_tensor(running[:], running[:], odd_ps[:, ROWT * EXPERTS:(ROWT + 1) * EXPERTS], ALU.add))
                        ro.step(v.tensor_tensor(picked[:], cand[:], onehot[:], ALU.mult)); ro.wait()
                        ro.step(v.tensor_reduce(rank[:], picked[:], AX.X, ALU.add)); ro.wait()
                        ro.step(v.tensor_scalar(far[:], rank[:], float(CAPACITY), float(SKIPPED), ALU.is_ge, ALU.mult))
                        ro.step(v.scalar_tensor_tensor(slot_f[:], first[:], float(CAPACITY), rank[:], ALU.mult, ALU.add)); ro.wait()
                        ro.step(v.scalar_tensor_tensor(slot_i[:], slot_f[:], float(CAPACITY * EXPERTS), far[:], ALU.add, ALU.add))
                        ro.wait()
                        ro.end()

                    stats_x(0)
                    bn1c.wait()
                    mean_var(bn1c, bn1, mv1)
                    stats_x(1)
                    bn1c.wait()
                    mean_var(bn1c, bn1, mv1)
                    context_low(0)
                    convert(0, 0)
                    convert(0, 1)

                    def batch(b, back, ahead, ahead2):
                        hc.begin(b)
                        hamilton(b, 1)
                        convert(b, 2)
                        if back:
                            add_attended(b - 1, 0)
                        hamilton(b, 2)
                        convert(b, 3)
                        if back:
                            add_attended(b - 1, 1)
                            stats_x2(b - 1)
                            bn2c.wait()
                        wait(dve, inv_mm, b * 4)
                        back_to_parts(b, 0, (lambda: mean_var(bn2c, bn2, mv2)) if back else None)
                        if ahead2:
                            stats_x(b + 2)
                            bn1c.wait()
                        convert(b, 4)
                        if ahead2:
                            mean_var(bn1c, bn1, mv1)
                        hamilton(b, 4)
                        convert(b, 5)
                        hamilton(b, 5, (lambda: context_low(b + 1)) if ahead else None)
                        if ahead:
                            convert(b + 1, 0)
                        back_to_parts(b, 1)
                        hc.end()
                        if back:
                            choose(b - 1)
                        if ahead:
                            convert(b + 1, 1)
                        if back:
                            place(b - 1)

                    batch(0, False, True, True)
                    dve.wait_ge(slots_clear, 64)
                    with dve.Fori(1, BATCH - 2) as b:
                        batch(b, True, True, True)
                    batch(BATCH - 2, True, True, False)
                    batch(BATCH - 1, True, False, False)
                    add_attended(BATCH - 1, 0)
                    add_attended(BATCH - 1, 1)
                    stats_x2(BATCH - 1)
                    bn2c.wait()
                    mean_var(bn2c, bn2, mv2)
                    choose(BATCH - 1)
                    place(BATCH - 1)

        experts(nc, outer, slots, gamma, beta, c_eye, wi, wo, out)


def experts(nc, outer, slots, gamma, beta, c_eye, wi, wo, out):
    f32, f32r, u32 = mybir.dt.float32, mybir.dt.float32r, mybir.dt.uint32
    ALU, ACT = mybir.AluOpType, mybir.ActivationFunctionType

    def sem(name):
        return outer.enter_context(nc.semaphore(name))

    with ExitStack() as mem:
        def sb(name, shape, dt=f32):
            return mem.enter_context(nc.sbuf_tensor(name, shape, dt))

        def pb(name, shape):
            return mem.enter_context(nc.psum_tensor(name, shape, f32))

        eye = sb("eye2", [P, P])
        gam, bet = sb("gam2", [P, CB]), sb("bet2", [P, CB])
        got = [sb(f"got{i}", [P, GT, ROW]) for i in (0, 1)]
        normed = sb("normed", [P, GT, DIM])
        tok32 = [sb(f"tok32_{i}", [P, GROUP]) for i in (0, 1)]
        tok_h = [sb(f"tok_h{i}", [P, CB, GROUP], f32r) for i in (0, 1)]
        tok_l = [sb(f"tok_l{i}", [P, CB, GROUP], f32r) for i in (0, 1)]
        w_raw = [sb(f"w_raw{i}", [P, 2, 1024]) for i in (0, 1)]
        w_h = [sb(f"w_h{i}", [P, 2, 1024], f32r) for i in range(RING)]
        w_l = [sb(f"w_l{i}", [P, 2, 1024], f32r) for i in range(RING)]
        act32 = [sb(f"act32_{i}", [P, GROUP]) for i in (0, 1)]
        act_h = [sb(f"act_h{i}", [P, GROUP], f32r) for i in range(4)]
        act_l = [sb(f"act_l{i}", [P, GROUP], f32r) for i in range(4)]
        res = sb("res", [P, GT, DIM])
        mixed = sb("mixed", [P, GT, DIM])
        tally, unit = sb("tally", [1, 1]), sb("unit", [1, 1])

        hid_ps = [pb(f"hid_ps{i}", [P, 512]) for i in (0, 1)]
        tr_ps = [pb(f"tr_ps{i}", [P, 512]) for i in (0, 1)]
        out_ps = [pb(f"out_ps{i}", [P, 512]) for i in range(GT)]

        const2_in = sem("const2_in")
        tallied, cleared = sem("tallied"), sem("cleared")
        got_in = [sem(f"got_in{i}") for i in (0, 1)]
        raw_in = [sem(f"raw_in{i}") for i in (0, 1)]
        wh_ready, wl_ready = sem("wh_ready"), sem("wl_ready")
        normed_ready = sem("normed_ready")
        tr_mm, th_ready, tv_ready, tl_ready = sem("tr_mm"), sem("th_ready"), sem("tv_ready"), sem("tl_ready")
        hid_mm, gelu, ah_ready, al_ready, out_mm = sem("hid_mm"), sem("gelu"), sem("ah_ready"), sem("al_ready"), sem("out_mm")
        res_ready, mixed_ready, mixed_stored = sem("res_ready"), sem("mixed_ready"), sem("mixed_stored")

        def group(e, g):
            return e * 2 + g

        with nc.Block() as block:
            @block.sync
            def _(sp):
                for dst, src in ((eye[:], c_eye), (gam[:], gamma),
                                 (bet[:], beta)):
                    sp.dma_start(dst, src).then_inc(const2_in, 16)

                def rows_of(e, g):
                    wait(sp, mixed_stored, e * 128 - 64 + 64 * g)
                    src = slots.rearrange("(a t p) n -> a p t n", t=GT, p=P)
                    sp.dma_start(got[g][:], src[bass.ds(e * 2 + g, 1)].rearrange("a p t n -> p (a t) n")).then_inc(got_in[g], 16)

                def weights(e, g, k):
                    n = group(e, g) * PAIRS + k
                    wait(sp, wl_ready, n - 1)
                    wait(sp, wh_ready, n - 1)
                    raw = w_raw[k % 2]
                    sp.dma_start(raw[:, 0].rearrange("p (c n) -> p c n", c=CB),
                                 wi[bass.ds(e, 1), :, k * 256:(k + 1) * 256].rearrange("a (c p) n -> p (a c) n", p=P)
                                 ).then_inc(raw_in[k % 2], 16)
                    sp.dma_start(raw[:, 1].rearrange("p (c n) -> p c n", c=2),
                                 wo[bass.ds(e, 1), k * 256:(k + 1) * 256, :].rearrange("a (c p) n -> p (a c) n", p=P)
                                 ).then_inc(raw_in[k % 2], 16)

                def expert(e, more):
                    for g in range(2):
                        for k in range(PAIRS):
                            weights(e, g, k)
                            if k == 1:
                                if g == 0:
                                    rows_of(e, 1)
                                elif more:
                                    rows_of(e + 1, 0)

                rows_of(0, 0)
                expert(0, True)
                with sp.Fori(1, EXPERTS - 1) as e:
                    expert(e, True)
                expert(EXPERTS - 1, False)

            @block.gpsimd
            def _(pool):
                nc.gpsimd.memset(tally[:], 0.0).then_inc(cleared, 1)
                nc.gpsimd.memset(unit[:], 1.0).then_inc(cleared, 1)
                pool.wait_ge(cleared, 2)

                def store(e, g):
                    wait(pool, tallied, group(e, g))
                    pool.wait_ge(mixed_ready, group(e, g) * GT + GT)
                    nc.gpsimd.tensor_tensor(tally[:], tally[:], unit[:], ALU.add).then_inc(tallied, 1)
                    for t in range(GT):
                        nc.gpsimd.indirect_dma_start(
                            out.rearrange("b s n -> (b s) n"),
                            bass.IndirectOffsetOnAxis(ap=got[g][:, t, DIM:DIM + 1].bitcast(u32), axis=0),
                            mixed[:, t, :], None, bounds_check=BATCH * SEQ - 1, oob_is_err=False).then_inc(mixed_stored, 16)

                store(0, 0)
                store(0, 1)
                with pool.Fori(1, EXPERTS) as e:
                    store(e, 0)
                    store(e, 1)
                pool.wait_ge(mixed_stored, 2 * EXPERTS * GT * 16)

            @block.tensor
            def _(pe):
                pe.wait_ge(const2_in, 48)

                def turn(e, g, c):
                    n = group(e, g)
                    pe.wait_ge(normed_ready, n * GT + GT)
                    wait(pe, tv_ready, n * CB + c - 1)
                    for t in range(GT):
                        last = nc.tensor.transpose(tr_ps[c % 2][:, t * P:(t + 1) * P], normed[:, t, c * P:(c + 1) * P], eye[:])
                    last.then_inc(tr_mm, 1)

                def up(e, g, i):
                    n = group(e, g)
                    if i == 0:
                        pe.wait_ge(tl_ready, n * CB + CB)
                    if i % 2 == 0:
                        pe.wait_ge(wh_ready, n * PAIRS + i // 2 + 1)
                        pe.wait_ge(wl_ready, n * PAIRS + i // 2 + 1)
                    wait(pe, gelu, n * ISTEPS + i - 1)
                    s = (i // 2) % RING
                    wh, wl = (w[s][:, 0].rearrange("p (c n) -> p c n", c=CB)[:, :, (i % 2) * P:(i % 2 + 1) * P] for w in (w_h, w_l))
                    for c in range(CB):
                        for a, b in ((wh, tok_h[g]), (wl, tok_h[g]), (wh, tok_l[g])):
                            first_, last_ = c == 0 and a is wh and b is tok_h[g], c == CB - 1 and b is tok_l[g]
                            last = nc.tensor.matmul(hid_ps[i % 2][:], a[:, c, :], b[:, c, :], start=first_, stop=last_)
                    last.then_inc(hid_mm, 1)

                def down(e, g, i):
                    n = group(e, g)
                    pe.wait_ge(ah_ready, n * ISTEPS + i + 1)
                    pe.wait_ge(al_ready, n * ISTEPS + i + 1)
                    s = (i // 2) % RING
                    oh, ol = (w[s][:, 1, (i % 2) * 512:(i % 2 + 1) * 512] for w in (w_h, w_l))
                    for t in range(GT):
                        if i == 0:
                            wait(pe, mixed_ready, (n - 1) * GT + t + 1)
                        ah, al = act_h[i % 4][:, t * P:(t + 1) * P], act_l[i % 4][:, t * P:(t + 1) * P]
                        nc.tensor.matmul(out_ps[t][:], ah, oh, start=(i == 0), stop=False)
                        nc.tensor.matmul(out_ps[t][:], al, oh, start=False, stop=False)
                        last = nc.tensor.matmul(out_ps[t][:], ah, ol, start=False, stop=(i == ISTEPS - 1))
                    last.then_inc(out_mm, 1)

                def expert(e, more):
                    for g in range(2):
                        for i in range(ISTEPS + 2):
                            if i < ISTEPS:
                                up(e, g, i)
                            if i >= 2:
                                down(e, g, i - 2)
                            if 8 <= i < 8 + CB and (g == 0 or more):
                                turn(e + g, 1 - g, i - 8)

                for c in range(CB):
                    turn(0, 0, c)
                expert(0, True)
                with pe.Fori(1, EXPERTS - 1) as e:
                    expert(e, True)
                expert(EXPERTS - 1, False)

            @block.scalar
            def _(act):
                act.wait_ge(const2_in, 48)

                def norm(e, g):
                    n = group(e, g)
                    act.wait_ge(got_in[g], e * 16 + 16)
                    wait(act, tr_mm, n * CB)
                    for t in range(GT):
                        nc.scalar.activation(normed[:, t, :], got[g][:, t, 0:DIM], ACT.Identity,
                                             bias=got[g][:, t, DIM + 3:DIM + 4],
                                             scale=got[g][:, t, DIM + 2:DIM + 3]).then_inc(normed_ready, 1)

                def affine(e, g, c):
                    n = group(e, g) * CB + c
                    act.wait_ge(tr_mm, n + 1)
                    wait(act, tl_ready, n - 1)
                    nc.scalar.activation(tok32[c % 2][:], tr_ps[c % 2][:], ACT.Identity, bias=bet[:, c:c + 1],
                                         scale=gam[:, c:c + 1]).then_inc(tv_ready, 1)

                def weight_high(e, g, k):
                    n = group(e, g) * PAIRS + k
                    if k % 2 == 0:
                        act.wait_ge(raw_in[0], (group(e, g) * (PAIRS // 2) + k // 2) * 32 + 32)
                    else:
                        act.wait_ge(raw_in[1], (group(e, g) * (PAIRS // 2) + k // 2) * 32 + 32)
                    wait(act, out_mm, (n - RING + 1) * 2)
                    nc.scalar.activation(w_h[k % RING][:], w_raw[k % 2][:], ACT.Copy).then_inc(wh_ready, 1)

                def gelu_of(e, g, i):
                    n = group(e, g) * ISTEPS + i
                    act.wait_ge(hid_mm, n + 1)
                    wait(act, al_ready, n - 1)
                    nc.scalar.activation(act32[i % 2][:], hid_ps[i % 2][:], ACT.Gelu).then_inc(gelu, 1)

                def residual(e, g):
                    n = group(e, g)
                    wait(act, mixed_ready, n * GT)
                    for t in range(GT):
                        nc.scalar.activation(res[:, t, :], got[g][:, t, 0:DIM], ACT.Identity,
                                             bias=got[g][:, t, DIM + 5:DIM + 6],
                                             scale=got[g][:, t, DIM + 4:DIM + 5]).then_inc(res_ready, 1)

                def expert(e, more):
                    for g in range(2):
                        for i in range(ISTEPS):
                            gelu_of(e, g, i)
                            if i % 2 == 1:
                                k = i // 2 + 2
                                if k < PAIRS:
                                    weight_high(e, g, k)
                                elif g == 0:
                                    weight_high(e, 1, k - PAIRS)
                                elif more:
                                    weight_high(e + 1, 0, k - PAIRS)
                            if i == 4:
                                residual(e, g)
                            if g == 0 or more:
                                if i == 6:
                                    norm(e + g, 1 - g)
                                if 8 <= i < 8 + CB:
                                    affine(e + g, 1 - g, i - 8)

                norm(0, 0)
                weight_high(0, 0, 0)
                weight_high(0, 0, 1)
                for c in range(CB):
                    affine(0, 0, c)
                expert(0, True)
                with act.Fori(1, EXPERTS - 1) as e:
                    expert(e, True)
                expert(EXPERTS - 1, False)

            @block.vector
            def _(dve):
                v = nc.vector
                dve.wait_ge(const2_in, 48)

                def token_split(e, g, c):
                    n = group(e, g) * CB + c
                    dve.wait_ge(tv_ready, n + 1)
                    v.tensor_copy(tok_h[g][:, c, :], tok32[c % 2][:]).then_inc(th_ready, 1)
                    dve.wait_ge(th_ready, n + 1)
                    v.tensor_tensor(tok_l[g][:, c, :], tok32[c % 2][:], tok_h[g][:, c, :].bitcast(f32),
                                    ALU.subtract).then_inc(tl_ready, 1)

                def weight_low(e, g, k):
                    n = group(e, g) * PAIRS + k
                    dve.wait_ge(wh_ready, n + 1)
                    v.tensor_tensor(w_l[k % RING][:], w_raw[k % 2][:], w_h[k % RING][:].bitcast(f32), ALU.subtract).then_inc(wl_ready, 1)

                def split(e, g, i):
                    n = group(e, g) * ISTEPS + i
                    dve.wait_ge(gelu, n + 1)
                    wait(dve, out_mm, n - 3)
                    v.tensor_copy(act_h[i % 4][:], act32[i % 2][:]).then_inc(ah_ready, 1)
                    dve.wait_ge(ah_ready, n + 1)
                    v.tensor_tensor(act_l[i % 4][:], act32[i % 2][:], act_h[i % 4][:].bitcast(f32),
                                    ALU.subtract).then_inc(al_ready, 1)

                def mix(e, g):
                    n = group(e, g)
                    dve.wait_ge(out_mm, n * ISTEPS + ISTEPS)
                    dve.wait_ge(res_ready, n * GT + GT)
                    wait(dve, mixed_stored, n * GT * 16)
                    for t in range(GT):
                        v.scalar_tensor_tensor(mixed[:, t, :], out_ps[t][:], got[g][:, t, DIM + 1:DIM + 2], res[:, t, :],
                                               ALU.mult, ALU.add).then_inc(mixed_ready, 1)

                def expert(e, more):
                    for g in range(2):
                        for i in range(ISTEPS):
                            split(e, g, i)
                            if i % 2 == 1:
                                k = i // 2 + 2
                                if k < PAIRS:
                                    weight_low(e, g, k)
                                elif g == 0:
                                    weight_low(e, 1, k - PAIRS)
                                elif more:
                                    weight_low(e + 1, 0, k - PAIRS)
                            if 8 <= i < 8 + CB and (g == 0 or more):
                                token_split(e + g, 1 - g, i - 8)
                        mix(e, g)

                weight_low(0, 0, 0)
                weight_low(0, 0, 1)
                for c in range(CB):
                    token_split(0, 0, c)
                expert(0, True)
                with dve.Fori(1, EXPERTS - 1) as e:
                    expert(e, True)
                expert(EXPERTS - 1, False)


def kernel(**inputs):
    import concourse.bacc as bacc
    from concourse.bass_utils import run_bass_kernel_spmd

    nc = bacc.Bacc("TRN2", target_bir_lowering=False, num_devices=1)
    turned = ("L0_xattn_Wq", "L0_xattn_Wk", "L0_xattn_Wv", "L0_ffn_gate_weight")
    vectors = ("L0_ffn_ln_gamma", "L0_ffn_ln_beta")
    names = ["x", "ctx_1024", "L0_xattn_Wq", "L0_xattn_Wk", "L0_xattn_Wv", "L0_xattn_bq", "L0_xattn_bk", "L0_xattn_bv",
             "L0_ffn_gate_weight", "L0_ffn_ln_gamma", "L0_ffn_ln_beta", "L0_ffn_wi", "L0_ffn_wo"]
    arrays, args = {}, []
    for name in names:
        a = np.asarray(inputs[name])
        if name in vectors:
            a = a.reshape(-1, P)
        a = np.ascontiguousarray(a.T if name in turned + vectors else a)
        arrays[f"in_{name}"] = a
        args.append(nc.dram_tensor(f"in_{name}", a.shape, mybir.dt.from_np(a.dtype), kind="ExternalInput").ap())
    out = nc.dram_tensor("out", (BATCH, SEQ, DIM), mybir.dt.float32, kind="ExternalOutput").ap()
    xattn_moe_kernel(nc, *args, out)
    r = run_bass_kernel_spmd(nc, [arrays], core_ids=[0])
    return r.results[0]["out"]
```

```python
import concourse.bass as bass
import numpy as np
from concourse import mybir
from contextlib import ExitStack

P = 128
BATCH, SEQ, DIM = 32, 512, 512
ROWT = SEQ // P
CB = DIM // P
EXPERTS, INNER = 8, 2048
CAPACITY = 2 * (4 * 1024) // EXPERTS
SLOTS = EXPERTS * CAPACITY
META = 8
ROW = DIM + META
EPS = 1e-5
R_MAP, MAP_STEPS = 3.9, 10
SKIPPED = 1 << 20

GROUP = 512
GT = GROUP // P
ISTEPS = INNER // P
PAIRS = ISTEPS // 2
RING = 4
ROWS_AT = 5


def sigmoid(v):
    return 1.0 / (1.0 + np.exp(-v))


def memory_scale():
    dop, ser, nor = (0.9 * 0.5 + 0.1 * sigmoid(v) for v in (0.7, 0.8, 0.6))
    return float(0.4 * dop + 0.3 * ser + 0.3 * nor)


def forward_matrix():
    n = np.arange(256)[:, None]
    j = np.arange(128)[None, :]
    m = np.empty((256, 2, 2, 128))
    for tile in (0, 1):
        angle = 2 * np.pi * (((2 * j + tile) * n) % 512) / 512
        m[:, tile, 0], m[:, tile, 1] = np.cos(angle), -np.sin(angle)
    m[:, 0, 1, 0] = 1 - 2 * (np.arange(256) % 2)
    return m.reshape(2, 128, 2, 256).transpose(1, 0, 2, 3).reshape(128, -1).astype(np.float32)


def inverse_matrix():
    k = np.arange(512)
    filt = np.exp(3j * 1.5 * np.arctan(np.log(k + 1e-10)))
    h = (filt + np.conj(filt[-k % 512])) / 2
    n = np.arange(256)[None, :]
    m = np.empty((128, 2, 2, 256))
    for tile in (0, 1):
        f = (2 * np.arange(128) + tile)[:, None]
        e = h[f] * np.exp(2j * np.pi * ((f * n) % 512) / 512) / 512
        m[:, tile, 0], m[:, tile, 1] = e.real, -e.imag
    m[0, 0, 0] = h[0].real / 512
    m[0, 0, 1] = h[256].real * (1 - 2 * (np.arange(256) % 2)) / 512
    return m.reshape(128, -1).astype(np.float32)


def position_scale():
    lam = np.arange(SEQ) / SEQ
    alpha = float(np.clip(1.0 * (1.0 + 0.5 * (1.5 - 2.0) / 2.0), 0.1, 3.0))
    wave = np.sin(alpha * lam) * np.cos(-2.0 * lam + 0.0 * lam ** 2)
    return (1 + 0.1 * wave).reshape(ROWT, P).T.astype(np.float32)


def quaternion_signs():
    return np.array([[-1, 1, -1, 1], [-1, 1, 1, -1], [-1, -1, 1, 1]], np.float32)


class Chain:

    def __init__(self, engine, sem, per):
        self.engine, self.sem, self.per = engine, sem, per

    def begin(self, round_, done=0):
        self.base, self.n = round_ * self.per, done

    def step(self, ins):
        self.n += 1
        ins.then_inc(self.sem, 1)
        return self.n

    def wait(self, n=None):
        self.engine.wait_ge(self.sem, self.base + (self.n if n is None else n))

    def end(self):
        assert self.n == self.per, (self.n, self.per)


def wait(engine, sem, value):
    if not isinstance(value, int) or value > 0:
        engine.wait_ge(sem, value)


def xattn_moe_kernel(nc, x, ctx_in, wq, wk, wv, bq, bk, bv, gate, gamma, beta, wi, wo, out):
    f32, f32r, bf16 = mybir.dt.float32, mybir.dt.float32r, mybir.dt.bfloat16
    i32, u32 = mybir.dt.int32, mybir.dt.uint32
    ALU, ACT, AX = mybir.AluOpType, mybir.ActivationFunctionType, mybir.AxisListType

    c_fwd = nc.inline_tensor(forward_matrix(), "c_fwd").ap()
    c_inv = nc.inline_tensor(inverse_matrix(), "c_inv").ap()
    c_pos = nc.inline_tensor(position_scale(), "c_pos").ap()
    c_sgn = nc.inline_tensor(np.tile(np.repeat(quaternion_signs().reshape(1, 12), 8, 1), (16, 1)), "c_sgn").ap()
    c_tri = nc.inline_tensor(np.triu(np.ones((P, P), np.float32), 1), "c_tri").ap()
    c_eye = nc.inline_tensor(np.eye(P, dtype=np.float32), "c_eye").ap()
    c_tok = nc.inline_tensor((np.arange(SEQ, dtype=np.float32)).reshape(ROWT, P).T.copy(), "c_tok").ap()
    c_exp = nc.inline_tensor(np.tile(np.arange(EXPERTS, dtype=np.float32) - EXPERTS, (P, ROWT)), "c_exp").ap()
    bins_in = nc.dram_tensor("bins_in", [1, 6 * DIM], f32, kind="Internal").ap()
    bins_out = nc.dram_tensor("bins_out", [1, 2 * DIM], f32, kind="Internal").ap()
    slots = nc.dram_tensor("slots", [SLOTS, ROW], f32, kind="Internal").ap()

    outer = ExitStack()
    with outer:
        def sem(name):
            return outer.enter_context(nc.semaphore(name))

        eye = outer.enter_context(nc.sbuf_tensor("eye", [P, P], f32))
        gam, bet = (outer.enter_context(nc.sbuf_tensor(n, [P, CB], f32)) for n in ("gam", "bet"))
        w_raw = [outer.enter_context(nc.sbuf_tensor(f"w_raw{i}", [P, 2, 1024], f32)) for i in (0, 1)]
        raw_in = [sem(f"raw_in{i}") for i in (0, 1)]

        with ExitStack() as mem:
            def sb(name, shape, dt=f32):
                return mem.enter_context(nc.sbuf_tensor(name, shape, dt))

            def pb(name, shape):
                return mem.enter_context(nc.psum_tensor(name, shape, f32))

            fwd = sb("fwd", [P, 2, 2, 256])
            inv = sb("inv", [P, 2, 2, 256])
            w_q = sb("w_q", [P, CB, DIM])
            w_kh, w_kl, w_vh, w_vl = (sb(n, [P, CB, DIM], f32r) for n in ("w_kh", "w_kl", "w_vh", "w_vl"))
            c_high, c_low = (sb(n, [P, CB, 512], f32r) for n in ("c_high", "c_low"))
            pos = sb("pos", [P, ROWT])
            signs = sb("signs", [16, 3, 4, 8])
            tri, ones = sb("tri", [P, P], bf16), sb("ones", [P, P], bf16)
            token = sb("token", [P, ROWT])
            iota8 = sb("iota8", [P, ROWT, EXPERTS])
            gate_t = sb("gate_t", [P, CB, EXPERTS])
            gate_b = sb("gate_b", [P, CB, EXPERTS])
            gate_g = sb("gate_g", [P, CB, EXPERTS])
            gate_c = sb("gate_c", [P, EXPERTS])
            values = dict(minus_half=-0.5, half=0.5, minus_one=-1.0, zero=0.0, one=1.0, eps=EPS, dim=float(DIM), seq=float(SEQ),
                          inv_dim=1.0 / DIM, minus_inv_dim=-1.0 / DIM, inv_e=float(np.exp(-1.0)), r_map=R_MAP, strength=0.1, rest=1.0 - 0.1 * 0.5)
            const = {n: sb(n, [P, ROWT]) for n in values}
            bias16 = sb("bias16", [16, 3, 4, 8])
            running = sb("running", [P, EXPERTS])

            x_in, c_in = (w[:].rearrange("p a (b n) -> p (a b) n", n=DIM) for w in w_raw)
            x_res = sb("x_res", [P, ROWT, DIM])
            q_rows = x_in
            q_fold, c_fold = (sb(n, [P, 2, 2, DIM]) for n in ("q_fold", "c_fold"))
            q_spec, c_spec = (sb(n, [P, CB, 512]) for n in ("q_spec", "c_spec"))

            def last_sequence(b):
                return isinstance(b, int) and b == BATCH - 1

            def residual(b):
                return c_fold[:].rearrange("p a t n -> p (a t) n") if last_sequence(b) else x_res[:]

            re_buf = [sb(f"re{i}", [P, DIM]) for i in (0, 1)]
            s1, s2 = ([sb(f"{n}_{i}", [P, 2, 4, P]) for i in (0, 1)] for n in ("s1", "s2"))
            tri32, ones32 = s2[0][:, 0, 0], s2[0][:, 0, 1]
            prod = sb("prod", [P, 4, 2, DIM])
            kv_raw = prod[:].rearrange("p (w a) b n -> p w (a b) n", w=2)
            r_spec = sb("r_spec", [P, 2, 2, 4, P])
            real_row = sb("real_row", [1, 3, 2, DIM])
            real_in = sb("real_in", [16, 3, 2, 4, 8])
            real_t = sb("real_t", [16, 2, 4, 4, 8])
            real_u = sb("real_u", [16, 2, 4, 8])
            real_v = sb("real_v", [16, 2, 4, 8])
            real_p = sb("real_p", [16, 2, 4, 8])
            rows = sb("rows", [P, ROWT, ROW])
            x_tok = sb("x_tok", [P, ROWT, DIM])
            empty = x_tok[:].rearrange("p t n -> p (t n)")[:, 0:ROW].rearrange("p (o n) -> p o n", o=1)
            x_tok_t = [sb(f"x_tok_t{i}", [P, CB, P]) for i in (0, 1)]
            sum1, sum2, square1, square2, neg1, neg2 = (sb(n, [P, ROWT]) for n in ("sum1", "sum2", "square1", "square2", "neg1", "neg2"))
            unused = [[sb(f"unused{i}{j}", [P, DIM], bf16) for j in (0, 1)] for i in (0, 1)]
            st = [sb(f"st{i}", [P, ROWT]) for i in range(11)]
            q_scale, q_bias = sb("q_scale", [P, ROWT]), sb("q_bias", [P, ROWT])
            tt = [sb(f"tt{i}", [P, ROWT]) for i in range(6)]
            logit, over, e_over, cand, picked = (sb(n, [P, ROWT, EXPERTS]) for n in ("logit", "over", "e_over", "cand", "picked"))
            onehot = sb("onehot", [P, ROWT, EXPERTS], bf16)
            top = sb("top", [P, ROWT])
            first = sb("first", [P, ROWT])
            denom = sb("denom", [P, ROWT])
            rank = sb("rank", [P, ROWT])
            far = sb("far", [P, ROWT])
            slot_f = sb("slot_f", [P, ROWT])
            slot_i = sb("slot_i", [P, ROWT], i32)

            pair = [pb(f"pair{i}", [P, 2, 512]) for i in (0, 1)]
            xt_ps = [pb(f"xt_ps{i}", [P, 512]) for i in (0, 1)]
            even_ps, odd_ps = pb("even_ps", [P, 512]), pb("odd_ps", [P, 512])

            SETUP_DMAS = 15
            ZEROED = len(values) + 5
            fwd_in, pos_in, consts_in = sem("fwd_in"), sem("pos_in"), sem("consts_in")
            zeroed = sem("zeroed")
            token_next = sem("token_next")
            setup_v = sem("setup_v")
            setup_mm = sem("setup_mm")
            scaled = sem("scaled")
            w_split, c_split = sem("w_split"), sem("c_split")
            slots_clear = sem("slots_clear")
            x_loaded, c_loaded, res_loaded = sem("x_loaded"), sem("c_loaded"), sem("res_loaded")
            last_res_loaded = sem("last_res_loaded")
            real_left, real_back = sem("real_left"), sem("real_back")
            real_loaded, real_stored = sem("real_loaded"), sem("real_stored")
            base_stored, scattered = sem("base_stored"), sem("scattered")
            sums1 = sem("sums1")
            stat1 = sem("stat1")
            q_ready = sem("q_ready")
            qf_ready, cf_ready = sem("qf_ready"), sem("cf_ready")
            f1_mm, f1_ev = sem("f1_mm"), sem("f1_ev")
            f2_mm, re_ready, conv = sem("f2_mm"), sem("re_ready"), sem("conv")
            ham = sem("ham")
            inv_mm, unfold = sem("inv_mm"), sem("unfold")
            sums2, stat2 = sem("sums2"), sem("stat2")
            tok_ready, base_ready = sem("tok_ready"), sem("base_ready")
            g_mm, g_ev, logit_mm = sem("g_mm"), sem("g_ev"), sem("logit_mm")
            route, exp_done, rank_mm = sem("route"), sem("exp_done"), sem("rank_mm")
            real_step = sem("real_step")

            SUMS, STAT1, STAT2, CONV, HAM, UNF, ROUTE, REAL = 8, 46, 12, 24, 54, 8, 16, 27
            HAM_E, HAM_O = 27, 54
            PROJ = [(0, 0), (0, 1), (0, 2), (1, 0), (1, 1), (1, 2)]

            def seq(v, b):
                return v[bass.ds(b, 1), :, :].rearrange("a (t p) n -> p (a t) n", p=P)

            with nc.Block() as block:

                @block.sync
                def _(sp):
                    def load_x(b):
                        wait(sp, qf_ready, b * 2)
                        sp.dma_start(x_in, seq(x, b)).then_inc(x_loaded, 16)

                    def load_c(b):
                        wait(sp, cf_ready, b * 2)
                        sp.dma_start(c_in, seq(ctx_in, b)).then_inc(c_loaded, 16)

                    def batch(b, back, ahead):
                        if last_sequence(b):
                            load_res(b)
                        if ahead:
                            load_c(b + 2)
                        sp.wait_ge(re_ready, b * 6 + 3)
                        sp.dma_start(bins_in, real_row[:].rearrange("o a s n -> o (a s n)")).then_inc(real_left, 16)
                        sp.wait_ge(real_left, b * 16 + 16)
                        sp.dma_start(real_in[:].rearrange("q a s c e -> q (a s c) e"),
                                     bins_in.rearrange("o (k q e) -> q (o k) e", q=16, e=8)).then_inc(real_loaded, 16)
                        if ahead:
                            load_x(b + 2)
                        if not back:
                            clear(1)
                        sp.wait_ge(real_step, b * REAL + REAL)
                        sp.dma_start(bins_out.rearrange("o (k q e) -> q (o k) e", q=16, e=8),
                                     real_p[:].rearrange("q s c e -> q (s c) e")).then_inc(real_back, 16)
                        sp.wait_ge(ham, b * HAM + HAM_E)
                        sp.wait_ge(real_back, b * 16 + 16)
                        sp.dma_start(r_spec[0:1, 0].rearrange("o s c e -> o (s c e)"), bins_out).then_inc(real_stored, 16)
                        if back:
                            store(b - 1)
                            if not last_sequence(b):
                                load_res(b)

                    def load_res(b):
                        if last_sequence(b):
                            sp.wait_ge(f1_mm, b * 8 + 4)
                            sp.dma_start(residual(b), seq(x, b)).then_inc(last_res_loaded, 16)
                        else:
                            wait(sp, base_stored, b * 16)
                            sp.dma_start(residual(b), seq(x, b)).then_inc(res_loaded, 16)

                    def store(b):
                        sp.wait_ge(base_ready, b * 4 + 4)
                        sp.dma_start(seq(out, b), residual(b)).then_inc(base_stored, 16)

                    def clear(t):
                        sp.dma_start(slots.rearrange("(s t p) n -> p s t n", t=ROWT, p=P)[:, :, t, :],
                                     empty.broadcast_to([P, SLOTS // (ROWT * P), ROW])).then_inc(slots_clear, 16)

                    load_x(0)
                    load_c(0)
                    sp.dma_start(fwd[:].rearrange("p a b c -> p (a b c)"), c_fwd).then_inc(fwd_in, 16)
                    sp.dma_start(pos[:], c_pos).then_inc(pos_in, 16)
                    for dst, src in ((signs[:].rearrange("p a b c -> p (a b c)"), c_sgn),
                                     (tri32, c_tri), (eye[:], c_eye), (token[:], c_tok),
                                     (iota8[:].rearrange("p t e -> p (t e)"), c_exp),
                                     (w_q[:], wq.rearrange("(k p) n -> p k n", p=P)),
                                     (kv_raw[:, 0], wk.rearrange("(k p) n -> p k n", p=P)),
                                     (kv_raw[:, 1], wv.rearrange("(k p) n -> p k n", p=P)),
                                     (inv[:].rearrange("p a b c -> p (a b c)"), c_inv),
                                     (gate_t[:], gate.rearrange("(k p) e -> p k e", p=P)),
                                     (gam[:], gamma),
                                     (bet[:], beta)):
                        sp.dma_start(dst, src).then_inc(consts_in, 16)
                    for a, v in enumerate((bq, bk, bv)):
                        sp.dma_start(bias16[:, a], v.rearrange("(c q e) -> q c e", c=4, q=16)).then_inc(consts_in, 16)
                    load_x(1)
                    load_c(1)
                    load_res(0)
                    sp.wait_ge(setup_v, 1)
                    clear(0)
                    batch(0, False, True)
                    clear(2)
                    clear(3)
                    with sp.Fori(1, BATCH - 2) as b:
                        batch(b, True, True)
                    batch(BATCH - 2, True, False)
                    batch(BATCH - 1, True, False)
                    sp.wait_ge(qf_ready, BATCH * 2)
                    sp.wait_ge(cf_ready, BATCH * 2)
                    for k in range(2):
                        load_weights(sp, w_raw, raw_in, wi, wo, 0, k)
                    store(BATCH - 1)
                    sp.wait_ge(base_stored, 16 * BATCH)
                    sp.wait_ge(scattered, 64 * BATCH)

                @block.tensor
                def _(pe):
                    pe.wait_ge(fwd_in, 16)

                    def dft(b, folded, ready, first_unit):
                        pe.wait_ge(ready, b * 2 + 2)
                        for u in range(4):
                            if first_unit + u < 2:
                                wait(pe, f1_ev, b * 8)
                            else:
                                pe.wait_ge(f1_ev, b * 8 + first_unit + u - 1)
                            ps = xt_ps[u % 2]
                            for eo in range(2):
                                for t in range(2):
                                    last = nc.tensor.matmul(ps[:, eo * 256:eo * 256 + 256],
                                                            folded[:, eo, t, u * P:(u + 1) * P], fwd[:, t, eo, :],
                                                            start=(t == 0), stop=(t == 1))
                            last.then_inc(f1_mm, 1)

                    def project(b, k, slots=(0, 1)):
                        tile, which = PROJ[k]
                        wh, wl = ((w_kh, w_kl), (w_vh, w_vl))[which - 1]
                        terms = ((q_spec, w_q),) if which == 0 else ((c_high, wh), (c_low, wh), (c_high, wl))
                        if k == 0 and 0 in slots:
                            pe.wait_ge(f1_ev, b * 8 + 8)
                        if k == 1:
                            pe.wait_ge(c_split, b * 2 + 2)
                        if 0 in slots:
                            wait(pe, conv, b * CONV + (k - 1) * 4)
                        for s in slots:
                            for c in range(CB):
                                for n, (spec, w) in enumerate(terms):
                                    last = nc.tensor.matmul(pair[k % 2][:, s, :],
                                                            spec[:, c, tile * 256 + s * P:tile * 256 + (s + 1) * P],
                                                            w[:, c, :], start=(c == 0 and n == 0),
                                                            stop=(c == CB - 1 and n == len(terms) - 1))
                        if 1 in slots:
                            last.then_inc(f2_mm, 1)

                    def inverse(b, t):
                        if t == 0:
                            pe.wait_ge(ham, b * HAM + HAM_O)
                            pe.wait_ge(real_stored, b * 16 + 16)
                            wait(pe, route, b * ROUTE)
                        for tile, ps in ((0, even_ps), (1, odd_ps)):
                            if t:
                                pe.wait_ge(unfold, b * UNF + (2 if tile == 0 else 4))
                            for s in range(2):
                                last = nc.tensor.matmul(ps[:], inv[:, tile, s, t * P:(t + 1) * P],
                                                        r_spec[:, tile, s].rearrange("p c e -> p (c e)"),
                                                        start=(s == 0), stop=(s == 1))
                            last.then_inc(inv_mm, 1)

                    def turn(b, t, f1_done):
                        pe.wait_ge(tok_ready, b * 4 + t + 1)
                        if t < 2:
                            pe.wait_ge(f1_ev, f1_done)
                        else:
                            pe.wait_ge(g_ev, b * 4 + t - 1)
                        for c in range(CB):
                            last = nc.tensor.transpose(xt_ps[t % 2][:, c * P:(c + 1) * P],
                                                       x_tok[:, t, c * P:(c + 1) * P], eye[:])
                        last.then_inc(g_mm, 1)

                    def logits(b, t):
                        pe.wait_ge(g_ev, b * 4 + t + 1)
                        if t == 0:
                            pe.wait_ge(unfold, b * UNF + UNF)
                        for c in range(CB):
                            last = nc.tensor.matmul(even_ps[:, t * EXPERTS:(t + 1) * EXPERTS], x_tok_t[t % 2][:, c, :],
                                                    gate_g[:, c, :], start=(c == 0), stop=(c == CB - 1))
                        last.then_inc(logit_mm, 1)

                    def ranks(b):
                        pe.wait_ge(route, b * ROUTE + 6)
                        for t in range(ROWT + 1):
                            o = odd_ps[:, t * EXPERTS:(t + 1) * EXPERTS]
                            for u in range(t):
                                last = nc.tensor.matmul(o, ones[:], onehot[:, u, :], start=(u == 0),
                                                        stop=(t == ROWT and u == t - 1))
                            if t < ROWT:
                                nc.tensor.matmul(o, tri[:], onehot[:, t, :], start=(t == 0), stop=True)
                        last.then_inc(rank_mm, 1)

                    dft(0, c_fold, cf_ready, 0)
                    dft(0, q_fold, qf_ready, 4)
                    pe.wait_ge(consts_in, 16 * SETUP_DMAS)
                    project(0, 0)
                    pe.wait_ge(setup_v, 11)
                    for c in range(CB):
                        last = nc.tensor.matmul(even_ps[:, 0:EXPERTS], ones32, gate_b[:, c, :], start=(c == 0), stop=(c == CB - 1))
                    last.then_inc(setup_mm, 1)
                    pe.wait_ge(w_split, 2)
                    project(0, 1)
                    pe.wait_ge(setup_v, 12)
                    project(0, 2)

                    def batch(b, back, ahead):
                        project(b, 3)
                        if back:
                            inverse(b - 1, 0)
                        project(b, 4)
                        if back:
                            inverse(b - 1, 1)
                        if ahead:
                            dft(b + 1, c_fold, cf_ready, 0)
                            dft(b + 1, q_fold, qf_ready, 4)
                        project(b, 5)
                        router(b - 1, b * 8 + (16 if ahead else 8), back, ahead)

                    def router(b, f1_done, back, ahead):
                        if ahead:
                            project(b + 2, 0, (0,))
                        if back:
                            turn(b, 0, f1_done)
                            turn(b, 1, f1_done)
                        if ahead:
                            project(b + 2, 0, (1,))
                        if back:
                            for t in range(2):
                                logits(b, t)
                                turn(b, t + 2, f1_done)
                        if ahead:
                            project(b + 2, 1)
                        if back:
                            logits(b, 2)
                            logits(b, 3)
                        if ahead:
                            project(b + 2, 2)
                        if back:
                            ranks(b)

                    batch(0, False, True)
                    with pe.Fori(1, BATCH - 1) as b:
                        batch(b, True, True)
                    batch(BATCH - 1, True, False)
                    inverse(BATCH - 1, 0)
                    inverse(BATCH - 1, 1)
                    router(BATCH - 1, BATCH * 8, True, False)

                @block.scalar
                def _(act):
                    def scale_weights():
                        act.wait_ge(consts_in, 16 * SETUP_DMAS)
                        for n in range(2):
                            nc.scalar.activation(kv_raw[:, n], kv_raw[:, n], ACT.Copy, scale=memory_scale()).then_inc(scaled, 1)

                    def weight_high(n, high):
                        act.wait_ge(scaled, n + 1)
                        nc.scalar.activation(high[:], kv_raw[:, n], ACT.Copy).then_inc(scaled, 1)

                    def row_sum(b, t, src, into, ready, read, sums, unused):
                        if t == 0:
                            act.wait_ge(*ready)
                            wait(act, *read)
                        if t > 1:
                            act.wait_ge(sums, b * SUMS + t - 1)
                        nc.scalar.activation(unused[t % 2][:], src[:, t, 0:DIM], ACT.Copy,
                                             accum_out=into[:, t:t + 1]).then_inc(sums, 1)

                    def square_sum(b, t, src, neg, into, mean, sums, unused):
                        if t == 0:
                            act.wait_ge(*mean)
                        act.wait_ge(sums, b * SUMS + 4 + t - 1)
                        nc.scalar.activation(unused[t % 2][:], src[:, t, 0:DIM], ACT.Square, bias=neg[:, t:t + 1],
                                             accum_out=into[:, t:t + 1]).then_inc(sums, 1)

                    def sum_x(b, t):
                        row_sum(b, t, x_in, sum1, (x_loaded, b * 16 + 16), (stat1, b * STAT1), sums1, unused[0])

                    def square_x(b, t):
                        square_sum(b, t, x_in, neg1, square1, (stat1, b * STAT1 + 1), sums1, unused[0])

                    def sum_x2(b, t):
                        row_sum(b, t, rows, sum2, (unfold, b * UNF + UNF), (stat2, b * STAT2), sums2, unused[1])

                    def square_x2(b, t):
                        square_sum(b, t, rows, neg2, square2, (stat2, b * STAT2 + 1), sums2, unused[1])

                    def all_tiles(b, *steps):
                        for step in steps:
                            for t in range(ROWT):
                                step(b, t)

                    def q_of(b):
                        act.wait_ge(stat1, b * STAT1 + STAT1)
                        for t in range(ROWT):
                            nc.scalar.activation(q_rows[:, t, :], x_in[:, t, :], ACT.Identity, bias=q_bias[:, t:t + 1],
                                                 scale=q_scale[:, t:t + 1]).then_inc(q_ready, 1)

                    def spectra(b, spec, first_unit, free, between):
                        for u in range(4):
                            act.wait_ge(f1_mm, b * 8 + first_unit + u + 1)
                            if u == 0:
                                wait(act, *free)
                            nc.scalar.activation(spec[:, u, :], xt_ps[u % 2][:], ACT.Copy).then_inc(f1_ev, 1)
                            for step, b_ in between:
                                step(b_, u)

                    def context_high(b):
                        act.wait_ge(f1_ev, b * 8 + 4)
                        wait(act, f2_mm, b * 6)
                        nc.scalar.activation(c_high[:], c_spec[:], ACT.Copy).then_inc(c_split, 1)

                    def real_parts(b, k):
                        tile, which = PROJ[k]
                        act.wait_ge(f2_mm, b * 6 + k + 1)
                        if k == 0:
                            wait(act, real_loaded, b * 16)
                        if tile == 0:
                            nc.scalar.activation(real_row[0:1, which], pair[k % 2][0:1, :, :], ACT.Copy)
                        wait(act, conv, b * CONV + (k - 1) * 4)
                        nc.scalar.activation(re_buf[k % 2][:], pair[k % 2][:, 0, :], ACT.Copy).then_inc(re_ready, 1)

                    def tokens(b):
                        act.wait_ge(stat2, b * STAT2 + STAT2)
                        wait(act, logit_mm, b * 4)
                        act.wait_ge(slots_clear, 64)
                        for t in range(ROWT):
                            nc.scalar.activation(x_tok[:, t, :], rows[:, t, 0:DIM], ACT.Identity,
                                                 bias=rows[:, t, DIM + 3:DIM + 4],
                                                 scale=rows[:, t, DIM + 2:DIM + 3]).then_inc(tok_ready, 1)

                    def base_of(b):
                        for t in range(ROWT):
                            nc.scalar.activation(residual(b)[:, t, :], rows[:, t, 0:DIM], ACT.Identity,
                                                 bias=rows[:, t, DIM + 5:DIM + 6],
                                                 scale=rows[:, t, DIM + 4:DIM + 5]).then_inc(base_ready, 1)

                    def token_blocks(b, tiles):
                        for t in tiles:
                            act.wait_ge(g_mm, b * 4 + t + 1)
                            if t < 2:
                                wait(act, logit_mm, b * 4)
                            else:
                                act.wait_ge(logit_mm, b * 4 + t - 1)
                            nc.scalar.activation(x_tok_t[t % 2][:].rearrange("p c e -> p (c e)"), xt_ps[t % 2][:],
                                                 ACT.Copy).then_inc(g_ev, 1)

                    def exps(b):
                        act.wait_ge(route, b * ROUTE + 3)
                        nc.scalar.activation(e_over[:], over[:], ACT.Exp).then_inc(exp_done, 1)

                    def spectra_c(b, *between):
                        spectra(b, c_spec, 0, (c_split, b * 2), between)

                    def spectra_q(b, *between):
                        spectra(b, q_spec, 4, (f2_mm, b * 6 - 2), between)

                    all_tiles(0, sum_x, square_x)
                    spectra_c(0)
                    scale_weights()
                    weight_high(0, w_kh)
                    q_of(0)
                    weight_high(1, w_vh)
                    context_high(0)
                    spectra_q(0)
                    all_tiles(1, sum_x, square_x)
                    real_parts(0, 0)
                    real_parts(0, 1)

                    def batch(b, back, ahead, ahead2):
                        if ahead:
                            q_of(b + 1)
                        real_parts(b, 2)
                        real_parts(b, 3)
                        real_parts(b, 4)
                        of_x2 = [[(step, b - 1)] if back else [] for step in (sum_x2, square_x2)]
                        of_x = [[(step, b + 2)] if ahead2 else [] for step in (sum_x, square_x)]
                        if ahead:
                            spectra_c(b + 1, *of_x[0])
                        if back:
                            all_tiles(b - 1, sum_x2)
                        if ahead:
                            spectra_q(b + 1, *of_x2[1], *of_x[1])
                        else:
                            all_tiles(b - 1, square_x2)
                        real_parts(b, 5)
                        if back:
                            tokens(b - 1)
                            token_blocks(b - 1, (0, 1))
                        if ahead:
                            context_high(b + 1)
                            real_parts(b + 1, 0)
                        if back:
                            token_blocks(b - 1, (2, 3))
                            base_of(b - 1)
                        if ahead:
                            real_parts(b + 1, 1)
                        if back:
                            exps(b - 1)

                    batch(0, False, True, True)
                    with act.Fori(1, BATCH - 2) as b:
                        batch(b, True, True, True)
                    batch(BATCH - 2, True, True, False)
                    batch(BATCH - 1, True, False, False)
                    all_tiles(BATCH - 1, sum_x2, square_x2)
                    tokens(BATCH - 1)
                    token_blocks(BATCH - 1, range(ROWT))
                    base_of(BATCH - 1)
                    exps(BATCH - 1)

                @block.gpsimd
                def _(pool):
                    s1c = Chain(pool, stat1, STAT1)
                    s2c = Chain(pool, stat2, STAT2)
                    rc = Chain(pool, real_step, REAL)
                    ts, tv = nc.gpsimd.tensor_scalar, nc.gpsimd.tensor_tensor

                    k = {n: t[:] for n, t in const.items()}
                    for n, v in values.items():
                        nc.gpsimd.memset(k[n], v).then_inc(zeroed, 1)
                    for dst, v in ((ones32, 1.0), (running[:], 0.0), (rows[:], 0.0), (empty, 0.0)):
                        nc.gpsimd.memset(dst, v).then_inc(zeroed, 1)
                    pool.wait_ge(zeroed, ZEROED - 1)
                    pool.wait_ge(pos_in, 16)

                    def mean_of(c, b, sums, total, neg):
                        pool.wait_ge(sums, b * SUMS + 4)
                        c.begin(b)
                        c.step(tv(neg[:], total[:], k["minus_inv_dim"], ALU.mult))

                    def stats1(b):
                        c = s1c
                        pool.wait_ge(sums1, b * SUMS + SUMS)
                        wait(pool, q_ready, b * 4)
                        a, rstd, r2, n2, norm, e, s, u, v, rs, var = (z[:] for z in st)
                        c.step(tv(var, square1[:], k["inv_dim"], ALU.mult)); c.wait()
                        c.step(tv(a, var, k["eps"], ALU.add)); c.wait()
                        c.step(tv(rstd, a, k["minus_half"], ALU.pow)); c.wait()
                        c.step(tv(r2, rstd, rstd, ALU.mult)); c.wait()
                        c.step(tv(n2, var, r2, ALU.mult)); c.wait()
                        c.step(tv(n2, n2, k["dim"], ALU.mult)); c.wait()
                        c.step(tv(norm, n2, k["half"], ALU.pow)); c.wait()
                        c.step(tv(e, k["inv_e"], norm, ALU.pow)); c.wait()
                        c.step(tv(e, e, k["one"], ALU.add)); c.wait()
                        c.step(tv(s, e, k["minus_one"], ALU.pow)); c.wait()
                        for _ in range(MAP_STEPS):
                            c.step(tv(u, s, k["r_map"], ALU.mult))
                            c.step(tv(v, k["one"], s, ALU.subtract)); c.wait()
                            c.step(tv(s, u, v, ALU.mult)); c.wait()
                        c.step(tv(s, s, k["strength"], ALU.mult)); c.wait()
                        c.step(tv(s, s, k["rest"], ALU.add)); c.wait()
                        c.step(tv(rs, s, pos[:], ALU.mult)); c.wait()
                        c.step(tv(q_scale[:], rs, rstd, ALU.mult)); c.wait()
                        c.step(tv(q_bias[:], neg1[:], q_scale[:], ALU.mult))
                        c.end()

                    def stats2(b):
                        c = s2c
                        pool.wait_ge(sums2, b * SUMS + SUMS)
                        a, rstd, r2, v2, n2, var = (z[:] for z in tt)
                        neg = neg2[:]
                        meta = rows[:, :, DIM:DIM + META]
                        a2, nb2, s1_, nb = (meta[:, :, k] for k in (2, 3, 4, 5))
                        c.step(tv(var, square2[:], k["inv_dim"], ALU.mult)); c.wait()
                        c.step(tv(a, var, k["eps"], ALU.add)); c.wait()
                        c.step(tv(rstd, a, k["minus_half"], ALU.pow)); c.wait()
                        c.step(tv(r2, rstd, rstd, ALU.mult)); c.wait()
                        c.step(tv(v2, var, r2, ALU.mult)); c.wait()
                        c.step(tv(v2, v2, k["eps"], ALU.add)); c.wait()
                        c.step(tv(n2, v2, k["minus_half"], ALU.pow)); c.wait()
                        c.step(tv(a2, rstd, n2, ALU.mult))
                        c.step(tv(s1_, rstd, k["one"], ALU.add)); c.wait()
                        c.step(tv(nb, neg, rstd, ALU.mult))
                        c.step(tv(nb2, neg, a2, ALU.mult))
                        c.end()

                    def real_bins(b):
                        pool.wait_ge(real_loaded, b * 16 + 16)
                        wait(pool, real_stored, b * 16)
                        c = rc
                        c.begin(b)
                        c.step(tv(real_in[:, :, 0], real_in[:, :, 0], bias16[:], ALU.add)); c.wait()
                        left = real_in[:, 0]
                        for which, to in ((1, real_u), (2, real_p)):
                            right = real_in[:, which]
                            for s in range(2):
                                for d in range(4):
                                    a_ = left[:, s, d:d + 1, :]
                                    if d == 0:
                                        o, i0, i1 = real_t[:, s, 0], a_.broadcast_to([16, 4, 8]), right[:, s]
                                    else:
                                        o = real_t[:, s, d].rearrange("q (h l) e -> q h l e", h=2)
                                        i0 = bass.AP(a_.tensor, a_.offset, [list(a_.ap[0]), [0, 2], [0, 2], [1, 8]])
                                        r0 = right[:, s, d:d + 1, :]
                                        i1 = bass.AP(r0.tensor, r0.offset, [list(r0.ap[0]), [16 if d == 1 else -16, 2],
                                                                            [8 if d == 2 else -8, 2], [1, 8]])
                                    c.step(tv(o, i0, i1, ALU.mult))
                            c.wait()
                            for s in range(2):
                                c.step(tv(real_t[:, s, 1:4], real_t[:, s, 1:4], signs[:], ALU.mult))
                            c.wait()
                            c.step(tv(real_v[:], real_t[:, :, 0], real_t[:, :, 1], ALU.add))
                            c.step(tv(real_t[:, :, 2], real_t[:, :, 2], real_t[:, :, 3], ALU.add)); c.wait()
                            c.step(tv(to[:], real_v[:], real_t[:, :, 2], ALU.add))
                            if which == 1:
                                c.wait()
                            left = real_u[:]
                        c.end()

                    def scatter(b):
                        pool.wait_ge(route, b * ROUTE + ROUTE)
                        pool.wait_ge(base_ready, b * 4 + 4)
                        tv(token[:], token[:], k["seq"], ALU.add).then_inc(token_next, 1)
                        for t in range(ROWT):
                            nc.gpsimd.indirect_dma_start(
                                slots, bass.IndirectOffsetOnAxis(ap=slot_i[:, t:t + 1].bitcast(u32), axis=0),
                                rows[:, t, :], None, bounds_check=SLOTS - 1, oob_is_err=False).then_inc(scattered, 16)

                    def batch(b, product, router, ahead):
                        if product:
                            real_bins(b - 1)
                        if ahead:
                            mean1(b + 1)
                        if router:
                            mean2(b - 2)
                            stats2(b - 2)
                        if ahead:
                            stats1(b + 1)
                        if router:
                            scatter(b - 2)

                    def mean1(b):
                        mean_of(s1c, b, sums1, sum1, neg1)

                    def mean2(b):
                        mean_of(s2c, b, sums2, sum2, neg2)

                    mean1(0)
                    stats1(0)
                    pool.wait_ge(consts_in, 16 * SETUP_DMAS)
                    ts(bias16[:], bias16[:], float(SEQ), 0.0, ALU.mult, ALU.add).then_inc(zeroed, 1)
                    pool.wait_ge(zeroed, ZEROED)
                    batch(0, False, False, True)
                    batch(1, True, False, True)
                    pool.wait_ge(slots_clear, 64)
                    with pool.Fori(2, BATCH - 1) as b:
                        batch(b, True, True, True)
                    batch(BATCH - 1, True, True, False)
                    real_bins(BATCH - 1)
                    for b in (BATCH - 2, BATCH - 1):
                        mean2(b)
                        stats2(b)
                        scatter(b)

                @block.vector
                def _(dve):
                    v = nc.vector
                    setup = Chain(dve, setup_v, 12)
                    hc, uc, ro = Chain(dve, ham, HAM), Chain(dve, unfold, UNF), Chain(dve, route, ROUTE)

                    def fold(b, src, dst, ready, source, users):
                        dve.wait_ge(*source)
                        wait(dve, f1_mm, users)
                        for eo, op in ((0, ALU.add), (1, ALU.subtract)):
                            v.tensor_tensor(dst[:, eo], src[:, 0:2], src[:, 2:4], op).then_inc(ready, 1)

                    def folds_q(b):
                        fold(b, q_rows, q_fold, qf_ready, (q_ready, b * 4 + 4), b * 8)

                    def folds_c(b):
                        fold(b, c_in, c_fold, cf_ready, (c_loaded, b * 16 + 16), b * 8 - 4)

                    def context_low(b):
                        dve.wait_ge(c_split, b * 2 + 1)
                        v.tensor_tensor(c_low[:], c_spec[:], c_high[:].bitcast(f32), ALU.subtract).then_inc(c_split, 1)

                    folds_c(0)
                    dve.wait_ge(consts_in, 16 * SETUP_DMAS)
                    dve.wait_ge(zeroed, ZEROED - 1)
                    setup.begin(0)
                    setup.step(v.tensor_scalar(empty[:, 0, DIM:DIM + 1].bitcast(i32), token[:, 0:1], 0.0,
                                               float(BATCH * SEQ), ALU.mult, ALU.add))
                    setup.step(v.tensor_copy(tri[:], tri32))
                    setup.step(v.tensor_copy(ones[:], ones32))
                    for c in range(CB):
                        setup.step(v.tensor_scalar(gate_b[:, c, :], gate_t[:, c, :], bet[:, c:c + 1], None, ALU.mult))
                        setup.step(v.tensor_scalar(gate_g[:, c, :], gate_t[:, c, :], gam[:, c:c + 1], None, ALU.mult))
                    folds_q(0)
                    dve.wait_ge(scaled, 4)
                    for n, (high, low) in enumerate(((w_kh, w_kl), (w_vh, w_vl))):
                        v.tensor_tensor(low[:], kv_raw[:, n], high[:].bitcast(f32), ALU.subtract).then_inc(w_split, 1)
                    dve.wait_ge(w_split, 2)
                    context_low(0)
                    folds_c(1)
                    dve.wait_ge(setup_mm, 1)
                    setup.step(v.tensor_copy(gate_c[:], even_ps[:, 0:EXPERTS]))
                    setup.end()
                    setup.wait()

                    def convert(b, k):
                        dve.wait_ge(re_ready, b * 6 + k + 1)
                        tile, which = PROJ[k]
                        dst = s1[tile] if which == 0 else s2[which - 1]
                        re = re_buf[k % 2][:].rearrange("p (h l e) -> p h l e", h=2, l=2)
                        im = pair[k % 2][:, 1, :].rearrange("p (h l e) -> p h l e", h=2, l=2)
                        a_b, d_c = dst[:, :, 0:2, :], down(dst, 3)
                        wy_re, xz_re, wy_im, xz_im = re[:, :, 0], re[:, :, 1], im[:, :, 0], im[:, :, 1]
                        v.tensor_tensor(a_b[:, 0], wy_re, xz_im, ALU.subtract).then_inc(conv, 1)
                        v.tensor_tensor(a_b[:, 1], xz_re, wy_im, ALU.add).then_inc(conv, 1)
                        v.tensor_tensor(d_c[0], wy_re, xz_im, ALU.add).then_inc(conv, 1)
                        v.tensor_tensor(d_c[1], wy_im, xz_re, ALU.subtract).then_inc(conv, 1)

                    def down(s, start):
                        out_ = []
                        for slot in range(2):
                            r = s[:, slot, start:start + 1, :]
                            out_.append(bass.AP(r.tensor, r.offset, [list(r.ap[0]), [-P, 2], [1, P]]))
                        return out_

                    def view(s, slot, first_, steps):
                        r = s[:, slot, first_:first_ + 1, :]
                        return bass.AP(r.tensor, r.offset, [list(r.ap[0]), [steps[0] * P, 2], [steps[1] * P, 2], [1, P]])

                    def hamilton(b, k, between=None):
                        products(b, k)
                        if between:
                            between()
                        sums(b, k)

                    def products(b, k):
                        l, r = s1[PROJ[k][0]], s2[PROJ[k][1] - 1]
                        dve.wait_ge(conv, b * CONV + (k + 1) * 4)
                        wait(dve, ham, hc.base + hc.n)
                        for m, (i, j) in enumerate(((0, 0), (1, 1), (0, 1), (1, 0))):
                            o = prod[:, m].rearrange("p w (h l e) -> p w h l e", h=2, l=2)
                            hc.step(v.tensor_tensor(o[:, 0], view(l, i, 0, (3, 0)), view(r, j, 0, (2, 1)), ALU.mult))
                            hc.step(v.tensor_tensor(o[:, 1], view(l, i, 1, (1, 0)), view(r, j, 2, (-2, 1)), ALU.mult))

                    def sums(b, k):
                        l, n0 = s1[PROJ[k][0]], hc.n - 8
                        hc.wait(n0 + 4)
                        hc.step(v.tensor_tensor(prod[:, 0], prod[:, 0], prod[:, 1], ALU.subtract))
                        hc.wait(n0 + 8)
                        hc.step(v.tensor_tensor(prod[:, 2], prod[:, 2], prod[:, 3], ALU.add))
                        hc.wait()
                        parts = prod[:].rearrange("p (s z) w (c e) -> p s z w c e", s=2, c=4)[:, :, 0]
                        hc.step(v.tensor_tensor(l[:, :, 1:3, :], parts[:, :, 0, 1:3], parts[:, :, 1, 1:3], ALU.add))
                        hc.step(v.tensor_tensor(l[:, :, 0:4:3, :], parts[:, :, 0, 0:4:3], parts[:, :, 1, 0:4:3], ALU.subtract))

                    def back_to_parts(b, tile):
                        hc.wait()
                        r = r_spec[:, tile].rearrange("p s (h l) e -> p s h l e", h=2)
                        s = s1[tile]
                        d_c = down(s, 3)
                        both = bass.AP(d_c[0].tensor, d_c[0].offset, [list(d_c[0].ap[0]), [4 * P, 2], [-P, 2], [1, P]])
                        hc.step(v.tensor_tensor(r[:, :, :, 0], s[:, :, 0:2, :], both, ALU.add))
                        hc.step(v.tensor_tensor(r[:, 0, :, 1], s[:, 1, 0:2, :], d_c[1], ALU.subtract))
                        hc.step(v.tensor_tensor(r[:, 1, :, 1], d_c[0], s[:, 0, 0:2, :], ALU.subtract))

                    def add_attended(b, t):
                        if t == 0:
                            uc.begin(b)
                            if last_sequence(b):
                                dve.wait_ge(last_res_loaded, 16)
                            else:
                                dve.wait_ge(res_loaded, b * 16 + 16)
                            wait(dve, scattered, b * 64)
                            wait(dve, base_ready, b * 4)
                        lo, hi = rows[:, t, 0:DIM], rows[:, t + 2, 0:DIM]
                        dve.wait_ge(inv_mm, b * 4 + 2 * t + 1)
                        uc.step(v.tensor_tensor(lo, residual(b)[:, t, :], even_ps[:], ALU.add))
                        n = uc.step(v.tensor_tensor(hi, residual(b)[:, t + 2, :], even_ps[:], ALU.add))
                        dve.wait_ge(inv_mm, b * 4 + 2 * t + 2)
                        uc.wait(n)
                        uc.step(v.tensor_tensor(lo, lo, odd_ps[:], ALU.add))
                        uc.step(v.tensor_tensor(hi, hi, odd_ps[:], ALU.subtract))
                        if t == 1:
                            uc.end()

                    def choose(b):
                        dve.wait_ge(logit_mm, b * 4 + 4)
                        wait(dve, rank_mm, b)
                        ro.begin(b)
                        lg = even_ps[:, 0:ROWT * EXPERTS].rearrange("p (t e) -> p t e", t=ROWT)
                        ro.step(v.tensor_tensor(logit[:], lg, bass.AP(gate_c[:].tensor, gate_c[:].offset, [list(gate_c[:].ap[0]), [0, ROWT], [1, EXPERTS]]), ALU.add)); ro.wait()
                        ro.step(v.tensor_reduce(top[:], logit[:], AX.X, ALU.max)); ro.wait()
                        ro.step(v.tensor_tensor(over[:], logit[:], top[:].unsqueeze(2).broadcast_to([P, ROWT, EXPERTS]), ALU.subtract)); ro.wait()
                        ro.step(v.scalar_tensor_tensor(cand[:], over[:], 0.0, iota8[:], ALU.is_ge, ALU.mult)); ro.wait()
                        ro.step(v.tensor_reduce(first[:], cand[:], AX.X, ALU.min)); ro.wait()
                        ro.step(v.tensor_tensor(onehot[:], iota8[:], first[:].unsqueeze(2).broadcast_to([P, ROWT, EXPERTS]), ALU.is_equal))

                    def place(b):
                        dve.wait_ge(exp_done, b + 1)
                        ro.step(v.tensor_reduce(denom[:], e_over[:], AX.X, ALU.add)); ro.wait()
                        ro.step(v.reciprocal(rows[:, :, DIM + 1], denom[:]))
                        wait(dve, token_next, b)
                        ro.step(v.tensor_scalar(rows[:, :, DIM].bitcast(i32), token[:], 1.0, None, ALU.mult))
                        dve.wait_ge(rank_mm, b + 1)
                        rk = odd_ps[:, 0:ROWT * EXPERTS].rearrange("p (t e) -> p t e", t=ROWT)
                        ro.step(v.tensor_tensor(cand[:], rk, bass.AP(running[:].tensor, running[:].offset, [list(running[:].ap[0]), [0, ROWT], [1, EXPERTS]]), ALU.add)); ro.wait()
                        ro.step(v.tensor_tensor(running[:], running[:], odd_ps[:, ROWT * EXPERTS:(ROWT + 1) * EXPERTS], ALU.add))
                        ro.step(v.tensor_tensor(picked[:], cand[:], onehot[:], ALU.mult)); ro.wait()
                        ro.step(v.tensor_reduce(rank[:], picked[:], AX.X, ALU.add)); ro.wait()
                        ro.step(v.tensor_scalar(far[:], rank[:], float(CAPACITY), float(SKIPPED), ALU.is_ge, ALU.mult))
                        ro.step(v.scalar_tensor_tensor(slot_f[:], first[:], float(CAPACITY), rank[:], ALU.mult, ALU.add)); ro.wait()
                        ro.step(v.scalar_tensor_tensor(slot_i[:], slot_f[:], float(CAPACITY * EXPERTS), far[:], ALU.add, ALU.add))
                        ro.wait()
                        ro.end()

                    convert(0, 0)
                    convert(0, 1)

                    def batch(b, back, ahead, ahead2):
                        hc.begin(b, 12)
                        convert(b, 2)
                        if ahead:
                            folds_q(b + 1)
                        if back:
                            add_attended(b - 1, 0)
                        hamilton(b, 2)
                        convert(b, 3)
                        if back:
                            add_attended(b - 1, 1)
                        wait(dve, inv_mm, b * 4)
                        back_to_parts(b, 0)
                        convert(b, 4)
                        hamilton(b, 4)
                        if ahead2:
                            folds_c(b + 2)
                        convert(b, 5)
                        hamilton(b, 5, (lambda: context_low(b + 1)) if ahead else None)
                        if ahead:
                            convert(b + 1, 0)
                        back_to_parts(b, 1)
                        hc.end()
                        if ahead:
                            convert(b + 1, 1)
                        if back:
                            choose(b - 1)
                        if ahead:
                            first_product(b + 1, (lambda: place(b - 1)) if back else None)
                        else:
                            place(b - 1)

                    def first_product(b, between):
                        hc.begin(b)
                        hamilton(b, 1, between)

                    first_product(0, None)
                    batch(0, False, True, True)
                    with dve.Fori(1, BATCH - 2) as b:
                        batch(b, True, True, True)
                    batch(BATCH - 2, True, True, False)
                    batch(BATCH - 1, True, False, False)
                    add_attended(BATCH - 1, 0)
                    add_attended(BATCH - 1, 1)
                    choose(BATCH - 1)
                    place(BATCH - 1)

        experts(nc, outer, slots, eye, gam, bet, w_raw, raw_in, wi, wo, out)


def load_weights(sp, w_raw, raw_in, wi, wo, e, k):
    raw = w_raw[k % 2]
    sp.dma_start(raw[:, 0].rearrange("p (c n) -> p c n", c=CB),
                 wi[bass.ds(e, 1), :, k * 256:(k + 1) * 256].rearrange("a (c p) n -> p (a c) n", p=P)
                 ).then_inc(raw_in[k % 2], 16)
    sp.dma_start(raw[:, 1].rearrange("p (c n) -> p c n", c=2),
                 wo[bass.ds(e, 1), k * 256:(k + 1) * 256, :].rearrange("a (c p) n -> p (a c) n", p=P)
                 ).then_inc(raw_in[k % 2], 16)


def experts(nc, outer, slots, eye, gam, bet, w_raw, raw_in, wi, wo, out):
    f32, f32r, u32 = mybir.dt.float32, mybir.dt.float32r, mybir.dt.uint32
    ALU, ACT = mybir.AluOpType, mybir.ActivationFunctionType

    def sem(name):
        return outer.enter_context(nc.semaphore(name))

    with ExitStack() as mem:
        def sb(name, shape, dt=f32):
            return mem.enter_context(nc.sbuf_tensor(name, shape, dt))

        def pb(name, shape):
            return mem.enter_context(nc.psum_tensor(name, shape, f32))

        got = [sb(f"got{i}", [P, GT, ROW]) for i in (0, 1)]
        normed = sb("normed", [P, GT, DIM])
        tok32 = [sb(f"tok32_{i}", [P, GROUP]) for i in (0, 1)]
        tok_h = [sb(f"tok_h{i}", [P, CB, GROUP], f32r) for i in (0, 1)]
        tok_l = [sb(f"tok_l{i}", [P, CB, GROUP], f32r) for i in (0, 1)]
        w_h = [sb(f"w_h{i}", [P, 2, 1024], f32r) for i in range(RING)]
        w_l = [sb(f"w_l{i}", [P, 2, 1024], f32r) for i in range(RING)]
        act32 = [sb(f"act32_{i}", [P, GROUP]) for i in (0, 1)]
        act_h = [sb(f"act_h{i}", [P, GROUP], f32r) for i in range(4)]
        act_l = [sb(f"act_l{i}", [P, GROUP], f32r) for i in range(4)]
        res = sb("res", [P, GT, DIM])
        mixed = sb("mixed", [P, GT, DIM])
        tally, unit = sb("tally", [1, 1]), sb("unit", [1, 1])

        hid_ps = [pb(f"hid_ps{i}", [P, 512]) for i in (0, 1)]
        tr_ps = [pb(f"tr_ps{i}", [P, 512]) for i in (0, 1)]
        out_ps = [pb(f"out_ps{i}", [P, 512]) for i in range(GT)]

        tallied, cleared = sem("tallied"), sem("cleared")
        got_in = [sem(f"got_in{i}") for i in (0, 1)]
        wh_ready, wl_ready = sem("wh_ready"), sem("wl_ready")
        normed_ready = sem("normed_ready")
        tr_mm, th_ready, tv_ready, tl_ready = sem("tr_mm"), sem("th_ready"), sem("tv_ready"), sem("tl_ready")
        hid_mm, gelu, ah_ready, al_ready, out_mm = sem("hid_mm"), sem("gelu"), sem("ah_ready"), sem("al_ready"), sem("out_mm")
        res_ready, mixed_ready, mixed_stored = sem("res_ready"), sem("mixed_ready"), sem("mixed_stored")

        def group(e, g):
            return e * 2 + g

        with nc.Block() as block:
            @block.sync
            def _(sp):
                def rows_of(e, g):
                    wait(sp, mixed_stored, e * 128 - 64 + 64 * g)
                    src = slots.rearrange("(a t p) n -> a p t n", t=GT, p=P)
                    sp.dma_start(got[g][:], src[bass.ds(e * 2 + g, 1)].rearrange("a p t n -> p (a t) n")).then_inc(got_in[g], 16)

                def weights(e, g, k):
                    n = group(e, g) * PAIRS + k
                    if isinstance(n, int) and n < 2:
                        return
                    wait(sp, wl_ready, n - 1)
                    wait(sp, wh_ready, n - 1)
                    load_weights(sp, w_raw, raw_in, wi, wo, e, k)

                def expert(e, more):
                    for g in range(2):
                        for k in range(PAIRS):
                            weights(e, g, k)
                            if k == ROWS_AT:
                                if g == 0:
                                    rows_of(e, 1)
                                elif more:
                                    rows_of(e + 1, 0)

                rows_of(0, 0)
                expert(0, True)
                with sp.Fori(1, EXPERTS - 1) as e:
                    expert(e, True)
                expert(EXPERTS - 1, False)

            @block.gpsimd
            def _(pool):
                nc.gpsimd.memset(tally[:], 0.0).then_inc(cleared, 1)
                nc.gpsimd.memset(unit[:], 1.0).then_inc(cleared, 1)
                pool.wait_ge(cleared, 2)

                def store(e, g):
                    wait(pool, tallied, group(e, g))
                    pool.wait_ge(mixed_ready, group(e, g) * GT + GT)
                    nc.gpsimd.tensor_tensor(tally[:], tally[:], unit[:], ALU.add).then_inc(tallied, 1)
                    for t in range(GT):
                        nc.gpsimd.indirect_dma_start(
                            out.rearrange("b s n -> (b s) n"),
                            bass.IndirectOffsetOnAxis(ap=got[g][:, t, DIM:DIM + 1].bitcast(u32), axis=0),
                            mixed[:, t, :], None, bounds_check=BATCH * SEQ - 1, oob_is_err=False).then_inc(mixed_stored, 16)

                store(0, 0)
                store(0, 1)
                with pool.Fori(1, EXPERTS) as e:
                    store(e, 0)
                    store(e, 1)
                pool.wait_ge(mixed_stored, 2 * EXPERTS * GT * 16)

            @block.tensor
            def _(pe):
                def turn(e, g, c):
                    n = group(e, g)
                    pe.wait_ge(normed_ready, n * GT + GT)
                    wait(pe, tv_ready, n * CB + c - 1)
                    for t in range(GT):
                        last = nc.tensor.transpose(tr_ps[c % 2][:, t * P:(t + 1) * P], normed[:, t, c * P:(c + 1) * P], eye[:])
                    last.then_inc(tr_mm, 1)

                def up(e, g, i):
                    n = group(e, g)
                    if i == 0:
                        pe.wait_ge(tl_ready, n * CB + CB)
                    if i % 2 == 0:
                        pe.wait_ge(wh_ready, n * PAIRS + i // 2 + 1)
                        pe.wait_ge(wl_ready, n * PAIRS + i // 2 + 1)
                    wait(pe, gelu, n * ISTEPS + i - 1)
                    s = (i // 2) % RING
                    wh, wl = (w[s][:, 0].rearrange("p (c n) -> p c n", c=CB)[:, :, (i % 2) * P:(i % 2 + 1) * P] for w in (w_h, w_l))
                    for c in range(CB):
                        for a, b in ((wh, tok_h[g]), (wl, tok_h[g]), (wh, tok_l[g])):
                            first_, last_ = c == 0 and a is wh and b is tok_h[g], c == CB - 1 and b is tok_l[g]
                            last = nc.tensor.matmul(hid_ps[i % 2][:], a[:, c, :], b[:, c, :], start=first_, stop=last_)
                    last.then_inc(hid_mm, 1)

                def down(e, g, i):
                    n = group(e, g)
                    pe.wait_ge(ah_ready, n * ISTEPS + i + 1)
                    pe.wait_ge(al_ready, n * ISTEPS + i + 1)
                    s = (i // 2) % RING
                    oh, ol = (w[s][:, 1, (i % 2) * 512:(i % 2 + 1) * 512] for w in (w_h, w_l))
                    for t in range(GT):
                        if i == 0:
                            wait(pe, mixed_ready, (n - 1) * GT + t + 1)
                        ah, al = act_h[i % 4][:, t * P:(t + 1) * P], act_l[i % 4][:, t * P:(t + 1) * P]
                        nc.tensor.matmul(out_ps[t][:], ah, oh, start=(i == 0), stop=False)
                        nc.tensor.matmul(out_ps[t][:], al, oh, start=False, stop=False)
                        last = nc.tensor.matmul(out_ps[t][:], ah, ol, start=False, stop=(i == ISTEPS - 1))
                    last.then_inc(out_mm, 1)

                def expert(e, more):
                    for g in range(2):
                        for i in range(ISTEPS + 2):
                            if i < ISTEPS:
                                up(e, g, i)
                            if i >= 2:
                                down(e, g, i - 2)
                            if 8 <= i < 8 + CB and (g == 0 or more):
                                turn(e + g, 1 - g, i - 8)

                for c in range(CB):
                    turn(0, 0, c)
                expert(0, True)
                with pe.Fori(1, EXPERTS - 1) as e:
                    expert(e, True)
                expert(EXPERTS - 1, False)

            @block.scalar
            def _(act):
                def norm(e, g):
                    n = group(e, g)
                    act.wait_ge(got_in[g], e * 16 + 16)
                    wait(act, tr_mm, n * CB)
                    for t in range(GT):
                        nc.scalar.activation(normed[:, t, :], got[g][:, t, 0:DIM], ACT.Identity,
                                             bias=got[g][:, t, DIM + 3:DIM + 4],
                                             scale=got[g][:, t, DIM + 2:DIM + 3]).then_inc(normed_ready, 1)

                def affine(e, g, c):
                    n = group(e, g) * CB + c
                    act.wait_ge(tr_mm, n + 1)
                    wait(act, tl_ready, n - 1)
                    nc.scalar.activation(tok32[c % 2][:], tr_ps[c % 2][:], ACT.Identity, bias=bet[:, c:c + 1],
                                         scale=gam[:, c:c + 1]).then_inc(tv_ready, 1)

                def weight_high(e, g, k):
                    n = group(e, g) * PAIRS + k
                    if k % 2 == 0:
                        act.wait_ge(raw_in[0], (group(e, g) * (PAIRS // 2) + k // 2) * 32 + 32)
                    else:
                        act.wait_ge(raw_in[1], (group(e, g) * (PAIRS // 2) + k // 2) * 32 + 32)
                    wait(act, out_mm, (n - RING + 1) * 2)
                    nc.scalar.activation(w_h[k % RING][:], w_raw[k % 2][:], ACT.Copy).then_inc(wh_ready, 1)

                def gelu_of(e, g, i):
                    n = group(e, g) * ISTEPS + i
                    act.wait_ge(hid_mm, n + 1)
                    wait(act, al_ready, n - 1)
                    nc.scalar.activation(act32[i % 2][:], hid_ps[i % 2][:], ACT.Gelu).then_inc(gelu, 1)

                def residual(e, g):
                    n = group(e, g)
                    wait(act, mixed_ready, n * GT)
                    for t in range(GT):
                        nc.scalar.activation(res[:, t, :], got[g][:, t, 0:DIM], ACT.Identity,
                                             bias=got[g][:, t, DIM + 5:DIM + 6],
                                             scale=got[g][:, t, DIM + 4:DIM + 5]).then_inc(res_ready, 1)

                def expert(e, more):
                    for g in range(2):
                        for i in range(ISTEPS):
                            gelu_of(e, g, i)
                            if i % 2 == 1:
                                k = i // 2 + 2
                                if k < PAIRS:
                                    weight_high(e, g, k)
                                elif g == 0:
                                    weight_high(e, 1, k - PAIRS)
                                elif more:
                                    weight_high(e + 1, 0, k - PAIRS)
                            if i == 4:
                                residual(e, g)
                            if g == 0 or more:
                                if i == 6:
                                    norm(e + g, 1 - g)
                                if 8 <= i < 8 + CB:
                                    affine(e + g, 1 - g, i - 8)

                weight_high(0, 0, 0)
                weight_high(0, 0, 1)
                norm(0, 0)
                for c in range(CB):
                    affine(0, 0, c)
                expert(0, True)
                with act.Fori(1, EXPERTS - 1) as e:
                    expert(e, True)
                expert(EXPERTS - 1, False)

            @block.vector
            def _(dve):
                v = nc.vector

                def token_split(e, g, c):
                    n = group(e, g) * CB + c
                    dve.wait_ge(tv_ready, n + 1)
                    v.tensor_copy(tok_h[g][:, c, :], tok32[c % 2][:]).then_inc(th_ready, 1)
                    dve.wait_ge(th_ready, n + 1)
                    v.tensor_tensor(tok_l[g][:, c, :], tok32[c % 2][:], tok_h[g][:, c, :].bitcast(f32),
                                    ALU.subtract).then_inc(tl_ready, 1)

                def weight_low(e, g, k):
                    n = group(e, g) * PAIRS + k
                    dve.wait_ge(wh_ready, n + 1)
                    v.tensor_tensor(w_l[k % RING][:], w_raw[k % 2][:], w_h[k % RING][:].bitcast(f32), ALU.subtract).then_inc(wl_ready, 1)

                def split(e, g, i):
                    n = group(e, g) * ISTEPS + i
                    dve.wait_ge(gelu, n + 1)
                    wait(dve, out_mm, n - 3)
                    v.tensor_copy(act_h[i % 4][:], act32[i % 2][:]).then_inc(ah_ready, 1)
                    dve.wait_ge(ah_ready, n + 1)
                    v.tensor_tensor(act_l[i % 4][:], act32[i % 2][:], act_h[i % 4][:].bitcast(f32),
                                    ALU.subtract).then_inc(al_ready, 1)

                def mix(e, g):
                    n = group(e, g)
                    dve.wait_ge(out_mm, n * ISTEPS + ISTEPS)
                    dve.wait_ge(res_ready, n * GT + GT)
                    wait(dve, mixed_stored, n * GT * 16)
                    for t in range(GT):
                        v.scalar_tensor_tensor(mixed[:, t, :], out_ps[t][:], got[g][:, t, DIM + 1:DIM + 2], res[:, t, :],
                                               ALU.mult, ALU.add).then_inc(mixed_ready, 1)

                def expert(e, more):
                    for g in range(2):
                        for i in range(ISTEPS):
                            split(e, g, i)
                            if i % 2 == 1:
                                k = i // 2 + 2
                                if k < PAIRS:
                                    weight_low(e, g, k)
                                elif g == 0:
                                    weight_low(e, 1, k - PAIRS)
                                elif more:
                                    weight_low(e + 1, 0, k - PAIRS)
                            if 8 <= i < 8 + CB and (g == 0 or more):
                                token_split(e + g, 1 - g, i - 8)
                        mix(e, g)

                weight_low(0, 0, 0)
                weight_low(0, 0, 1)
                for c in range(CB):
                    token_split(0, 0, c)
                expert(0, True)
                with dve.Fori(1, EXPERTS - 1) as e:
                    expert(e, True)
                expert(EXPERTS - 1, False)


def kernel(**inputs):
    import concourse.bacc as bacc
    from concourse.bass_utils import run_bass_kernel_spmd

    nc = bacc.Bacc("TRN2", target_bir_lowering=False, num_devices=1)
    turned = ("L0_xattn_Wq", "L0_xattn_Wk", "L0_xattn_Wv", "L0_ffn_gate_weight")
    vectors = ("L0_ffn_ln_gamma", "L0_ffn_ln_beta")
    names = ["x", "ctx_1024", "L0_xattn_Wq", "L0_xattn_Wk", "L0_xattn_Wv", "L0_xattn_bq", "L0_xattn_bk", "L0_xattn_bv",
             "L0_ffn_gate_weight", "L0_ffn_ln_gamma", "L0_ffn_ln_beta", "L0_ffn_wi", "L0_ffn_wo"]
    arrays, args = {}, []
    for name in names:
        a = np.asarray(inputs[name])
        if name in vectors:
            a = a.reshape(-1, P)
        a = np.ascontiguousarray(a.T if name in turned + vectors else a)
        arrays[f"in_{name}"] = a
        args.append(nc.dram_tensor(f"in_{name}", a.shape, mybir.dt.from_np(a.dtype), kind="ExternalInput").ap())
    out = nc.dram_tensor("out", (BATCH, SEQ, DIM), mybir.dt.float32, kind="ExternalOutput").ap()
    xattn_moe_kernel(nc, *args, out)
    r = run_bass_kernel_spmd(nc, [arrays], core_ids=[0])
    return r.results[0]["out"]
```
